# Optimizing a Trainium2 kernel written in Bass

```python
import numpy as np
import jax
import jax.numpy as jnp

def _softmax(x, axis=-1):
    return jax.nn.softmax(x, axis=axis)

def _gelu(x):
    return jax.nn.gelu(x, approximate=True)

def _silu(x):
    return jax.nn.silu(x)

def _sigmoid(x):
    return jax.nn.sigmoid(x)

def _layernorm(x, axis=-1, eps=1e-05):
    m = jnp.mean(x, axis=axis, keepdims=True)
    v = jnp.var(x, axis=axis, keepdims=True)
    return (x - m) / jnp.sqrt(v + eps)

def _scatter_add(tgt, idx, src, axis=0):
    return tgt.at[idx].add(src)

def _segment_sum(src, seg, n):
    return jax.ops.segment_sum(src, seg, n)
kernel_name = 'mk_adj_ffn_d2_adj_r2_0d2c06'

def setup_inputs(seed: int=0):
    np.random.seed(seed)
    _w = jnp.asarray

    def _rec_inputs():
        import jax
        import jax.numpy as jnp
        _gk = jax.random.key(seed)
        x = -0.0002928 + 1 * jax.random.normal(jax.random.fold_in(_gk, 1), (128, 128, 128), jnp.float32)
        _a = jax.random.bernoulli(jax.random.fold_in(_gk, 2), 0.03125, (128, 128))
        adj = _a.astype(jnp.int32)
        return (x, adj)
    x, adj = _rec_inputs()

    def _L0_gnn_setup():
        import jax, jax.numpy as jnp
        import numpy as np
        IN_F = 128
        OUT_F = 128
        ALPHA = 0.01
        NEG_INF = -1000000000.0
        key = jax.random.key(seed)
        k_inp, k_adj, k_W, k_a = jax.random.split(key, 4)
        inp = jax.random.normal(k_inp, (8, 1024, IN_F), dtype=jnp.float32)
        adj = jax.random.randint(k_adj, (1024, 1024), 0, 2, dtype=jnp.int32)
        gain = 1.414
        lim_W = gain * np.sqrt(6.0 / (IN_F + OUT_F))
        W = jax.random.uniform(k_W, (IN_F, OUT_F), minval=-lim_W, maxval=lim_W, dtype=jnp.float32)
        lim_a = gain * np.sqrt(6.0 / (2 * OUT_F + 1))
        a = jax.random.uniform(k_a, (2 * OUT_F, 1), minval=-lim_a, maxval=lim_a, dtype=jnp.float32)
        return {'inp': inp, 'adj': adj, 'W': W, 'a': a}
    _L0_gnn_all = _L0_gnn_setup()
    _L0_gnn_in = {k: v for k, v in _L0_gnn_all.items() if k in ('W', 'a')}
    del _L0_gnn_all

    def _L0_ffn_setup():
        import jax, jax.numpy as jnp
        import numpy as np
        B, K, D = (256, 16, 128)
        E = 32
        H = int(D * 0.25)
        key = jax.random.key(seed)
        ks = jax.random.split(key, 7)
        d_rs = D ** (-0.5)
        h_rs = H ** (-0.5)
        x = jax.random.normal(ks[0], (B, K, D), dtype=jnp.float32)
        router_w = jax.random.uniform(ks[1], (E, D), jnp.float32, -d_rs, d_rs)
        router_b = jax.random.uniform(ks[2], (E,), jnp.float32, -d_rs, d_rs)
        W1 = jax.random.uniform(ks[3], (E, D, H), jnp.float32, -h_rs, h_rs)
        b1 = jax.random.uniform(ks[4], (E, H), jnp.float32, -h_rs, h_rs)
        W2 = jax.random.uniform(ks[5], (E, H, D), jnp.float32, -d_rs, d_rs)
        b2 = jax.random.uniform(ks[6], (E, D), jnp.float32, -d_rs, d_rs)
        return {'x': x, 'router_w': router_w, 'router_b': router_b, 'W1': W1, 'b1': b1, 'W2': W2, 'b2': b2}
    _L0_ffn_all = _L0_ffn_setup()
    _L0_ffn_in = {k: v for k, v in _L0_ffn_all.items() if k in ('router_w', 'router_b', 'W1', 'b1', 'W2', 'b2')}
    del _L0_ffn_all

    def _L1_gnn_setup():
        import jax, jax.numpy as jnp
        import numpy as np
        B, N, D_IN, D_OUT, H = (64, 256, 128, 128, 4)
        HD = D_OUT // H
        key = jax.random.key(seed)
        ks = jax.random.split(key, 10)
        x = jax.random.normal(ks[0], (B, N, D_IN), dtype=jnp.float32)
        adj = jax.random.randint(ks[1], (N, N), 0, 2, dtype=jnp.int32)
        adj = adj.at[jnp.arange(N), jnp.arange(N)].set(1)
        s_in = 1.0 / np.sqrt(D_IN)
        s_out = 1.0 / np.sqrt(D_OUT)
        wq = jax.random.uniform(ks[2], (D_OUT, D_IN), jnp.float32, -s_in, s_in)
        bq = jax.random.uniform(ks[3], (D_OUT,), jnp.float32, -s_in, s_in)
        wk = jax.random.uniform(ks[4], (D_OUT, D_IN), jnp.float32, -s_in, s_in)
        bk = jax.random.uniform(ks[5], (D_OUT,), jnp.float32, -s_in, s_in)
        wv = jax.random.uniform(ks[6], (D_OUT, D_IN), jnp.float32, -s_in, s_in)
        bv = jax.random.uniform(ks[7], (D_OUT,), jnp.float32, -s_in, s_in)
        wo = jax.random.uniform(ks[8], (D_OUT, D_OUT), jnp.float32, -s_out, s_out)
        bo = jax.random.uniform(ks[9], (D_OUT,), jnp.float32, -s_out, s_out)
        return {'x': x, 'adj': adj, 'wq': wq, 'bq': bq, 'wk': wk, 'bk': bk, 'wv': wv, 'bv': bv, 'wo': wo, 'bo': bo}
    _L1_gnn_all = _L1_gnn_setup()
    _L1_gnn_in = {k: v for k, v in _L1_gnn_all.items() if k in ('wq', 'bq', 'wk', 'bk', 'wv', 'bv', 'wo', 'bo')}
    del _L1_gnn_all

    def _L1_ffn_setup():
        import jax, jax.numpy as jnp
        import numpy as np
        C = 128
        HID = 512
        E = 8
        TEMP = 1.0
        key = jax.random.key(seed)
        ks = jax.random.split(key, 7)
        x = jax.random.normal(ks[0], (8, 8192, C), dtype=jnp.float32)
        W1 = jax.random.normal(ks[1], (C, HID), dtype=jnp.float32) * 0.02
        b1 = jnp.zeros((HID,), dtype=jnp.float32)
        Wg = jax.random.normal(ks[2], (HID, E), dtype=jnp.float32) * 0.02
        bg = jnp.zeros((E,), dtype=jnp.float32)
        Wd = jax.random.normal(ks[3], (E, HID, C), dtype=jnp.float32) * 0.02
        bd = jnp.zeros((E, C), dtype=jnp.float32)
        return {'x': x, 'W1': W1, 'b1': b1, 'Wg': Wg, 'bg': bg, 'Wd': Wd, 'bd': bd}
    _L1_ffn_all = _L1_ffn_setup()
    _L1_ffn_in = {k: v for k, v in _L1_ffn_all.items() if k in ('W1', 'b1', 'Wg', 'bg', 'Wd', 'bd')}
    del _L1_ffn_all
    return {'x': x, 'adj': adj, 'L0_gnn_W': _L0_gnn_in['W'], 'L0_gnn_a': _L0_gnn_in['a'], 'L0_ffn_router_w': _L0_ffn_in['router_w'], 'L0_ffn_router_b': _L0_ffn_in['router_b'], 'L0_ffn_W1': _L0_ffn_in['W1'], 'L0_ffn_b1': _L0_ffn_in['b1'], 'L0_ffn_W2': _L0_ffn_in['W2'], 'L0_ffn_b2': _L0_ffn_in['b2'], 'L1_gnn_wq': _L1_gnn_in['wq'], 'L1_gnn_bq': _L1_gnn_in['bq'], 'L1_gnn_wk': _L1_gnn_in['wk'], 'L1_gnn_bk': _L1_gnn_in['bk'], 'L1_gnn_wv': _L1_gnn_in['wv'], 'L1_gnn_bv': _L1_gnn_in['bv'], 'L1_gnn_wo': _L1_gnn_in['wo'], 'L1_gnn_bo': _L1_gnn_in['bo'], 'L1_ffn_W1': _L1_ffn_in['W1'], 'L1_ffn_b1': _L1_ffn_in['b1'], 'L1_ffn_Wg': _L1_ffn_in['Wg'], 'L1_ffn_bg': _L1_ffn_in['bg'], 'L1_ffn_Wd': _L1_ffn_in['Wd'], 'L1_ffn_bd': _L1_ffn_in['bd']}

def reference(x, adj, L0_gnn_W, L0_gnn_a, L0_ffn_router_w, L0_ffn_router_b, L0_ffn_W1, L0_ffn_b1, L0_ffn_W2, L0_ffn_b2, L1_gnn_wq, L1_gnn_bq, L1_gnn_wk, L1_gnn_bk, L1_gnn_wv, L1_gnn_bv, L1_gnn_wo, L1_gnn_bo, L1_ffn_W1, L1_ffn_b1, L1_ffn_Wg, L1_ffn_bg, L1_ffn_Wd, L1_ffn_bd):
    import jax
    import jax.numpy as jnp

    def _L0_gnn_ref(inp, adj, W, a):
        import jax, jax.numpy as jnp
        import numpy as np
        IN_F = 128
        OUT_F = 128
        ALPHA = 0.01
        NEG_INF = -1000000000.0
        h = jnp.matmul(inp, W)
        a1 = a[:OUT_F, 0]
        a2 = a[OUT_F:, 0]
        e_src = jnp.einsum('bnf,f->bn', h, a1)
        e_dst = jnp.einsum('bnf,f->bn', h, a2)
        e = jax.nn.leaky_relu(e_src[:, :, None] + e_dst[:, None, :], negative_slope=ALPHA)
        e = jnp.where(adj[None, :, :] == 0, NEG_INF, e)
        attention = jax.nn.softmax(e, axis=-1)
        h_prime = jnp.matmul(attention, h)
        return jax.nn.relu(h_prime)

    def _L0_ffn_ref(x, router_w, router_b, W1, b1, W2, b2):
        import jax, jax.numpy as jnp
        import numpy as np
        B, K, D = (256, 16, 128)
        E = 32
        H = int(D * 0.25)
        xf = x.reshape(-1, D)
        logits = xf @ router_w.T + router_b
        idx = jnp.argmax(logits, axis=-1)
        w1t = jnp.take(W1, idx, axis=0)
        h = jnp.einsum('nd,ndh->nh', xf, w1t) + jnp.take(b1, idx, axis=0)
        h = jax.nn.relu(h)
        w2t = jnp.take(W2, idx, axis=0)
        out = jnp.einsum('nh,nhd->nd', h, w2t) + jnp.take(b2, idx, axis=0)
        out = jax.nn.relu(out)
        return out.reshape(x.shape)

    def _L1_gnn_ref(x, adj, wq, bq, wk, bk, wv, bv, wo, bo):
        import jax, jax.numpy as jnp
        import numpy as np
        B, N, D_IN, D_OUT, H = (64, 256, 128, 128, 4)
        HD = D_OUT // H
        b, n, _ = x.shape
        q = (x @ wq.T + bq).reshape(b, n, H, HD).transpose(0, 2, 1, 3)
        k = (x @ wk.T + bk).reshape(b, n, H, HD).transpose(0, 2, 1, 3)
        v = (x @ wv.T + bv).reshape(b, n, H, HD).transpose(0, 2, 1, 3)
        scores = jnp.einsum('bhnd,bhmd->bhnm', q, k) / jnp.sqrt(jnp.float32(HD))
        scores = jnp.where(adj[None, None] == 0, -jnp.inf, scores)
        attn = jnp.nan_to_num(jax.nn.softmax(scores, axis=-1), nan=0.0)
        out = jnp.einsum('bhnm,bhmd->bhnd', attn, v)
        out = out.transpose(0, 2, 1, 3).reshape(b, n, D_OUT)
        return out @ wo.T + bo

    def _L1_ffn_ref(x, W1, b1, Wg, bg, Wd, bd):
        import jax, jax.numpy as jnp
        import numpy as np
        C = 128
        HID = 512
        E = 8
        TEMP = 1.0
        orig_shape = x.shape
        xf = x.reshape(-1, orig_shape[-1])
        H = jax.nn.gelu(xf @ W1 + b1, approximate=False)
        probs = jax.nn.softmax((H @ Wg + bg) / TEMP, axis=-1)
        assign = jnp.argmax(probs, axis=-1)
        out = jnp.zeros_like(xf)
        for e in range(Wd.shape[0]):
            y = H @ Wd[e] + bd[e]
            sel = (assign == e)[:, None]
            out = out + jnp.where(sel, probs[:, e:e + 1] * y, 0.0)
        return out.reshape(orig_shape)
    x = x + _L0_gnn_ref(_layernorm(x, axis=-1), adj, L0_gnn_W, L0_gnn_a)
    x = x + _L0_ffn_ref(_layernorm(x, axis=-1), L0_ffn_router_w, L0_ffn_router_b, L0_ffn_W1, L0_ffn_b1, L0_ffn_W2, L0_ffn_b2)
    x = x + _L1_gnn_ref(_layernorm(x, axis=-1), adj, L1_gnn_wq, L1_gnn_bq, L1_gnn_wk, L1_gnn_bk, L1_gnn_wv, L1_gnn_bv, L1_gnn_wo, L1_gnn_bo)
    x = x + _L1_ffn_ref(_layernorm(x, axis=-1), L1_ffn_W1, L1_ffn_b1, L1_ffn_Wg, L1_ffn_bg, L1_ffn_Wd, L1_ffn_bd)
    return x

_drawn_inputs = setup_inputs


def setup_inputs(seed=0):
    import zlib

    import numpy as np

    out = dict(_drawn_inputs(seed))
    spreads = {'L1_ffn_b1': (0.0, 0.8), 'L1_ffn_bg': (0.0, 0.565), 'L1_ffn_bd': (0.0, 0.717)}
    factors = {'L0_ffn_b1': 5.031,
     'L1_gnn_bq': 8.0,
     'L1_gnn_bk': 8.0,
     'L1_ffn_W1': 5.21,
     'L1_ffn_Wg': 5.073,
     'L1_ffn_Wd': 8.0}
    for name, (base, spread) in spreads.items():
        noise = np.random.default_rng([zlib.crc32(name.encode()), seed]).standard_normal(out[name].shape)
        drawn = base * np.exp(spread * noise) if base else spread * noise
        out[name] = jnp.asarray(drawn.astype(out[name].dtype))
    for name, factor in factors.items():
        out[name] = (out[name] * factor).astype(out[name].dtype)
    return out
```

```python
from contextlib import ExitStack

import concourse.bass as bass
from concourse import mybir

ALU = mybir.AluOpType
ACT = mybir.ActivationFunctionType
AX = mybir.AxisListType
F32 = mybir.dt.float32
F16 = mybir.dt.float16
BF16 = mybir.dt.bfloat16
I32 = mybir.dt.int32

P = 128
B = 128
ROWS = B * P
E0, H0 = 32, 32
E1, HID = 8, 512
NCH = HID // P
HEADS, HD = 4, 32
EPS = 1e-5
REGION = ROWS + 2 * P
NT0 = ROWS // P + E0
NT1 = ROWS // P + E1
ROW = P + 4
MEAN, RSTD, PROB, NUM = P, P + 1, P + 2, P + 3
NO_ROW = 1 << 20
MASKED_E0 = -1e9
SLOPE = 0.01
FAR = -1e30

B1_AT = 0
B2_AT = B1_AT + E0 * H0
BD_AT = B2_AT + E0 * P
RB_AT = BD_AT + E1 * P
BO_AT = RB_AT + E0
BG_AT = BO_AT + P
NBIAS = BG_AT + E1


def pipeline(eng, n, unroll, steps, peel=8):
    last = max(lag for lag, _ in steps)
    assert last <= peel and peel % unroll == 0

    def peeled(t):
        for lag, f in steps:
            if 0 <= t - lag < n:
                f(t - lag, (t - lag) % unroll, (t - lag) // unroll)

    for t in range(peel):
        peeled(t)
    with eng.Fori(peel // unroll, n // unroll) as i:
        for u in range(unroll):
            for lag, f in steps:
                f(i * unroll + (u - lag), (u - lag) % unroll, i + (u - lag) // unroll)
    for t in range(n // unroll * unroll, n + last):
        peeled(t)


def freed(eng, sem, g, depth, per=1, k=1):
    if not isinstance(g, int) or g >= depth:
        eng.wait_ge(sem, (g - depth) * per + k)


def wait_alone(K, eng, sem, value):
    eng.wait_ge(sem, value)
    if not isinstance(value, int):
        eng.sem_inc(K["passed"], 1)


class Phase:

    def __init__(self, nc, name):
        self.nc, self.name, self.ctx, self.used = nc, name, ExitStack(), []

    def __enter__(self):
        return self

    def __exit__(self, *exc):
        self.ctx.__exit__(*exc)
        self.nc.clear_and_free_semaphores(self.used)
        self.nc.all_engine_barrier()

    def sb(self, name, shape, dt):
        return self.ctx.enter_context(self.nc.sbuf_tensor(f"{self.name}_{name}", shape, dt))

    def psum(self, name, shape, dt=F32):
        return self.ctx.enter_context(self.nc.psum_tensor(f"{self.name}_{name}", shape, dt))

    def sem(self, name):
        self.used.append(self.nc.alloc_semaphore(f"{self.name}_{name}"))
        return self.used[-1]

    def sems(self, name, n):
        return [self.sem(f"{name}{i}") for i in range(n)]

    def block(self):
        return self.ctx.enter_context(self.nc.Block())


def setup(nc, K, T):
    with Phase(nc, "setup") as ph:
        wload = ph.sb("wload", [P, 6, P], F32)
        acol = ph.sb("acol", [P, 2], F32)
        wT = ph.sb("wT", [P, P], F32)
        wa = ph.sb("wa", [P, 2], F32)
        adj = ph.sb("adj", [P, P], I32)
        off = ph.sb("off", [P, P], F32)
        biasf = ph.sb("biasf", [P, 64], F32)
        res1 = ph.sb("res1", [P, 64], F32)
        res2 = ph.sb("res2", [P, 64], F32)
        part = [ph.sb(f"part{k}", [P, 64], BF16) for k in range(3)]
        bvrow = ph.sb("bvrow", [P, P], F32)
        pt = ph.psum("pt", [P, 8, 512])

        loads = ph.sem("loads")
        bias_zero = ph.sem("bias_zero")
        ones_set = ph.sem("ones_set")
        pool_step = ph.sem("pool_step")
        transposed = ph.sem("transposed")
        wT_ready = ph.sem("wT_ready")
        wa_ready = ph.sem("wa_ready")
        dve_step = ph.sem("dve_step")
        parts_ready = ph.sem("parts_ready")
        rows_stored = ph.sem("rows_stored")
        fills = ph.sem("fills")
        zero_rows = ph.sem("zero_rows")
        block = ph.block()

        pieces = [
            ("L0_ffn_b1", 0, E0 * H0 // P, P, B1_AT),
            ("L0_ffn_b2", 8, E0, P, B2_AT),
            ("L1_ffn_bd", 40, E1, P, BD_AT),
            ("L0_ffn_router_b", 48, 1, E0, RB_AT),
            ("L1_gnn_bo", 49, 1, P, BO_AT),
            ("L1_ffn_bg", 50, 1, E1, BG_AT),
        ]

        def flat(ap):
            return ap.rearrange("a b -> (a b)") if len(ap.shape) == 2 else ap

        @block.sync
        def _(sp):
            n = 0
            for k, name in enumerate(["L0_gnn_W", "L1_gnn_wq", "L1_gnn_wk", "L1_gnn_wv", "L1_gnn_wo"]):
                sp.dma_start(wload[:, k, :], T[name]).then_inc(loads, 16)
            sp.dma_start(wload[0:E0, 5, :], T["L0_ffn_router_w"]).then_inc(loads, 16)
            sp.dma_start(adj[:], T["adj"]).then_inc(loads, 16)
            with nc.allow_non_contiguous_dma(reason="a few hundred bias values"):
                sp.dma_start(acol[:], T["L0_gnn_a"].rearrange("(t p) o -> p (t o)", p=P)).then_inc(loads, 16)
                sp.dma_start(K["bqk"][:, 0:1], T["L1_gnn_bq"].rearrange("(p o) -> p o", o=1)).then_inc(loads, 16)
                sp.dma_start(K["bqk"][:, 1:2], T["L1_gnn_bk"].rearrange("(p o) -> p o", o=1)).then_inc(loads, 16)
                sp.dma_start(K["b1"][:], T["L1_ffn_b1"].rearrange("(c p) -> p c", p=P)).then_inc(loads, 16)
            sp.dma_start(K["bv"][0:1, :], T["L1_gnn_bv"].rearrange("(o n) -> o n", o=1)).then_inc(loads, 16)
            sp.dma_start(K["wg"][:], T["L1_ffn_Wg"].rearrange("(c p) e -> p c e", p=P)).then_inc(loads, 16)
            sp.dma_start(K["w1"][:], T["L1_ffn_W1"]).then_inc(loads, 16)
            sp.wait_ge(bias_zero, 1)
            with nc.allow_non_contiguous_dma(reason="a few hundred bias values"):
                for name, at, cols, parts, _ in pieces:
                    sp.dma_start(biasf[0:parts, at:at + cols],
                                 flat(T[name]).rearrange("(p c) -> p c", c=cols)).then_inc(loads, 16)
            sp.wait_ge(parts_ready, 3)
            with nc.allow_non_contiguous_dma(reason="a few hundred bias values"):
                for k in range(3):
                    for name, at, cols, parts, to in pieces:
                        sp.dma_start(K["biasrows"][k:k + 1, to:to + parts * cols],
                                     part[k][0:parts, at:at + cols]).then_inc(rows_stored, 16)
                        n += 16
            sp.wait_ge(rows_stored, n)
            sp.wait_ge(fills, 16 * (3 + 2))

        NLOADS = 14 + len(pieces)

        @block.scalar
        def _(act):
            act.dma_start(K["w1e"][:], T["L0_ffn_W1"].rearrange("e d h -> d e h")).then_inc(fills, 16)
            act.dma_start(K["w2e"][:], T["L0_ffn_W2"].rearrange("e h d -> h e d")).then_inc(fills, 16)
            act.dma_start(K["wd"][:].rearrange("p e c d -> p (e c) d"),
                          T["L1_ffn_Wd"].rearrange("e (c p) d -> p (e c) d", p=P)).then_inc(fills, 16)
            act.wait_ge(zero_rows, 2)
            for dst, experts in ((K["sorted0"], E0), (K["sorted1"], E1)):
                act.dma_start(dst[experts // 2 * REGION:, :], K["padrow"][:]).then_inc(fills, 16)

        @block.gpsimd
        def _(pool):
            pool.memset(K["padrow"][:], 0.0).then_inc(pool_step, 1)
            pool.memset(K["onesf"][:], 1.0).then_inc(pool_step, 1)
            pool.memset(K["onesb"][:], 1.0).then_inc(pool_step, 1)
            pool.memset(K["ident"][:], 0.0).then_inc(pool_step, 1)
            pool.wait_ge(pool_step, 4)
            pool.memset(K["padrow"][:, NUM:NUM + 1].bitcast(I32), NO_ROW).then_inc(zero_rows, 1)
            pool.affine_select(out=K["ident"][:], in_=K["ident"][:], compare_op=ALU.not_equal, fill=1.0, base=0,
                               pattern=[[-1, P]], channel_multiplier=1).then_inc(pool_step, 1)
            pool.affine_select(out=K["before"][:], in_=K["onesb"][:], compare_op=ALU.is_gt, fill=0.0, base=0,
                               pattern=[[1, P]], channel_multiplier=-1).then_inc(pool_step, 1)
            pool.affine_select(out=K["upto"][:], in_=K["onesf"][0:E0, 0:E0], compare_op=ALU.is_ge, fill=0.0,
                               base=0, pattern=[[1, E0]], channel_multiplier=-1).then_inc(pool_step, 1)
            pool.iota(K["count"][:], [[1, 256]], base=0, channel_multiplier=0,
                      allow_small_or_imprecise_dtypes=True).then_inc(pool_step, 1)
            pool.iota(K["rev0"][:], [[-1, E0]], base=E0, channel_multiplier=0,
                      allow_small_or_imprecise_dtypes=True).then_inc(pool_step, 1)
            pool.iota(K["number"][:], [[P, B]], base=0, channel_multiplier=1,
                      allow_small_or_imprecise_dtypes=True).then_inc(pool_step, 1)
            pool.memset(K["minus_half"][:], -0.5).then_inc(zero_rows, 1)
            pool.wait_ge(loads, 16 * NLOADS)
            pool.partition_broadcast(bvrow[:], K["bv"][0:1, :]).then_inc(pool_step, 1)

        @block.tensor
        def _(pe):
            pe.wait_ge(loads, 16 * NLOADS)
            pe.wait_ge(pool_step, 5)
            for k in range(5):
                pe.transpose(pt[:, k, 0:P], wload[:, k, :], K["ident"][:])
            pe.transpose(pt[:, 5, 0:E0], wload[0:E0, 5, :], K["ident"][0:E0, 0:E0]).then_inc(transposed, 1)
            pe.wait_ge(wT_ready, 1)
            pe.matmul(pt[:, 6, 0:2], wT[:], acol[:], start=True, stop=True).then_inc(wa_ready, 1)

        @block.vector
        def _(dve):
            steps = [0]

            def then(ins):
                steps[0] += 1
                ins.then_inc(dve_step, 1)
                dve.wait_ge(dve_step, steps[0])

            dve.memset(biasf[:], 0.0).then_inc(bias_zero, 1)
            dve.wait_ge(loads, 16 * NLOADS)
            dve.wait_ge(pool_step, 11)
            for j in range(2):
                dve.tensor_copy(K["bvg"][:, j * P:(j + 1) * P], bvrow[:])
            then(dve.tensor_scalar(off[:], adj[:], 0.0, None, ALU.is_equal))
            then(dve.tensor_scalar(K["cap"][:], off[:], -1.0, -3e38, ALU.add, ALU.mult))
            dve.scalar_tensor_tensor(K["cap"][:], off[:], MASKED_E0 / SLOPE, K["cap"][:], ALU.mult, ALU.add)
            dve.tensor_scalar(K["far"][:], off[:], FAR, None, ALU.mult)
            then(dve.tensor_reduce(K["linked"][:], off[:], AX.X, ALU.min))
            then(dve.tensor_scalar(K["linked"][:], K["linked"][:], -1.0, 1.0, ALU.mult, ALU.add))
            dve.tensor_copy(K["identb"][:], K["ident"][:])
            then(dve.tensor_copy(part[0][:], biasf[:]))
            then(dve.tensor_tensor(res1[:], biasf[:], part[0][:], ALU.subtract))
            then(dve.tensor_copy(part[1][:], res1[:]))
            then(dve.tensor_tensor(res2[:], res1[:], part[1][:], ALU.subtract))
            then(dve.tensor_copy(part[2][:], res2[:]))
            dve.tensor_copy(K["w1hi"][:], K["w1"][:]).then_inc(parts_ready, 3)
            then(dve.memset(K["kbd"][:], 0.0))
            dve.memset(K["vaug"][:], 1.0)
            then(dve.tensor_tensor(K["w1lo"][:], K["w1"][:], K["w1hi"][:], ALU.subtract))
            pair = K["count"][:, 0:E0 // 2]
            dve.memset(K["sign"][:, 0::2], 1.0)
            dve.memset(K["sign"][:, 1::2], -1.0)
            dve.tensor_scalar(K["tile0"][:, 0::2], pair, float(REGION // P), None, ALU.mult)
            dve.tensor_scalar(K["tile0"][:, 1::2], pair, float(REGION // P), float(REGION // P - 1), ALU.mult, ALU.add)
            dve.tensor_scalar(K["start"][:, 0::2], pair, float(REGION), None, ALU.mult)
            then(dve.tensor_scalar(K["start"][:, 1::2], pair, -float(REGION), float(1 - REGION), ALU.mult, ALU.add))
            dve.tensor_copy(K["base0"][:], K["start"][:])
            then(dve.tensor_copy(K["base1"][:], K["start"][:, 0:E1]))
            dve.wait_ge(transposed, 1)
            dve.tensor_copy(wT[:], pt[:, 0, 0:P]).then_inc(wT_ready, 1)
            for k, name in ((1, "wqT"), (2, "wkT"), (3, "wvT"), (4, "woT")):
                dve.tensor_copy(K[name][:], pt[:, k, 0:P])
            dve.tensor_copy(K["rwT"][:], pt[:, 5, 0:E0])
            dve.tensor_copy(K["wh"][:], wload[:, 0, :])
            dve.wait_ge(wa_ready, 1)
            then(dve.tensor_copy(K["wa"][:], pt[:, 6, 0:2]))
            dve.tensor_scalar(K["wa2"][:], K["onesf"][:], K["wa"][:, 1:2], None, ALU.mult)


def argmax_onehot(dve, ph_sem, n0, logits, top, eq, key, best, onehot, rev, groups, experts, psum_read=None):
    def then(ins, k):
        ins.then_inc(ph_sem, 1)
        dve.wait_ge(ph_sem, n0 + k)

    shape = [P, groups, experts]
    then(dve.tensor_reduce(top, logits, AX.X, ALU.max), 1)
    then(dve.tensor_tensor(eq, logits, top.unsqueeze(2).to_broadcast(shape), ALU.is_ge), 2)
    then(dve.tensor_tensor(key, eq, rev.unsqueeze(1).to_broadcast(shape), ALU.mult), 3)
    then(dve.tensor_reduce(best, key, AX.X, ALU.max), 4)
    return dve.tensor_tensor(onehot, key, best.unsqueeze(2).to_broadcast(shape), ALU.is_equal)


def normalise_rows(dve, out, x, mean, rstd, groups):
    for j in range(groups):
        ins = dve.tensor_scalar(out[:, j, :], x[:, j, :], mean[:, j, :], rstd[:, j, :], ALU.subtract, ALU.mult)
    return ins


def gat(nc, K, T):
    G, N = 4, B // 4
    x_in = T["x"].rearrange("(g j) n d -> g n j d", j=G)
    with Phase(nc, "gat") as ph:
        x = ph.sb("x", [P, 4, G, P], F32)
        bn = ph.sb("bn", [P, 2, G, 6], F32)
        mv = ph.sb("mv", [P, 4, G, 2], F32)
        xn = ph.sb("xn", [P, 2, G, P], F32)
        xT = ph.sb("xT", [P, 2, G, P], F32)
        h = ph.sb("h", [P, 4, G, P], F32)
        es = ph.sb("es", [P, 2, G], F32)
        ev = ph.sb("ev", [P, 2, G, P], F32)
        el = ph.sb("el", [P, 2, G, P], F32)
        nmax = ph.sb("nmax", [P, 2, G], F32)
        pr = ph.sb("pr", [P, 2, G, P], F32)
        prsum = ph.sb("prsum", [P, 4, G], F32)
        rsum = ph.sb("rsum", [P, 4, G], F32)
        prT = ph.sb("prT", [P, 2, G, P], F32)
        hp = ph.sb("hp", [P, 2, G, P], F32)
        row = ph.sb("row", [P, 4, G, ROW], F32)
        bn2 = ph.sb("bn2", [P, 2, G, 6], F32)
        xn2 = ph.sb("xn2", [P, 2, G, P], F32)
        xT2 = ph.sb("xT2", [P, 2, G, P], F32)
        top = ph.sb("top", [P, G], F32)
        eq = ph.sb("eq", [P, G, E0], F32)
        key = ph.sb("key", [P, G, E0], F32)
        best = ph.sb("best", [P, G], F32)
        onehot = ph.sb("onehot", [P, 2, G, E0], BF16)
        place = ph.sb("place", [P, G, E0], F32)
        place1 = ph.sb("place1", [P, G, E0], F32)
        dest = ph.sb("dest", [P, G], F32)
        idx = ph.sb("idx", [P, 4, G], I32)

        ps_xT = ph.psum("ps_xT", [P, G, P])
        ps_ed = ph.psum("ps_ed", [P, G, P])
        ps_h = ph.psum("ps_h", [P, G, P])
        ps_es = ph.psum("ps_es", [P, 512])
        ps_prT = ph.psum("ps_prT", [P, G, P])
        ps_hp = ph.psum("ps_hp", [P, G, P])
        ps_xT2 = ph.psum("ps_xT2", [P, G, P])
        ps_r = ph.psum("ps_r", [P, 512])
        ps_logit = ps_r[:, 0:G * E0].rearrange("p (j e) -> p j e", j=G)
        ps_rank = ps_r[:, 256:256 + (G + 1) * E0].rearrange("p (j e) -> p j e", j=G + 1)

        x_loaded = ph.sems("x_loaded", 4)
        s_stats = ph.sem("s_stats")
        var_ready = ph.sem("var_ready")
        rstd_ready = ph.sem("rstd_ready")
        xn_ready = ph.sem("xn_ready")
        xn_turned = ph.sem("xn_turned")
        xT_ready = ph.sem("xT_ready")
        projected = ph.sem("projected")
        es_ready = ph.sem("es_ready")
        h_ready = ph.sem("h_ready")
        s_scores = ph.sem("s_scores")
        el_ready = ph.sem("el_ready")
        pr_ready = ph.sem("pr_ready")
        pr_turned = ph.sem("pr_turned")
        prT_ready = ph.sem("prT_ready")
        attended = ph.sem("attended")
        hp_ready = ph.sem("hp_ready")
        rsum_ready = ph.sem("rsum_ready")
        s_row = ph.sem("s_row")
        var2_ready = ph.sem("var2_ready")
        rstd2_ready = ph.sem("rstd2_ready")
        xn2_ready = ph.sem("xn2_ready")
        xn2_turned = ph.sem("xn2_turned")
        xT2_ready = ph.sem("xT2_ready")
        logit_ready = ph.sem("logit_ready")
        s_arg = ph.sem("s_arg")
        onehot_ready = ph.sem("onehot_ready")
        rank_ready = ph.sem("rank_ready")
        s_place = ph.sem("s_place")
        idx_ready = ph.sem("idx_ready")
        rows_stored = ph.sems("rows_stored", 4)
        block = ph.block()

        @block.sync
        def _(sp):
            def load(g, s, r):
                freed(sp, s_row, g, 4, per=3)
                src = x_in[g] if isinstance(g, int) else x_in[bass.ds(g, 1)].rearrange("o n j d -> (o n) j d")
                sp.dma_start(x[:, s], src).then_inc(x_loaded[s], 16)

            pipeline(sp, N, 4, [(0, load)])

        @block.gpsimd
        def _(pool):
            def rstd(g, s, r):
                pool.wait_ge(var_ready, g + 1)
                pool.tensor_tensor(mv[:, s, :, 1], mv[:, s, :, 1], K["minus_half"][:, 0:G],
                                   ALU.pow).then_inc(rstd_ready, 1)

            def rstd2(g, s, r):
                pool.wait_ge(var2_ready, g + 1)
                pool.tensor_tensor(row[:, s, :, RSTD], row[:, s, :, RSTD], K["minus_half"][:, 0:G],
                                   ALU.pow).then_inc(rstd2_ready, 1)

            def scatter(g, s, r):
                wait_alone(K, pool, idx_ready, g + 1)
                for j in range(G):
                    pool.indirect_dma_start(
                        K["sorted0"], bass.IndirectOffsetOnAxis(ap=idx[:, s, j:j + 1], axis=0),
                        row[:, s, j, :], None).then_inc(rows_stored[s], 16)

            pipeline(pool, N, 4, [(5, scatter), (3, rstd2), (0, rstd)])
            for s in range(4):
                pool.wait_ge(rows_stored[s], 16 * G * (N // 4))

        @block.vector
        def _(dve):
            def stats(g, s, r):
                dve.wait_ge(x_loaded[s], r * 16 + 16)
                for j in range(G):
                    ins = dve.bn_stats(bn[:, s % 2, j, :], x[:, s, j, :])
                ins.then_inc(s_stats, 1)
                wait_alone(K, dve, s_stats, g * 2 + 1)
                for j in range(G):
                    ins = dve.bn_aggr(mv[:, s, j, :], bn[:, s % 2, j, :])
                ins.then_inc(s_stats, 1)
                dve.wait_ge(s_stats, g * 2 + 2)
                dve.tensor_scalar(mv[:, s, :, 1], mv[:, s, :, 1], EPS, None, ALU.add).then_inc(var_ready, 1)

            def normalise(g, s, r):
                dve.wait_ge(rstd_ready, g + 1)
                freed(dve, xn_turned, g, 2)
                normalise_rows(dve, xn[:, s % 2], x[:, s], mv[:, s, :, 0:1], mv[:, s, :, 1:2],
                               G).then_inc(xn_ready, 1)

            def scores(g, s, r):
                dve.wait_ge(es_ready, g + 1)
                for j in range(G):
                    ins = dve.scalar_tensor_tensor(ev[:, s % 2, j, :], ps_ed[:, j, :], es[:, s % 2, j:j + 1],
                                                   K["cap"][:], ALU.add, ALU.min)
                ins.then_inc(s_scores, 1)
                dve.wait_ge(s_scores, g * 2 + 1)
                freed(dve, pr_ready, g, 2)
                dve.scalar_tensor_tensor(el[:, s % 2], ev[:, s % 2], SLOPE, ev[:, s % 2], ALU.mult,
                                         ALU.max).then_inc(s_scores, 1)
                dve.wait_ge(s_scores, g * 2 + 2)
                dve.tensor_reduce(nmax[:, s % 2], el[:, s % 2], AX.X, ALU.max, negate=True).then_inc(el_ready, 1)

            def inverse(g, s, r):
                dve.wait_ge(pr_ready, g + 1)
                dve.reciprocal(rsum[:, s], prsum[:, s]).then_inc(rsum_ready, 1)

            def residual(g, s, r):
                dve.wait_ge(hp_ready, g + 1)
                if not isinstance(r, int) or r:
                    dve.wait_ge(rows_stored[s], r * (16 * G))
                dve.tensor_tensor(row[:, s, :, 0:P], x[:, s], hp[:, s % 2], ALU.add).then_inc(s_row, 1)
                dve.wait_ge(s_row, g * 3 + 1)
                for j in range(G):
                    ins = dve.bn_stats(bn2[:, s % 2, j, :], row[:, s, j, 0:P])
                ins.then_inc(s_row, 1)
                wait_alone(K, dve, s_row, g * 3 + 2)
                for j in range(G):
                    ins = dve.bn_aggr(row[:, s, j, MEAN:RSTD + 1], bn2[:, s % 2, j, :])
                ins.then_inc(s_row, 1)
                dve.wait_ge(s_row, g * 3 + 3)
                dve.memset(row[:, s, :, PROB:NUM + 1], 0.0)
                dve.tensor_scalar(row[:, s, :, RSTD], row[:, s, :, RSTD], EPS, None, ALU.add).then_inc(var2_ready, 1)

            def normalise2(g, s, r):
                dve.wait_ge(rstd2_ready, g + 1)
                freed(dve, xn2_turned, g, 2)
                normalise_rows(dve, xn2[:, s % 2], row[:, s, :, 0:P], row[:, s, :, MEAN:MEAN + 1],
                               row[:, s, :, RSTD:RSTD + 1], G).then_inc(xn2_ready, 1)

            def choose(g, s, r):
                dve.wait_ge(logit_ready, g + 1)
                argmax_onehot(dve, s_arg, g * 4, ps_logit, top[:], eq[:], key[:], best[:], onehot[:, s % 2],
                              K["rev0"][:], G, E0).then_inc(onehot_ready, 1)

            def places(g, s, r):
                dve.wait_ge(rank_ready, g + 1)
                row_places(dve, s_place, g * 4, ps_rank, place[:], place1[:], dest[:], onehot[:, s % 2],
                           K["base0"][:], G, E0)
                first = g * G
                dve.tensor_scalar(K["dest0"][:, first:first + G] if isinstance(g, int) else
                                  K["dest0"][:, bass.ds(first, G)], dest[:], 0.0, None, ALU.add)
                dve.scalar_tensor_tensor(idx[:, s], dest[:], -1.0, dest[:], ALU.mult, ALU.max).then_inc(idx_ready, 1)

            pipeline(dve, N, 4, [(5, choose), (1, normalise), (2, scores), (5, places), (4, normalise2),
                                 (3, inverse), (3, residual), (0, stats)])

        @block.scalar
        def _(act):
            def relu(g, s, r):
                act.wait_ge(attended, g + 1)
                act.wait_ge(rsum_ready, g + 1)
                freed(act, s_row, g, 2, per=3)
                for j in range(G):
                    ins = act.activation(hp[:, s % 2, j, :], ps_hp[:, j, :], ACT.Relu, scale=rsum[:, s, j:j + 1])
                ins.then_inc(hp_ready, 1)

            def copy_xT(g, s, r):
                act.wait_ge(xn_turned, g + 1)
                freed(act, projected, g, 2)
                act.activation(xT[:, s % 2], ps_xT[:], ACT.Copy).then_inc(xT_ready, 1)

            def copy_h(g, s, r):
                act.wait_ge(projected, g + 1)
                freed(act, s_scores, g, 2, per=2)
                act.activation(es[:, s % 2], ps_es[:, 0:G], ACT.Copy).then_inc(es_ready, 1)
                freed(act, attended, g, 4)
                act.activation(h[:, s], ps_h[:], ACT.Copy).then_inc(h_ready, 1)

            def exps(g, s, r):
                act.wait_ge(el_ready, g + 1)
                freed(act, pr_turned, g, 2)
                for j in range(G):
                    ins = act.activation(pr[:, s % 2, j, :], el[:, s % 2, j, :], ACT.Exp,
                                         bias=nmax[:, s % 2, j:j + 1], accum_out=prsum[:, s, j:j + 1])
                ins.then_inc(pr_ready, 1)

            def copy_prT(g, s, r):
                act.wait_ge(pr_turned, g + 1)
                freed(act, attended, g, 2)
                act.activation(prT[:, s % 2], ps_prT[:], ACT.Copy).then_inc(prT_ready, 1)

            def copy_xT2(g, s, r):
                act.wait_ge(xn2_turned, g + 1)
                freed(act, logit_ready, g, 2)
                act.activation(xT2[:, s % 2], ps_xT2[:], ACT.Copy).then_inc(xT2_ready, 1)

            pipeline(act, N, 4, [(3, relu), (1, copy_xT), (1, copy_h), (2, exps), (4, copy_xT2), (2, copy_prT)])

        @block.tensor
        def _(pe):
            def attend(g, s, r):
                pe.wait_ge(prT_ready, g + 1)
                pe.wait_ge(h_ready, g + 1)
                freed(pe, hp_ready, g, 1)
                for j in range(G):
                    ins = pe.matmul(ps_hp[:, j, :], prT[:, s % 2, j, :], h[:, s, j, :], start=True, stop=True)
                ins.then_inc(attended, 1)

            def turn_x(g, s, r):
                pe.wait_ge(xn_ready, g + 1)
                freed(pe, xT_ready, g, 1)
                for j in range(G):
                    ins = pe.transpose(ps_xT[:, j, :], xn[:, s % 2, j, :], K["ident"][:])
                ins.then_inc(xn_turned, 1)

            def project(g, s, r):
                pe.wait_ge(xT_ready, g + 1)
                freed(pe, s_scores, g, 1, per=2)
                freed(pe, h_ready, g, 1)
                pe.matmul(ps_ed[:].rearrange("p j n -> p (j n)"), K["wa2"][:],
                          xT[:, s % 2].rearrange("p j n -> p (j n)"), start=True, stop=True)
                for j in range(G):
                    pe.matmul(ps_es[:, j:j + 1], xT[:, s % 2, j, :], K["wa"][:, 0:1], start=True, stop=True)
                for j in range(G):
                    ins = pe.matmul(ps_h[:, j, :], xT[:, s % 2, j, :], K["wh"][:], start=True, stop=True)
                ins.then_inc(projected, 1)

            def rank(g, s, r):
                pe.wait_ge(onehot_ready, g + 1)
                rank_rows(pe, K, ps_rank, onehot[:, s % 2], G).then_inc(rank_ready, 1)

            def turn_x2(g, s, r):
                pe.wait_ge(xn2_ready, g + 1)
                freed(pe, xT2_ready, g, 1)
                for j in range(G):
                    ins = pe.transpose(ps_xT2[:, j, :], xn2[:, s % 2, j, :], K["ident"][:])
                ins.then_inc(xn2_turned, 1)

            def turn_pr(g, s, r):
                pe.wait_ge(pr_ready, g + 1)
                freed(pe, prT_ready, g, 1)
                for j in range(G):
                    ins = pe.transpose(ps_prT[:, j, :], pr[:, s % 2, j, :], K["ident"][:])
                ins.then_inc(pr_turned, 1)

            def route(g, s, r):
                pe.wait_ge(xT2_ready, g + 1)
                freed(pe, idx_ready, g, 1)
                pe.matmul(ps_logit, K["onesb"][0:3, :],
                          K["biasrows"][:, RB_AT:RB_AT + E0].unsqueeze(1).to_broadcast([3, G, E0]),
                          start=True, stop=False, skip_group_check=True)
                for j in range(G):
                    ins = pe.matmul(ps_logit[:, j, :], xT2[:, s % 2, j, :], K["rwT"][:], start=False, stop=True,
                                    skip_group_check=True)
                ins.then_inc(logit_ready, 1)

            pipeline(pe, N, 4, [(3, attend), (1, turn_x), (5, rank), (1, project), (4, turn_x2), (2, turn_pr),
                                (4, route)])


def rank_rows(pe, K, ps_rank, onehot, groups):
    for j in range(groups):
        for k in range(j):
            pe.matmul(ps_rank[:, j, :], K["onesb"][:], onehot[:, k, :], start=(k == 0), stop=False,
                      skip_group_check=True)
        pe.matmul(ps_rank[:, j, :], K["before"][:], onehot[:, j, :], start=(j == 0), stop=True,
                  skip_group_check=True)
    for k in range(groups):
        ins = pe.matmul(ps_rank[:, groups, :], K["onesb"][:], onehot[:, k, :], start=(k == 0),
                        stop=(k == groups - 1), skip_group_check=True)
    return ins


def row_places(dve, sem, n0, ps_rank, place, place1, dest, onehot, base, groups, experts):
    shape = [P, groups, experts]
    dve.tensor_tensor(place, ps_rank[:, 0:groups, :], base.unsqueeze(1).to_broadcast(shape),
                      ALU.add).then_inc(sem, 1)
    dve.wait_ge(sem, n0 + 1)
    dve.tensor_tensor(place1, place, onehot, ALU.mult).then_inc(sem, 1)
    dve.tensor_tensor(base, base, ps_rank[:, groups, :], ALU.add).then_inc(sem, 1)
    dve.wait_ge(sem, n0 + 3)
    dve.tensor_reduce(dest, place1, AX.X, ALU.add).then_inc(sem, 1)
    dve.wait_ge(sem, n0 + 4)


def table(nc, K, layer):
    E, NT = ((E0, NT0), (E1, NT1))[layer]
    base, rows = K[f"base{layer}"], K[f"sorted{layer}"]
    with Phase(nc, f"table{layer}") as ph:
        ends = ph.sb("ends", [1, E], I32)
        rowsof = ph.sb("rowsof", [P, E], F32)
        full = ph.sb("full", [P, E], I32)
        shifted = ph.sb("shifted", [P, E], I32)
        tilesof = ph.sb("tilesof", [P, E], F32)
        cols = ph.sb("cols", [E, 3], F32)
        upto = ph.sb("upto", [E, 1], F32)
        before = ph.sb("before", [E, 1], F32)
        signed = ph.sb("signed", [E, 1], F32)
        origin = ph.sb("origin", [E, 1], F32)
        passed = ph.sb("passed", [E, NT], F32)
        reached = ph.sb("reached", [E, NT], F32)
        within = ph.sb("within", [E, NT], F32)
        surplus = ph.sb("surplus", [1, NT], F32)
        along = ph.sb("along", [1, NT], F32)
        first = ph.sb("first", [1, NT], F32)
        jump = ph.sb("jump", [P, E], F32)
        tiles_all = ph.sb("tiles_all", [P, 1], F32)
        lift = ph.sb("lift", [P, 1], F32)
        move = ph.sb("move", [P, 2, B], F32)
        placed = ph.sb("placed", [P, B], F32)
        flip = ph.sb("flip", [P, B], I32)
        unflipped = ph.sb("unflipped", [P, B], I32)
        pt = ph.psum("pt", [P, 512])
        pc = ph.psum("pc", [P, 512])
        pr = ph.psum("pr", [P, 512])
        ends_ready = ph.sem("ends_ready")
        tilesof_ready = ph.sem("tilesof_ready")
        turned = ph.sem("turned")
        cols_ready = ph.sem("cols_ready")
        summed = ph.sem("summed")
        passed_ready = ph.sem("passed_ready")
        listed = ph.sem("listed")
        dve_step = ph.sem("dve_step")
        pads_sp = ph.sem("pads_sp")
        pads_act = ph.sem("pads_act")
        block = ph.block()

        def pads(eng, half, sem):
            eng.wait_ge(ends_ready, 1)
            with eng.Fori(0, E // 2) as i:
                end = eng.value_load(ends[0:1, bass.ds(i * 2 + half, 1)], min_val=0, max_val=E // 2 * REGION - P)
                eng.dma_start(rows[bass.ds(end, P), :], K["padrow"][:]).then_inc(sem, 16)
            eng.wait_ge(sem, 16 * (E // 2))

        @block.sync
        def _(sp):
            pads(sp, 0, pads_sp)

        @block.scalar
        def _(act):
            pads(act, 1, pads_act)

        @block.tensor
        def _(pe):
            pe.wait_ge(tilesof_ready, 1)
            for k, rowform in enumerate((tilesof[:], K["sign"][:, 0:E], K["tile0"][:, 0:E])):
                ins = pe.transpose(pt[0:E, k * P:(k + 1) * P], rowform, K["ident"][:])
            ins.then_inc(turned, 1)
            pe.wait_ge(cols_ready, 1)
            pe.matmul(pc[0:E, 0:1], K["upto"][0:E, 0:E], cols[:, 0:1], start=True, stop=True).then_inc(summed, 1)
            pe.wait_ge(passed_ready, 1)
            pe.matmul(pt[0:1, 0:NT], K["onesf"][0:E, 0:1], passed[:], start=True, stop=True)
            pe.matmul(pc[0:1, 0:NT], origin[:], within[:], start=True, stop=True)
            pe.matmul(pr[0:1, 0:NT], cols[:, 1:2], within[:], start=True, stop=True).then_inc(listed, 1)

        @block.vector
        def _(dve):
            steps = [0]

            def then(ins):
                steps[0] += 1
                ins.then_inc(dve_step, 1)
                dve.wait_ge(dve_step, steps[0])

            dve.tensor_scalar(ends[:, 0::2], base[0:1, 0::2], 0.0, None, ALU.add)
            dve.tensor_scalar(ends[:, 1::2], base[0:1, 1::2], -1.0, float(1 - P), ALU.mult,
                              ALU.add).then_inc(ends_ready, 1)
            then(dve.tensor_tensor(rowsof[:], base[:], K["start"][:, 0:E], ALU.subtract))
            then(dve.tensor_scalar(full[:], rowsof[:], float(P - 1), None, ALU.add))
            then(dve.tensor_scalar(shifted[:], full[:], 7, None, ALU.logical_shift_right))
            dve.tensor_copy(tilesof[:], shifted[:]).then_inc(tilesof_ready, 1)
            dve.wait_ge(turned, 1)
            dve.tensor_copy(cols[:], pt[0:E, 0:3 * P].rearrange("e (k p) -> e k p", k=3)[:, :, 0]).then_inc(cols_ready, 1)
            dve.wait_ge(summed, 1)
            then(dve.tensor_copy(upto[:], pc[0:E, 0:1]))
            dve.tensor_tensor(before[:], upto[:], cols[:, 0:1], ALU.subtract)
            then(dve.tensor_scalar(passed[:], K["count"][0:E, 0:NT], upto[:], None, ALU.is_ge))
            dve.tensor_tensor(signed[:], before[:], cols[:, 1:2], ALU.mult)
            then(dve.tensor_scalar(reached[:], K["count"][0:E, 0:NT], before[:], None, ALU.is_ge))
            dve.tensor_tensor(origin[:], cols[:, 2:3], signed[:], ALU.subtract)
            dve.tensor_tensor(within[:], reached[:], passed[:], ALU.subtract).then_inc(passed_ready, 1)
            dve.wait_ge(listed, 1)
            dve.tensor_scalar(K["table"][0:1, 0, 0:NT], pt[0:1, 0:NT], float(E - 1), None, ALU.min)
            dve.tensor_scalar(surplus[:], pt[0:1, 0:NT], float(E), float(E // 2 * REGION // P), ALU.is_ge, ALU.mult)
            then(dve.tensor_tensor(along[:], pr[0:1, 0:NT], K["count"][0:1, 0:NT], ALU.mult))
            then(dve.tensor_tensor(first[:], pc[0:1, 0:NT], along[:], ALU.add))
            then(dve.tensor_tensor(along[:], first[:], surplus[:], ALU.add))
            then(dve.tensor_scalar(K["table"][0:1, 1, 0:NT], along[:], float(P), None, ALU.mult))
            if layer == 0:
                dve.memset(jump[:], 0.0)
                then(dve.tensor_reduce(tiles_all[:], tilesof[:, 0:E - 1], AX.X, ALU.add))
                then(dve.tensor_tensor(jump[:, 1:E - 1:2], tilesof[:, 1:E - 1:2], tilesof[:, 2:E:2], ALU.add))
                dve.tensor_copy(jump[:, 0:1], tilesof[:, 0:1])
                then(dve.tensor_tensor(jump[:, 2:E:2], tilesof[:, 0:E - 2:2], tilesof[:, 1:E - 1:2], ALU.add))
                dve.tensor_scalar(lift[:], tiles_all[:], float(P), float(E // 2 * REGION - 1), ALU.mult, ALU.add)
                dve.tensor_scalar(jump[:, 1:E - 1:2], jump[:, 1:E - 1:2], -float(P), -float(REGION), ALU.mult, ALU.add)
                dve.tensor_scalar(jump[:, 0:1], jump[:, 0:1], -float(P), float(1 - REGION), ALU.mult, ALU.add)
                then(dve.tensor_scalar(jump[:, 2:E:2], jump[:, 2:E:2], float(P), -float(REGION), ALU.mult, ALU.add))
                dest = K["dest0"]
                dve.tensor_scalar(flip[:], dest[:], 0.0, float(P - 1), ALU.is_lt, ALU.mult)
                then(dve.tensor_scalar(placed[:], dest[:], lift[:], None, ALU.add))
                upwards = list(range(E - 3, 0, -2)) + list(range(0, E, 2))
                for n, e in enumerate(upwards):
                    start = e // 2 * REGION if e % 2 == 0 else 1 - (e + 1) // 2 * REGION
                    then(dve.tensor_scalar(move[:, n % 2, :], dest[:], float(start), jump[:, e:e + 1],
                                           ALU.is_ge, ALU.mult))
                    then(dve.tensor_tensor(placed[:], placed[:], move[:, n % 2, :], ALU.add))
                then(dve.tensor_copy(unflipped[:], placed[:]))
                then(dve.tensor_tensor(K["place0"][:], unflipped[:], flip[:], ALU.bitwise_xor))


def load_tiles(sp, K, rows, x, sem, g, G, limit):
    for j in range(G):
        tile = g * G + j
        at = K["table"][0:1, 1, tile:tile + 1] if isinstance(g, int) else K["table"][0:1, 1, bass.ds(tile, 1)]
        row = sp.value_load(at, min_val=0, max_val=limit)
        sp.dma_start(x[:, j, :], rows[bass.ds(row, P), :]).then_inc(sem, 16)


def tile_expert(pe, K, g, j, G, experts):
    tile = g * G + j
    at = K["table"][0:1, 0, tile:tile + 1] if isinstance(g, int) else K["table"][0:1, 0, bass.ds(tile, 1)]
    return pe.value_load(at, min_val=0, max_val=experts - 1)


def expert0(nc, K):
    G, N = 4, NT0 // 4
    y_out = K["mixed0"].rearrange("(g j p) d -> g p j d", j=G, p=P)
    with Phase(nc, "expert0") as ph:
        x = ph.sb("x", [P, 4, G, ROW], F32)
        xn = ph.sb("xn", [P, 2, G, P], F32)
        xT = ph.sb("xT", [P, 2, G, P], F32)
        hid = ph.sb("hid", [P, 2, G, H0], F32)
        hT = ph.sb("hT", [H0, 2, G, P], F32)
        y = ph.sb("y", [P, 4, G, P], F32)
        ps_xT = ph.psum("ps_xT", [P, G, P])
        ps_hid = ph.psum("ps_hid", [P, G, H0])
        ps_hT = ph.psum("ps_hT", [P, G, P])
        ps_y = ph.psum("ps_y", [P, G, P])
        x_loaded = ph.sems("x_loaded", 4)
        xn_ready = ph.sem("xn_ready")
        xn_turned = ph.sem("xn_turned")
        xT_ready = ph.sem("xT_ready")
        hid_done = ph.sem("hid_done")
        hid_ready = ph.sem("hid_ready")
        hid_turned = ph.sem("hid_turned")
        hT_ready = ph.sem("hT_ready")
        y_done = ph.sem("y_done")
        y_ready = ph.sem("y_ready")
        y_stored = ph.sems("y_stored", 4)
        block = ph.block()

        @block.sync
        def _(sp):
            def load(g, s, r):
                if not isinstance(g, int) or g >= 4:
                    wait_alone(K, sp, y_ready, g - 3)
                load_tiles(sp, K, K["sorted0"], x[:, s], x_loaded[s], g, G, E0 // 2 * REGION)

            pipeline(sp, N, 4, [(0, load)])

        @block.gpsimd
        def _(pool):
            def store(g, s, r):
                wait_alone(K, pool, y_ready, g + 1)
                dst = y_out[g] if isinstance(g, int) else y_out[bass.ds(g, 1)].rearrange("o p j d -> (o p) j d")
                pool.dma_start(dst, y[:, s]).then_inc(y_stored[s], 16)

            pipeline(pool, N, 4, [(3, store)])
            for s in range(4):
                pool.wait_ge(y_stored[s], 16 * (N // 4))

        @block.vector
        def _(dve):
            def normalise(g, s, r):
                dve.wait_ge(x_loaded[s], r * (16 * G) + 16 * G)
                freed(dve, xn_turned, g, 2)
                normalise_rows(dve, xn[:, s % 2], x[:, s, :, 0:P], x[:, s, :, MEAN:MEAN + 1],
                               x[:, s, :, RSTD:RSTD + 1], G).then_inc(xn_ready, 1)

            def finish(g, s, r):
                dve.wait_ge(y_done, g + 1)
                if not isinstance(r, int) or r:
                    dve.wait_ge(y_stored[s], r * 16)
                dve.scalar_tensor_tensor(y[:, s], ps_y[:], 0.0, x[:, s, :, 0:P], ALU.max,
                                         ALU.add).then_inc(y_ready, 1)

            pipeline(dve, N, 4, [(3, finish), (1, normalise)])

        @block.scalar
        def _(act):
            def copy_xT(g, s, r):
                act.wait_ge(xn_turned, g + 1)
                freed(act, hid_done, g, 2)
                act.activation(xT[:, s % 2], ps_xT[:], ACT.Copy).then_inc(xT_ready, 1)

            def relu(g, s, r):
                act.wait_ge(hid_done, g + 1)
                freed(act, hid_turned, g, 2)
                act.activation(hid[:, s % 2], ps_hid[:], ACT.Relu).then_inc(hid_ready, 1)

            def copy_hT(g, s, r):
                act.wait_ge(hid_turned, g + 1)
                freed(act, y_done, g, 2)
                act.activation(hT[:, s % 2], ps_hT[0:H0], ACT.Copy).then_inc(hT_ready, 1)

            pipeline(act, N, 4, [(2, relu), (1, copy_xT), (2, copy_hT)])

        @block.tensor
        def _(pe):
            def turn_x(g, s, r):
                pe.wait_ge(xn_ready, g + 1)
                freed(pe, xT_ready, g, 1)
                for j in range(G):
                    ins = pe.transpose(ps_xT[:, j, :], xn[:, s % 2, j, :], K["ident"][:])
                ins.then_inc(xn_turned, 1)

            def hidden(g, s, r):
                e = [tile_expert(pe, K, g, j, G, E0) for j in range(G)]
                pe.wait_ge(xT_ready, g + 1)
                freed(pe, hid_ready, g, 1)
                for j in range(G):
                    pe.matmul(ps_hid[:, j, :], K["onesb"][0:3, :], K["biasrows"][:, bass.ds(e[j] * H0 + B1_AT, H0)],
                              start=(j == 0), stop=False, skip_group_check=True)
                    ins = pe.matmul(ps_hid[:, j, :], xT[:, s % 2, j, :],
                                    K["w1e"][:, bass.ds(e[j], 1), :].rearrange("p o h -> p (o h)"),
                                    start=False, stop=True, skip_group_check=True)
                ins.then_inc(hid_done, 1)

            def turn_hid(g, s, r):
                pe.wait_ge(hid_ready, g + 1)
                freed(pe, hT_ready, g, 1)
                for j in range(G):
                    ins = pe.transpose(ps_hT[0:H0, j, :], hid[:, s % 2, j, :], K["ident"][:])
                ins.then_inc(hid_turned, 1)

            def mix(g, s, r):
                e = [tile_expert(pe, K, g, j, G, E0) for j in range(G)]
                pe.wait_ge(hT_ready, g + 1)
                freed(pe, y_ready, g, 1)
                for j in range(G):
                    pe.matmul(ps_y[:, j, :], K["onesb"][0:3, :], K["biasrows"][:, bass.ds(e[j] * P + B2_AT, P)],
                              start=(j == 0), stop=False, skip_group_check=True)
                    ins = pe.matmul(ps_y[:, j, :], hT[:, s % 2, j, :],
                                    K["w2e"][:, bass.ds(e[j], 1), :].rearrange("p o h -> p (o h)"),
                                    start=False, stop=True, skip_group_check=True)
                ins.then_inc(y_done, 1)

            pipeline(pe, N, 4, [(2, hidden), (3, mix), (1, turn_x), (2, turn_hid)])


def mha(nc, K):
    G, N, U = 2, B // 2, 8
    J = G * HEADS
    SCALE = float(HD) ** -0.5
    x_out = K["x3"].rearrange("(g j p) d -> g p j d", j=G, p=P)
    with Phase(nc, "mha") as ph:
        idx = ph.sb("idx", [P, U, G], I32)
        x = ph.sb("x", [P, U, G, P], F32)
        bn = ph.sb("bn", [P, 2, G, 6], F32)
        mv = ph.sb("mv", [P, 4, G, 2], F32)
        xn = ph.sb("xn", [P, 2, G, P], F32)
        xT = ph.sb("xT", [P, 2, G, P], F32)
        qT = ph.sb("qT", [P, 2, G, P], F32)
        mx = ph.sb("mx", [P, J], F32)
        pr = ph.sb("pr", [P, 2, J, P], F32)
        prT = ph.sb("prT", [P, 2, J, P], F32)
        rs = ph.sb("rs", [P, J], F32)
        o = ph.sb("o", [P, 2, J, HD], F32)
        oT = ph.sb("oT", [P, 2, G, P], F32)
        kbd, vaug = K["kbd"], K["vaug"]

        ps_a = ph.psum("ps_a", [P, 512])
        ps_xT = ps_a[:, 0:G * P].rearrange("p (j n) -> p j n", j=G)
        ps_out = ps_a[:, G * P:2 * G * P].rearrange("p (j n) -> p j n", j=G)
        ps_qk = ph.psum("ps_qk", [P, 2, G * P])
        ps_b = ph.psum("ps_b", [P, 512])
        ps_v = ps_b[:, 0:G * P].rearrange("p (j n) -> p j n", j=G)
        ps_oT = ps_b[:, G * P:2 * G * P].rearrange("p (j n) -> p j n", j=G)
        ps_s = ph.psum("ps_s", [P, J, P])
        ps_prT = ph.psum("ps_prT", [P, J, P])
        ps_o = ph.psum("ps_o", [P, 512])
        ps_oh = ps_o[:, 0:J * (HD + 1)].rearrange("p (j d) -> p j d", j=J)

        idx_ready = ph.sem("idx_ready")
        x_loaded = ph.sems("x_loaded", U)
        s_stats = ph.sem("s_stats")
        var_ready = ph.sem("var_ready")
        rstd_ready = ph.sem("rstd_ready")
        xn_ready = ph.sem("xn_ready")
        xn_turned = ph.sem("xn_turned")
        xT_ready = ph.sem("xT_ready")
        qk_done = ph.sem("qk_done")
        v_done = ph.sem("v_done")
        q_ready = ph.sem("q_ready")
        k_ready = ph.sem("k_ready")
        v_ready = ph.sem("v_ready")
        scored = ph.sem("scored")
        mx_ready = ph.sem("mx_ready")
        less_ready = ph.sem("less_ready")
        pr_ready = ph.sem("pr_ready")
        pr_turned = ph.sem("pr_turned")
        prT_ready = ph.sem("prT_ready")
        attended = ph.sem("attended")
        rs_ready = ph.sem("rs_ready")
        o_ready = ph.sem("o_ready")
        o_turned = ph.sem("o_turned")
        oT_ready = ph.sem("oT_ready")
        out_done = ph.sem("out_done")
        x3_ready = ph.sem("x3_ready")
        x3_stored = ph.sems("x3_stored", U)
        block = ph.block()

        @block.sync
        def _(sp):
            def store(g, s, r):
                sp.wait_ge(x3_ready, g + 1)
                dst = x_out[g] if isinstance(g, int) else x_out[bass.ds(g, 1)].rearrange("o p j d -> (o p) j d")
                sp.dma_start(dst, x[:, s]).then_inc(x3_stored[s], 16)

            pipeline(sp, N, U, [(7, store)])
            for s in range(U):
                sp.wait_ge(x3_stored[s], 16 * (N // U))

        @block.gpsimd
        def _(pool):
            def gather(g, s, r):
                wait_alone(K, pool, idx_ready, g + 1)
                if not isinstance(r, int) or r:
                    wait_alone(K, pool, x3_stored[s], r * 16)
                for j in range(G):
                    pool.indirect_dma_start(
                        x[:, s, j, :], None, K["mixed0"],
                        bass.IndirectOffsetOnAxis(ap=idx[:, s, j:j + 1], axis=0)).then_inc(x_loaded[s], 16)

            def rstd(g, s, r):
                pool.wait_ge(var_ready, g + 1)
                pool.tensor_tensor(mv[:, s % 4, :, 1], mv[:, s % 4, :, 1], K["minus_half"][:, 0:G],
                                   ALU.pow).then_inc(rstd_ready, 1)

            pipeline(pool, N, U, [(0, gather), (1, rstd)])

        @block.vector
        def _(dve):
            def indices(g, s, r):
                freed(dve, var_ready, g, U)
                first = g * G
                src = K["place0"][:, first:first + G] if isinstance(g, int) else K["place0"][:, bass.ds(first, G)]
                dve.tensor_copy(idx[:, s], src).then_inc(idx_ready, 1)

            def stats(g, s, r):
                dve.wait_ge(x_loaded[s], r * (16 * G) + 16 * G)
                for j in range(G):
                    ins = dve.bn_stats(bn[:, s % 2, j, :], x[:, s, j, :])
                ins.then_inc(s_stats, 1)
                wait_alone(K, dve, s_stats, g * 2 + 1)
                for j in range(G):
                    ins = dve.bn_aggr(mv[:, s % 4, j, :], bn[:, s % 2, j, :])
                ins.then_inc(s_stats, 1)
                dve.wait_ge(s_stats, g * 2 + 2)
                dve.tensor_scalar(mv[:, s % 4, :, 1], mv[:, s % 4, :, 1], EPS, None, ALU.add).then_inc(var_ready, 1)

            def normalise(g, s, r):
                dve.wait_ge(rstd_ready, g + 1)
                freed(dve, xn_turned, g, 2)
                normalise_rows(dve, xn[:, s % 2], x[:, s], mv[:, s % 4, :, 0:1], mv[:, s % 4, :, 1:2],
                               G).then_inc(xn_ready, 1)

            def values(g, s, r):
                dve.wait_ge(v_done, g + 1)
                freed(dve, attended, g, 4)
                dve.tensor_tensor(vaug[:, s % 4, :, 0:HD], ps_v.rearrange("p j (h d) -> p (j h) d", h=HEADS),
                                  K["bvg"][:].rearrange("p (j d) -> p j d", j=J), ALU.add).then_inc(v_ready, 1)

            def less_max(g, s, r):
                dve.wait_ge(scored, g + 1)
                dve.tensor_reduce(mx[:], ps_s[:], AX.X, ALU.max).then_inc(mx_ready, 1)
                dve.wait_ge(mx_ready, g + 1)
                freed(dve, pr_turned, g, 2)
                dve.tensor_tensor(pr[:, s % 2], ps_s[:], mx[:].unsqueeze(2).to_broadcast([P, J, P]),
                                  ALU.subtract).then_inc(less_ready, 1)

            def weigh(g, s, r):
                dve.wait_ge(attended, g + 1)
                dve.reciprocal(rs[:], ps_oh[:, :, HD]).then_inc(rs_ready, 1)
                dve.wait_ge(rs_ready, g + 1)
                freed(dve, o_turned, g, 2)
                dve.scalar_tensor_tensor(o[:, s % 2], ps_oh[:, :, 0:HD], K["linked"][:],
                                         rs[:].unsqueeze(2).to_broadcast([P, J, HD]), ALU.mult,
                                         ALU.mult).then_inc(o_ready, 1)

            def residual(g, s, r):
                dve.wait_ge(out_done, g + 1)
                dve.tensor_tensor(x[:, s], ps_out, x[:, s], ALU.add).then_inc(x3_ready, 1)

            pipeline(dve, N, U, [(0, indices), (2, normalise), (7, residual), (6, weigh), (3, values),
                                 (4, less_max), (1, stats)])

        @block.scalar
        def _(act):
            def exps(g, s, r):
                act.wait_ge(less_ready, g + 1)
                act.activation(pr[:, s % 2], pr[:, s % 2], ACT.Exp, scale=SCALE).then_inc(pr_ready, 1)

            def copy_q(g, s, r):
                act.wait_ge(qk_done, g + 1)
                freed(act, scored, g, 2)
                act.activation(qT[:, s % 2], ps_qk[:, 0, :].rearrange("p (j n) -> p j n", j=G), ACT.Identity,
                               bias=K["bqk"][:, 0:1]).then_inc(q_ready, 1)

            def copy_k(g, s, r):
                for hd in range(HEADS):
                    part = slice(hd * HD, (hd + 1) * HD)
                    ins = act.activation(kbd[part, s % 2, :, hd, :], ps_qk[part, 1, :].rearrange("p (j n) -> p j n", j=G),
                                         ACT.Identity, bias=K["bqk"][part, 1:2])
                ins.then_inc(k_ready, 1)

            def copy_xT(g, s, r):
                act.wait_ge(xn_turned, g + 1)
                freed(act, v_done, g, 2)
                act.activation(xT[:, s % 2], ps_xT, ACT.Copy).then_inc(xT_ready, 1)

            def copy_prT(g, s, r):
                act.wait_ge(pr_turned, g + 1)
                freed(act, attended, g, 2)
                for j in range(G):
                    ins = act.activation(prT[:, s % 2, j * HEADS:(j + 1) * HEADS],
                                         ps_prT[:, j * HEADS:(j + 1) * HEADS, :], ACT.Copy)
                ins.then_inc(prT_ready, 1)

            def copy_oT(g, s, r):
                act.wait_ge(o_turned, g + 1)
                freed(act, out_done, g, 1)
                act.activation(oT[:, s % 2], ps_oT, ACT.Copy).then_inc(oT_ready, 1)

            pipeline(act, N, U, [(5, exps), (3, copy_q), (3, copy_k), (2, copy_xT), (5, copy_prT), (6, copy_oT)])

        @block.tensor
        def _(pe):
            def upto(count):
                return min(count, N) if isinstance(count, int) else count

            def out(g, s, r):
                pe.wait_ge(oT_ready, g + 1)
                pe.wait_ge(xT_ready, upto(g + 5))
                freed(pe, x3_ready, g, 1)
                pe.matmul(ps_out, K["onesb"][0:3, :],
                          K["biasrows"][:, BO_AT:BO_AT + P].unsqueeze(1).to_broadcast([3, G, P]),
                          start=True, stop=False, skip_group_check=True)
                for j in range(G):
                    ins = pe.matmul(ps_out[:, j, :], oT[:, s % 2, j, :], K["woT"][:], start=False, stop=True,
                                    skip_group_check=True)
                ins.then_inc(out_done, 1)

            def attend(g, s, r):
                pe.wait_ge(prT_ready, g + 1)
                freed(pe, o_ready, g, 1)
                for j in range(J):
                    ins = pe.matmul(ps_oh[:, j, :], prT[:, s % 2, j, :], vaug[:, s % 4, j, :], start=True, stop=True)
                ins.then_inc(attended, 1)

            def project(g, s, r):
                flat = xT[:, s % 2].rearrange("p j n -> p (j n)")
                pe.wait_ge(xT_ready, g + 1)
                freed(pe, k_ready, g, 1)
                pe.matmul(ps_qk[:, 0, :], K["wqT"][:], flat, start=True, stop=True)
                pe.matmul(ps_qk[:, 1, :], K["wkT"][:], flat, start=True, stop=True).then_inc(qk_done, 1)
                freed(pe, v_ready, g, 1)
                freed(pe, oT_ready, g, 4)
                for j in range(G):
                    ins = pe.matmul(ps_v[:, j, :], xT[:, s % 2, j, :], K["wvT"][:], start=True, stop=True)
                ins.then_inc(v_done, 1)

            def turn_x(g, s, r):
                pe.wait_ge(xn_ready, g + 1)
                freed(pe, xT_ready, g, 1)
                freed(pe, x3_ready, g, 5)
                for j in range(G):
                    ins = pe.transpose(ps_xT[:, j, :], xn[:, s % 2, j, :], K["ident"][:])
                ins.then_inc(xn_turned, 1)

            def turn_pr(g, s, r):
                pe.wait_ge(pr_ready, g + 1)
                freed(pe, prT_ready, g, 1)
                for j in range(J):
                    ins = pe.transpose(ps_prT[:, j, :], pr[:, s % 2, j, :], K["ident"][:])
                ins.then_inc(pr_turned, 1)

            def score(g, s, r):
                pe.wait_ge(k_ready, g + 1)
                freed(pe, less_ready, g, 1)
                for j in range(G):
                    rows = ps_s[:, j * HEADS:(j + 1) * HEADS, :]
                    pe.matmul(rows, K["identb"][:], K["far"][:].unsqueeze(1).to_broadcast([P, HEADS, P]),
                              start=True, stop=False)
                    ins = pe.matmul(rows, qT[:, s % 2, j, :], kbd[:, s % 2, j], start=False, stop=True)
                ins.then_inc(scored, 1)

            def turn_o(g, s, r):
                pe.wait_ge(o_ready, g + 1)
                pe.wait_ge(v_ready, upto(g + 4))
                freed(pe, oT_ready, g, 1)
                for j in range(G):
                    ins = pe.transpose(ps_oT[:, j, :],
                                       o[:, s % 2, j * HEADS:(j + 1) * HEADS].rearrange("p h d -> p (h d)"),
                                       K["ident"][:])
                ins.then_inc(o_turned, 1)

            pipeline(pe, N, U, [(7, out), (6, attend), (3, project), (2, turn_x), (5, turn_pr), (4, score),
                                (6, turn_o)])


def hidden_layer(pe, K, ps_h, xhi, xlo, gelu_done, h_done, g):
    for c in range(NCH):
        cols = slice(c * P, (c + 1) * P)
        freed(pe, gelu_done, g, 1, per=NCH, k=c + 1)
        pe.matmul(ps_h[:, c, :], K["w1lo"][:, cols], xhi, start=True, stop=False)
        pe.matmul(ps_h[:, c, :], K["w1hi"][:, cols], xlo, start=False, stop=False)
        pe.matmul(ps_h[:, c, :], K["w1hi"][:, cols], xhi, start=False, stop=True).then_inc(h_done, 1)


def gate(nc, K):
    G, N, U = 4, B // 4, 8
    x_in = K["x3"].rearrange("(g j p) d -> g p j d", j=G, p=P)
    with Phase(nc, "gate") as ph:
        row = ph.sb("row", [P, U, G, ROW], F32)
        bn = ph.sb("bn", [P, 2, G, 6], F32)
        xn = ph.sb("xn", [P, 2, G, P], F32)
        xhi = ph.sb("xhi", [P, 2, G * P], F16)
        xlo = ph.sb("xlo", [P, 2, G * P], F16)
        h = ph.sb("h", [P, 2, NCH, G * P], F32)
        top = ph.sb("top", [P, G], F32)
        eq = ph.sb("eq", [P, G, E1], F32)
        key = ph.sb("key", [P, G, E1], F32)
        best = ph.sb("best", [P, G], F32)
        onehot = ph.sb("onehot", [P, 2, G, E1], BF16)
        less = ph.sb("less", [P, G, E1], F32)
        th = ph.sb("th", [P, G, E1], F32)
        den = ph.sb("den", [P, G, E1], F32)
        rden = ph.sb("rden", [P, G, E1], F32)
        ex = ph.sb("ex", [P, G, E1], F32)
        total = ph.sb("total", [P, G], F32)
        place = ph.sb("place", [P, G, E1], F32)
        place1 = ph.sb("place1", [P, G, E1], F32)
        dest = ph.sb("dest", [P, G], F32)
        idx = ph.sb("idx", [P, U, G], I32)
        ps_xT = ph.psum("ps_xT", [P, G * P])
        ps_h = ph.psum("ps_h", [P, NCH, G * P])
        ps_r = ph.psum("ps_r", [P, 512])
        ps_logit = ps_r[:, 0:G * E1].rearrange("p (j e) -> p j e", j=G)
        ps_rank = ps_r[:, 256:256 + (G + 1) * E1].rearrange("p (j e) -> p j e", j=G + 1)
        x_loaded = ph.sems("x_loaded", U)
        s_stats = ph.sem("s_stats")
        var_ready = ph.sem("var_ready")
        rstd_ready = ph.sem("rstd_ready")
        xn_ready = ph.sem("xn_ready")
        xn_turned = ph.sem("xn_turned")
        xhi_ready = ph.sem("xhi_ready")
        xlo_ready = ph.sem("xlo_ready")
        h_done = ph.sem("h_done")
        gelu_done = ph.sem("gelu_done")
        logit_ready = ph.sem("logit_ready")
        s_arg = ph.sem("s_arg")
        onehot_ready = ph.sem("onehot_ready")
        less_ready = ph.sem("less_ready")
        th_ready = ph.sem("th_ready")
        rank_ready = ph.sem("rank_ready")
        s_place = ph.sem("s_place")
        s_prob = ph.sem("s_prob")
        idx_ready = ph.sem("idx_ready")
        rows_stored = ph.sems("rows_stored", U)
        block = ph.block()

        @block.sync
        def _(sp):
            def load(g, s, r):
                if not isinstance(r, int) or r:
                    sp.wait_ge(rows_stored[s], r * (16 * G))
                src = x_in[g] if isinstance(g, int) else x_in[bass.ds(g, 1)].rearrange("o p j d -> (o p) j d")
                sp.dma_start(row[:, s, :, 0:P], src).then_inc(x_loaded[s], 16)

            pipeline(sp, N, U, [(0, load)])

        @block.gpsimd
        def _(pool):
            def rstd(g, s, r):
                pool.wait_ge(var_ready, g + 1)
                pool.tensor_tensor(row[:, s, :, RSTD], row[:, s, :, RSTD], K["minus_half"][:, 0:G],
                                   ALU.pow).then_inc(rstd_ready, 1)

            def scatter(g, s, r):
                wait_alone(K, pool, idx_ready, g + 1)
                for j in range(G):
                    pool.indirect_dma_start(
                        K["sorted1"], bass.IndirectOffsetOnAxis(ap=idx[:, s, j:j + 1], axis=0),
                        row[:, s, j, :], None).then_inc(rows_stored[s], 16)

            pipeline(pool, N, U, [(5, scatter), (1, rstd)])
            for s in range(U):
                pool.wait_ge(rows_stored[s], 16 * G * (N // U))

        @block.vector
        def _(dve):
            def stats(g, s, r):
                dve.wait_ge(x_loaded[s], r * 16 + 16)
                for j in range(G):
                    ins = dve.bn_stats(bn[:, s % 2, j, :], row[:, s, j, 0:P])
                ins.then_inc(s_stats, 1)
                wait_alone(K, dve, s_stats, g * 2 + 1)
                for j in range(G):
                    ins = dve.bn_aggr(row[:, s, j, MEAN:RSTD + 1], bn[:, s % 2, j, :])
                ins.then_inc(s_stats, 1)
                dve.wait_ge(s_stats, g * 2 + 2)
                dve.tensor_scalar(row[:, s, :, RSTD], row[:, s, :, RSTD], EPS, None, ALU.add).then_inc(var_ready, 1)

            def normalise(g, s, r):
                dve.wait_ge(rstd_ready, g + 1)
                freed(dve, xn_turned, g, 2)
                normalise_rows(dve, xn[:, s % 2], row[:, s, :, 0:P], row[:, s, :, MEAN:MEAN + 1],
                               row[:, s, :, RSTD:RSTD + 1], G).then_inc(xn_ready, 1)

            def low_part(g, s, r):
                dve.wait_ge(xhi_ready, g + 1)
                freed(dve, h_done, g, 2, per=NCH, k=NCH)
                dve.tensor_tensor(xlo[:, s % 2], ps_xT[:], xhi[:, s % 2], ALU.subtract).then_inc(xlo_ready, 1)

            def choose(g, s, r):
                dve.wait_ge(logit_ready, g + 1)
                argmax_onehot(dve, s_arg, g * 4, ps_logit, top[:], eq[:], key[:], best[:], onehot[:, s % 2],
                              K["rev0"][:, E0 - E1:E0], G, E1).then_inc(onehot_ready, 1)
                dve.tensor_tensor(less[:], ps_logit, top[:].unsqueeze(2).to_broadcast([P, G, E1]),
                                  ALU.subtract).then_inc(less_ready, 1)

            def probability(g, s, r):
                dve.wait_ge(th_ready, g + 1)
                dve.tensor_scalar(den[:], th[:], -1.0, 1.0, ALU.mult, ALU.add).then_inc(s_prob, 1)
                dve.wait_ge(s_prob, g * 4 + 1)
                dve.reciprocal(rden[:], den[:]).then_inc(s_prob, 1)
                dve.wait_ge(s_prob, g * 4 + 2)
                dve.scalar_tensor_tensor(ex[:], th[:], 1.0, rden[:], ALU.add, ALU.mult).then_inc(s_prob, 1)
                dve.wait_ge(s_prob, g * 4 + 3)
                dve.tensor_reduce(total[:], ex[:], AX.X, ALU.add).then_inc(s_prob, 1)
                dve.wait_ge(s_prob, g * 4 + 4)
                dve.reciprocal(row[:, s, :, PROB], total[:])

            def places(g, s, r):
                dve.wait_ge(rank_ready, g + 1)
                row_places(dve, s_place, g * 4, ps_rank, place[:], place1[:], dest[:], onehot[:, s % 2],
                           K["base1"][:], G, E1)
                first = g * G
                number = K["number"][:, first:first + G] if isinstance(g, int) else K["number"][:, bass.ds(first, G)]
                dve.tensor_copy(row[:, s, :, NUM:NUM + 1].bitcast(I32).rearrange("p j o -> p (j o)"), number)
                dve.scalar_tensor_tensor(idx[:, s], dest[:], -1.0, dest[:], ALU.mult, ALU.max).then_inc(idx_ready, 1)

            pipeline(dve, N, U, [(5, choose), (2, normalise), (1, stats), (2, low_part), (5, probability),
                                 (5, places)])

        @block.scalar
        def _(act):
            def high_part(g, s, r):
                act.wait_ge(xn_turned, g + 1)
                freed(act, h_done, g, 2, per=NCH, k=NCH)
                act.activation(xhi[:, s % 2], ps_xT[:], ACT.Copy).then_inc(xhi_ready, 1)

            def tanh(g, s, r):
                act.wait_ge(less_ready, g + 1)
                act.activation(th[:], less[:], ACT.Tanh, scale=0.5).then_inc(th_ready, 1)

            def gelu(g, s, r):
                freed(act, logit_ready, g, 2)
                for c in range(NCH):
                    act.wait_ge(h_done, g * NCH + c + 1)
                    act.activation(h[:, s % 2, c, :], ps_h[:, c, :], ACT.Gelu,
                                   bias=K["b1"][:, c:c + 1]).then_inc(gelu_done, 1)

            pipeline(act, N, U, [(2, high_part), (5, tanh), (3, gelu)])

        @block.tensor
        def _(pe):
            def logits(g, s, r):
                pe.wait_ge(gelu_done, g * NCH + NCH)
                freed(pe, idx_ready, g, 1)
                pe.matmul(ps_logit, K["onesb"][0:3, :],
                          K["biasrows"][:, BG_AT:BG_AT + E1].unsqueeze(1).to_broadcast([3, G, E1]),
                          start=True, stop=False, skip_group_check=True)
                for j in range(G):
                    for c in range(NCH):
                        ins = pe.matmul(ps_logit[:, j, :], h[:, s % 2, c, j * P:(j + 1) * P], K["wg"][:, c, :],
                                        start=False, stop=(c == NCH - 1), skip_group_check=True)
                ins.then_inc(logit_ready, 1)

            def turn_x(g, s, r):
                pe.wait_ge(xn_ready, g + 1)
                freed(pe, xlo_ready, g, 1)
                for j in range(G):
                    ins = pe.transpose(ps_xT[:, j * P:(j + 1) * P], xn[:, s % 2, j, :], K["ident"][:])
                ins.then_inc(xn_turned, 1)

            def rank(g, s, r):
                pe.wait_ge(onehot_ready, g + 1)
                pe.wait_ge(less_ready, g + 1)
                rank_rows(pe, K, ps_rank, onehot[:, s % 2], G).then_inc(rank_ready, 1)

            def hidden(g, s, r):
                pe.wait_ge(xlo_ready, g + 1)
                hidden_layer(pe, K, ps_h, xhi[:, s % 2], xlo[:, s % 2], gelu_done, h_done, g)

            pipeline(pe, N, U, [(2, turn_x), (5, rank), (3, hidden), (4, logits)])


def expert1(nc, K, out_rows):
    G, N = 4, NT1 // 4
    with Phase(nc, "expert1") as ph:
        x = ph.sb("x", [P, 4, G, ROW], F32)
        xn = ph.sb("xn", [P, 2, G, P], F32)
        xhi = ph.sb("xhi", [P, 2, G * P], F16)
        xlo = ph.sb("xlo", [P, 2, G * P], F16)
        h = ph.sb("h", [P, 2, NCH, G * P], F32)
        y = ph.sb("y", [P, 4, G, P], F32)
        ps_xT = ph.psum("ps_xT", [P, G * P])
        ps_h = ph.psum("ps_h", [P, NCH, G * P])
        ps_y = ph.psum("ps_y", [P, G, P])
        x_loaded = ph.sems("x_loaded", 4)
        xn_ready = ph.sem("xn_ready")
        xn_turned = ph.sem("xn_turned")
        xhi_ready = ph.sem("xhi_ready")
        xlo_ready = ph.sem("xlo_ready")
        h_done = ph.sem("h_done")
        gelu_done = ph.sem("gelu_done")
        y_done = ph.sem("y_done")
        y_ready = ph.sem("y_ready")
        y_stored = ph.sems("y_stored", 4)
        block = ph.block()

        @block.sync
        def _(sp):
            def load(g, s, r):
                if not isinstance(r, int) or r:
                    wait_alone(K, sp, y_stored[s], r * (16 * G))
                load_tiles(sp, K, K["sorted1"], x[:, s], x_loaded[s], g, G, E1 // 2 * REGION)

            pipeline(sp, N, 4, [(0, load)])

        @block.gpsimd
        def _(pool):
            def scatter(g, s, r):
                wait_alone(K, pool, y_ready, g + 1)
                for j in range(G):
                    pool.indirect_dma_start(
                        out_rows, bass.IndirectOffsetOnAxis(ap=x[:, s, j, NUM:NUM + 1].bitcast(I32), axis=0),
                        y[:, s, j, :], None, bounds_check=ROWS - 1, oob_is_err=False).then_inc(y_stored[s], 16)

            pipeline(pool, N, 4, [(3, scatter)])
            for s in range(4):
                pool.wait_ge(y_stored[s], 16 * G * len(range(s, N, 4)))

        @block.vector
        def _(dve):
            def normalise(g, s, r):
                dve.wait_ge(x_loaded[s], r * (16 * G) + 16 * G)
                freed(dve, xn_turned, g, 2)
                normalise_rows(dve, xn[:, s % 2], x[:, s, :, 0:P], x[:, s, :, MEAN:MEAN + 1],
                               x[:, s, :, RSTD:RSTD + 1], G).then_inc(xn_ready, 1)

            def low_part(g, s, r):
                dve.wait_ge(xhi_ready, g + 1)
                freed(dve, h_done, g, 2, per=NCH, k=NCH)
                dve.tensor_tensor(xlo[:, s % 2], ps_xT[:], xhi[:, s % 2], ALU.subtract).then_inc(xlo_ready, 1)

            def finish(g, s, r):
                dve.wait_ge(y_done, g + 1)
                if not isinstance(r, int) or r:
                    dve.wait_ge(y_stored[s], r * (16 * G))
                for j in range(G):
                    ins = dve.scalar_tensor_tensor(y[:, s, j, :], ps_y[:, j, :], x[:, s, j, PROB:PROB + 1],
                                                   x[:, s, j, 0:P], ALU.mult, ALU.add)
                ins.then_inc(y_ready, 1)

            pipeline(dve, N, 4, [(1, normalise), (3, finish), (1, low_part)])

        @block.scalar
        def _(act):
            def high_part(g, s, r):
                act.wait_ge(xn_turned, g + 1)
                freed(act, h_done, g, 2, per=NCH, k=NCH)
                act.activation(xhi[:, s % 2], ps_xT[:], ACT.Copy).then_inc(xhi_ready, 1)

            def gelu(g, s, r):
                freed(act, y_done, g, 2)
                for c in range(NCH):
                    act.wait_ge(h_done, g * NCH + c + 1)
                    act.activation(h[:, s % 2, c, :], ps_h[:, c, :], ACT.Gelu,
                                   bias=K["b1"][:, c:c + 1]).then_inc(gelu_done, 1)

            pipeline(act, N, 4, [(1, high_part), (2, gelu)])

        @block.tensor
        def _(pe):
            def turn_x(g, s, r):
                pe.wait_ge(xn_ready, g + 1)
                freed(pe, xlo_ready, g, 1)
                for j in range(G):
                    ins = pe.transpose(ps_xT[:, j * P:(j + 1) * P], xn[:, s % 2, j, :], K["ident"][:])
                ins.then_inc(xn_turned, 1)

            def hidden(g, s, r):
                pe.wait_ge(xlo_ready, g + 1)
                hidden_layer(pe, K, ps_h, xhi[:, s % 2], xlo[:, s % 2], gelu_done, h_done, g)

            def mix(g, s, r):
                e = [tile_expert(pe, K, g, j, G, E1) for j in range(G)]
                pe.wait_ge(gelu_done, g * NCH + NCH)
                freed(pe, y_ready, g, 1)
                for j in range(G):
                    pe.matmul(ps_y[:, j, :], K["onesb"][0:3, :], K["biasrows"][:, bass.ds(e[j] * P + BD_AT, P)],
                              start=(j == 0), stop=False, skip_group_check=True)
                    for c in range(NCH):
                        w = K["wd"][:, bass.ds(e[j], 1), c, :].rearrange("p o d -> p (o d)")
                        ins = pe.matmul(ps_y[:, j, :], h[:, s % 2, c, j * P:(j + 1) * P], w,
                                        start=False, stop=(c == NCH - 1), skip_group_check=True)
                ins.then_inc(y_done, 1)

            pipeline(pe, N, 4, [(1, turn_x), (2, hidden), (3, mix)])


def build(nc, T, out):
    with ExitStack() as ctx:
        K = {}
        for name, shape, dt in [
            ("ident", [P, P], F32), ("identb", [P, P], BF16), ("onesf", [P, P], F32), ("onesb", [P, P], BF16),
            ("before", [P, P], BF16), ("upto", [E0, E0], F32), ("count", [P, 256], F32), ("rev0", [P, E0], F32),
            ("sign", [P, E0], F32), ("tile0", [P, E0], F32), ("start", [P, E0], F32), ("number", [P, B], I32), ("minus_half", [P, 4], F32), ("padrow", [P, ROW], F32),
            ("cap", [P, P], F32), ("far", [P, P], BF16), ("linked", [P, 1], F32),
            ("wa", [P, 2], F32), ("wa2", [P, P], F32), ("wh", [P, P], F32), ("rwT", [P, E0], F32),
            ("wqT", [P, P], F32), ("wkT", [P, P], F32), ("wvT", [P, P], F32), ("woT", [P, P], F32),
            ("bqk", [P, 2], F32), ("bv", [P, P], F32), ("bvg", [P, 2 * P], F32), ("b1", [P, NCH], F32),
            ("biasrows", [3, NBIAS], BF16), ("w1e", [P, E0, H0], F32), ("w2e", [H0, E0, P], F32),
            ("w1", [P, HID], F32), ("w1hi", [P, HID], F16), ("w1lo", [P, HID], F16),
            ("wg", [P, NCH, E1], F32), ("wd", [P, E1, NCH, P], F32),
            ("kbd", [P, 2, 2, HEADS, P], F32), ("vaug", [P, 4, 2 * HEADS, HD + 1], F32),
            ("base0", [P, E0], F32), ("base1", [P, E1], F32), ("dest0", [P, B], F32), ("place0", [P, B], I32),
            ("table", [1, 2, NT0], I32),
        ]:
            K[name] = ctx.enter_context(nc.sbuf_tensor(f"k_{name}", shape, dt))
        K["passed"] = ctx.enter_context(nc.semaphore("passed"))
        K["sorted0"] = nc.dram_tensor("sorted0", (E0 // 2 * REGION + P, ROW), F32, kind="Internal").ap()
        K["sorted1"] = nc.dram_tensor("sorted1", (E1 // 2 * REGION + P, ROW), F32, kind="Internal").ap()
        K["mixed0"] = nc.dram_tensor("mixed0", (NT0 * P, P), F32, kind="Internal").ap()
        K["x3"] = nc.dram_tensor("x3", (ROWS, P), F32, kind="Internal").ap()
        setup(nc, K, T)
        gat(nc, K, T)
        table(nc, K, 0)
        expert0(nc, K)
        mha(nc, K)
        gate(nc, K)
        table(nc, K, 1)
        expert1(nc, K, out.rearrange("b n d -> (b n) d"))


_INS = ["x", "adj", "L0_gnn_W", "L0_gnn_a", "L0_ffn_router_w", "L0_ffn_router_b", "L0_ffn_W1", "L0_ffn_b1",
        "L0_ffn_W2", "L0_ffn_b2", "L1_gnn_wq", "L1_gnn_bq", "L1_gnn_wk", "L1_gnn_bk", "L1_gnn_wv", "L1_gnn_bv",
        "L1_gnn_wo", "L1_gnn_bo", "L1_ffn_W1", "L1_ffn_b1", "L1_ffn_Wg", "L1_ffn_bg", "L1_ffn_Wd", "L1_ffn_bd"]


def kernel(**inputs):
    import numpy as _np
    import concourse.bacc as _bacc
    from concourse import mybir as _mybir
    from concourse.bass_utils import run_bass_kernel_spmd as _run

    nc = _bacc.Bacc("TRN2", target_bir_lowering=False, num_devices=1)
    arrays, T = {}, {}
    for name in _INS:
        a = _np.ascontiguousarray(inputs[name])
        arrays[f"in_{name}"] = a
        T[name] = nc.dram_tensor(f"in_{name}", a.shape, _mybir.dt.from_np(a.dtype), kind="ExternalInput").ap()
    out = nc.dram_tensor("out_0", (B, P, P), F32, kind="ExternalOutput").ap()
    build(nc, T, out)
    r = _run(nc, [arrays], core_ids=[0])
    return r.results[0]["out_0"]
```

```python
from contextlib import ExitStack

import concourse.bass as bass
from concourse import mybir

ALU = mybir.AluOpType
ACT = mybir.ActivationFunctionType
AX = mybir.AxisListType
F32 = mybir.dt.float32
F16 = mybir.dt.float16
BF16 = mybir.dt.bfloat16
I32 = mybir.dt.int32

P = 128
B = 128
ROWS = B * P
E0, H0 = 32, 32
E1, HID = 8, 512
NCH = HID // P
HEADS, HD = 4, 32
EPS = 1e-5
REGION = ROWS + 2 * P
NT0 = ROWS // P + E0
NT1 = ROWS // P + E1
ROW = P + 4
MEAN, RSTD, PROB, NUM = P, P + 1, P + 2, P + 3
NO_ROW = 1 << 20
MASKED_E0 = -1e9
SLOPE = 0.01
FAR = -1e30

B1_AT = 0
B2_AT = B1_AT + E0 * H0
BD_AT = B2_AT + E0 * P
RB_AT = BD_AT + E1 * P
BO_AT = RB_AT + E0
BG_AT = BO_AT + P
NBIAS = BG_AT + E1


def pipeline(eng, n, unroll, steps, peel=8):
    last = max(lag for lag, _ in steps)
    assert last <= peel and peel % unroll == 0

    def peeled(t):
        for lag, f in steps:
            if 0 <= t - lag < n:
                f(t - lag, (t - lag) % unroll, (t - lag) // unroll)

    for t in range(peel):
        peeled(t)
    with eng.Fori(peel // unroll, n // unroll) as i:
        for u in range(unroll):
            for lag, f in steps:
                f(i * unroll + (u - lag), (u - lag) % unroll, i + (u - lag) // unroll)
    for t in range(n // unroll * unroll, n + last):
        peeled(t)


def freed(eng, sem, g, depth, per=1, k=1):
    if not isinstance(g, int) or g >= depth:
        eng.wait_ge(sem, (g - depth) * per + k)


def wait_alone(K, eng, sem, value):
    eng.wait_ge(sem, value)
    if not isinstance(value, int):
        eng.sem_inc(K["passed"], 1)


class Phase:

    def __init__(self, nc, name):
        self.nc, self.name, self.ctx, self.used = nc, name, ExitStack(), []

    def __enter__(self):
        return self

    def __exit__(self, *exc):
        self.ctx.__exit__(*exc)
        self.nc.clear_and_free_semaphores(self.used)
        self.nc.all_engine_barrier()

    def sb(self, name, shape, dt):
        return self.ctx.enter_context(self.nc.sbuf_tensor(f"{self.name}_{name}", shape, dt))

    def psum(self, name, shape, dt=F32):
        return self.ctx.enter_context(self.nc.psum_tensor(f"{self.name}_{name}", shape, dt))

    def sem(self, name):
        self.used.append(self.nc.alloc_semaphore(f"{self.name}_{name}"))
        return self.used[-1]

    def sems(self, name, n):
        return [self.sem(f"{name}{i}") for i in range(n)]

    def block(self):
        return self.ctx.enter_context(self.nc.Block())


def setup(nc, K, T):
    with Phase(nc, "setup") as ph:
        wload = ph.sb("wload", [P, 6, P], F32)
        acol = ph.sb("acol", [P, 2], F32)
        wT = ph.sb("wT", [P, P], F32)
        wa = ph.sb("wa", [P, 2], F32)
        adj = ph.sb("adj", [P, P], I32)
        off = ph.sb("off", [P, P], F32)
        biasf = ph.sb("biasf", [P, 64], F32)
        res1 = ph.sb("res1", [P, 64], F32)
        res2 = ph.sb("res2", [P, 64], F32)
        part = [ph.sb(f"part{k}", [P, 64], BF16) for k in range(3)]
        bvrow = ph.sb("bvrow", [P, P], F32)
        pt = ph.psum("pt", [P, 8, 512])

        loads = ph.sem("loads")
        bias_zero = ph.sem("bias_zero")
        ones_set = ph.sem("ones_set")
        pool_step = ph.sem("pool_step")
        transposed = ph.sem("transposed")
        wT_ready = ph.sem("wT_ready")
        wa_ready = ph.sem("wa_ready")
        dve_step = ph.sem("dve_step")
        parts_ready = ph.sem("parts_ready")
        rows_stored = ph.sem("rows_stored")
        fills = ph.sem("fills")
        zero_rows = ph.sem("zero_rows")
        block = ph.block()

        pieces = [
            ("L0_ffn_b1", 0, E0 * H0 // P, P, B1_AT),
            ("L0_ffn_b2", 8, E0, P, B2_AT),
            ("L1_ffn_bd", 40, E1, P, BD_AT),
            ("L0_ffn_router_b", 48, 1, E0, RB_AT),
            ("L1_gnn_bo", 49, 1, P, BO_AT),
            ("L1_ffn_bg", 50, 1, E1, BG_AT),
        ]

        def flat(ap):
            return ap.rearrange("a b -> (a b)") if len(ap.shape) == 2 else ap

        @block.sync
        def _(sp):
            n = 0
            for k, name in enumerate(["L0_gnn_W", "L1_gnn_wq", "L1_gnn_wk", "L1_gnn_wv", "L1_gnn_wo"]):
                sp.dma_start(wload[:, k, :], T[name]).then_inc(loads, 16)
            sp.dma_start(wload[0:E0, 5, :], T["L0_ffn_router_w"]).then_inc(loads, 16)
            sp.dma_start(adj[:], T["adj"]).then_inc(loads, 16)
            with nc.allow_non_contiguous_dma(reason="a few hundred bias values"):
                sp.dma_start(acol[:], T["L0_gnn_a"].rearrange("(t p) o -> p (t o)", p=P)).then_inc(loads, 16)
                sp.dma_start(K["bqk"][:, 0:1], T["L1_gnn_bq"].rearrange("(p o) -> p o", o=1)).then_inc(loads, 16)
                sp.dma_start(K["bqk"][:, 1:2], T["L1_gnn_bk"].rearrange("(p o) -> p o", o=1)).then_inc(loads, 16)
                sp.dma_start(K["b1"][:], T["L1_ffn_b1"].rearrange("(c p) -> p c", p=P)).then_inc(loads, 16)
            sp.dma_start(K["bv"][0:1, :], T["L1_gnn_bv"].rearrange("(o n) -> o n", o=1)).then_inc(loads, 16)
            sp.dma_start(K["wg"][:], T["L1_ffn_Wg"].rearrange("(c p) e -> p c e", p=P)).then_inc(loads, 16)
            sp.dma_start(K["w1"][:], T["L1_ffn_W1"]).then_inc(loads, 16)
            sp.wait_ge(bias_zero, 1)
            with nc.allow_non_contiguous_dma(reason="a few hundred bias values"):
                for name, at, cols, parts, _ in pieces:
                    sp.dma_start(biasf[0:parts, at:at + cols],
                                 flat(T[name]).rearrange("(p c) -> p c", c=cols)).then_inc(loads, 16)
            sp.wait_ge(parts_ready, 3)
            with nc.allow_non_contiguous_dma(reason="a few hundred bias values"):
                for k in range(3):
                    for name, at, cols, parts, to in pieces:
                        sp.dma_start(K["biasrows"][k:k + 1, to:to + parts * cols],
                                     part[k][0:parts, at:at + cols]).then_inc(rows_stored, 16)
                        n += 16
            sp.wait_ge(rows_stored, n)
            sp.wait_ge(fills, 16 * (3 + 2))

        NLOADS = 14 + len(pieces)

        @block.scalar
        def _(act):
            act.dma_start(K["w1e"][:], T["L0_ffn_W1"].rearrange("e d h -> d e h")).then_inc(fills, 16)
            act.dma_start(K["w2e"][:], T["L0_ffn_W2"].rearrange("e h d -> h e d")).then_inc(fills, 16)
            act.dma_start(K["wd"][:].rearrange("p e c d -> p (e c) d"),
                          T["L1_ffn_Wd"].rearrange("e (c p) d -> p (e c) d", p=P)).then_inc(fills, 16)
            act.wait_ge(zero_rows, 2)
            for dst, experts in ((K["sorted0"], E0), (K["sorted1"], E1)):
                act.dma_start(dst[experts // 2 * REGION:, :], K["padrow"][:]).then_inc(fills, 16)

        @block.gpsimd
        def _(pool):
            pool.memset(K["padrow"][:], 0.0).then_inc(pool_step, 1)
            pool.memset(K["onesf"][:], 1.0).then_inc(pool_step, 1)
            pool.memset(K["onesb"][:], 1.0).then_inc(pool_step, 1)
            pool.memset(K["ident"][:], 0.0).then_inc(pool_step, 1)
            pool.wait_ge(pool_step, 4)
            pool.memset(K["padrow"][:, NUM:NUM + 1].bitcast(I32), NO_ROW).then_inc(zero_rows, 1)
            pool.affine_select(out=K["ident"][:], in_=K["ident"][:], compare_op=ALU.not_equal, fill=1.0, base=0,
                               pattern=[[-1, P]], channel_multiplier=1).then_inc(pool_step, 1)
            pool.affine_select(out=K["before"][:], in_=K["onesb"][:], compare_op=ALU.is_gt, fill=0.0, base=0,
                               pattern=[[1, P]], channel_multiplier=-1).then_inc(pool_step, 1)
            pool.affine_select(out=K["upto"][:], in_=K["onesf"][0:E0, 0:E0], compare_op=ALU.is_ge, fill=0.0,
                               base=0, pattern=[[1, E0]], channel_multiplier=-1).then_inc(pool_step, 1)
            pool.iota(K["count"][:], [[1, 256]], base=0, channel_multiplier=0,
                      allow_small_or_imprecise_dtypes=True).then_inc(pool_step, 1)
            pool.iota(K["rev0"][:], [[-1, E0]], base=E0, channel_multiplier=0,
                      allow_small_or_imprecise_dtypes=True).then_inc(pool_step, 1)
            pool.iota(K["number"][:], [[P, B]], base=0, channel_multiplier=1,
                      allow_small_or_imprecise_dtypes=True).then_inc(pool_step, 1)
            pool.memset(K["minus_half"][:], -0.5).then_inc(zero_rows, 1)
            pool.wait_ge(loads, 16 * NLOADS)
            pool.partition_broadcast(bvrow[:], K["bv"][0:1, :]).then_inc(pool_step, 1)

        @block.tensor
        def _(pe):
            pe.wait_ge(loads, 16 * NLOADS)
            pe.wait_ge(pool_step, 5)
            for k in range(5):
                pe.transpose(pt[:, k, 0:P], wload[:, k, :], K["ident"][:])
            pe.transpose(pt[:, 5, 0:E0], wload[0:E0, 5, :], K["ident"][0:E0, 0:E0]).then_inc(transposed, 1)
            pe.wait_ge(wT_ready, 1)
            pe.matmul(pt[:, 6, 0:2], wT[:], acol[:], start=True, stop=True).then_inc(wa_ready, 1)

        @block.vector
        def _(dve):
            steps = [0]

            def then(ins):
                steps[0] += 1
                ins.then_inc(dve_step, 1)
                dve.wait_ge(dve_step, steps[0])

            dve.memset(biasf[:], 0.0).then_inc(bias_zero, 1)
            dve.wait_ge(loads, 16 * NLOADS)
            dve.wait_ge(pool_step, 11)
            for j in range(2):
                dve.tensor_copy(K["bvg"][:, j * P:(j + 1) * P], bvrow[:])
            then(dve.tensor_scalar(off[:], adj[:], 0.0, None, ALU.is_equal))
            then(dve.tensor_scalar(K["cap"][:], off[:], -1.0, -3e38, ALU.add, ALU.mult))
            dve.scalar_tensor_tensor(K["cap"][:], off[:], MASKED_E0 / SLOPE, K["cap"][:], ALU.mult, ALU.add)
            dve.tensor_scalar(K["far"][:], off[:], FAR, None, ALU.mult)
            then(dve.tensor_reduce(K["linked"][:], off[:], AX.X, ALU.min))
            then(dve.tensor_scalar(K["linked"][:], K["linked"][:], -1.0, 1.0, ALU.mult, ALU.add))
            dve.tensor_copy(K["identb"][:], K["ident"][:])
            then(dve.tensor_copy(part[0][:], biasf[:]))
            then(dve.tensor_tensor(res1[:], biasf[:], part[0][:], ALU.subtract))
            then(dve.tensor_copy(part[1][:], res1[:]))
            then(dve.tensor_tensor(res2[:], res1[:], part[1][:], ALU.subtract))
            then(dve.tensor_copy(part[2][:], res2[:]))
            dve.tensor_copy(K["w1hi"][:], K["w1"][:]).then_inc(parts_ready, 3)
            then(dve.memset(K["kbd"][:], 0.0))
            dve.memset(K["vaug"][:], 1.0)
            then(dve.tensor_tensor(K["w1lo"][:], K["w1"][:], K["w1hi"][:], ALU.subtract))
            pair = K["count"][:, 0:E0 // 2]
            dve.memset(K["sign"][:, 0::2], 1.0)
            dve.memset(K["sign"][:, 1::2], -1.0)
            dve.tensor_scalar(K["tile0"][:, 0::2], pair, float(REGION // P), None, ALU.mult)
            dve.tensor_scalar(K["tile0"][:, 1::2], pair, float(REGION // P), float(REGION // P - 1), ALU.mult, ALU.add)
            dve.tensor_scalar(K["start"][:, 0::2], pair, float(REGION), None, ALU.mult)
            then(dve.tensor_scalar(K["start"][:, 1::2], pair, -float(REGION), float(1 - REGION), ALU.mult, ALU.add))
            dve.tensor_copy(K["base0"][:], K["start"][:])
            then(dve.tensor_copy(K["base1"][:], K["start"][:, 0:E1]))
            dve.wait_ge(transposed, 1)
            dve.tensor_copy(wT[:], pt[:, 0, 0:P]).then_inc(wT_ready, 1)
            for k, name in ((1, "wqT"), (2, "wkT"), (3, "wvT"), (4, "woT")):
                dve.tensor_copy(K[name][:], pt[:, k, 0:P])
            dve.tensor_copy(K["rwT"][:], pt[:, 5, 0:E0])
            dve.tensor_copy(K["wh"][:], wload[:, 0, :])
            dve.wait_ge(wa_ready, 1)
            then(dve.tensor_copy(K["wa"][:], pt[:, 6, 0:2]))
            dve.tensor_scalar(K["wa2"][:], K["onesf"][:], K["wa"][:, 1:2], None, ALU.mult)


class Router:

    def __init__(self, ph, K, dve_sems, groups, experts, base, ps_logit, ps_rank, onehot):
        self.base, self.ps_logit, self.ps_rank, self.onehot = base, ps_logit, ps_rank, onehot
        self.logit_ready, self.rank_ready, self.onehot_ready = dve_sems
        self.shape = [P, groups, experts]
        self.G = groups
        self.rev = K["rev0"][:, E0 - experts:E0]
        self.top_of = ph.sb("top", [P, 2, groups], F32)
        self.eq_of = ph.sb("eq", self.shape, F32)
        self.key_of = ph.sb("key", self.shape, F32)
        self.first_of = ph.sb("first", [P, groups], F32)
        self.place_of = ph.sb("place", self.shape, F32)
        self.own_of = ph.sb("own", self.shape, F32)
        self.dest_of = ph.sb("dest", [P, groups], F32)
        self.top_ready = ph.sem("top_ready")
        self.eq_ready = ph.sem("eq_ready")
        self.key_ready = ph.sem("key_ready")
        self.first_ready = ph.sem("first_ready")
        self.place_ready = ph.sem("place_ready")
        self.own_ready = ph.sem("own_ready")
        self.dest_ready = ph.sem("dest_ready")

    def top(self, dve, g, s):
        dve.wait_ge(self.logit_ready, g + 1)
        dve.tensor_reduce(self.top_of[:, s % 2], self.ps_logit, AX.X, ALU.max).then_inc(self.top_ready, 1)

    def equal(self, dve, g, s):
        dve.wait_ge(self.top_ready, g + 1)
        dve.tensor_tensor(self.eq_of[:], self.ps_logit, self.top_of[:, s % 2].unsqueeze(2).to_broadcast(self.shape),
                          ALU.is_ge).then_inc(self.eq_ready, 1)

    def key(self, dve, g, s):
        dve.wait_ge(self.eq_ready, g + 1)
        dve.tensor_tensor(self.key_of[:], self.eq_of[:], self.rev.unsqueeze(1).to_broadcast(self.shape),
                          ALU.mult).then_inc(self.key_ready, 1)

    def first(self, dve, g, s):
        dve.wait_ge(self.key_ready, g + 1)
        dve.tensor_reduce(self.first_of[:], self.key_of[:], AX.X, ALU.max).then_inc(self.first_ready, 1)

    def choose(self, dve, g, s):
        dve.wait_ge(self.first_ready, g + 1)
        dve.tensor_tensor(self.onehot[:, s % 2], self.key_of[:],
                          self.first_of[:].unsqueeze(2).to_broadcast(self.shape),
                          ALU.is_equal).then_inc(self.onehot_ready, 1)

    def place(self, dve, g, s):
        dve.wait_ge(self.rank_ready, g + 1)
        freed(dve, self.own_ready, g, 1)
        dve.tensor_tensor(self.place_of[:], self.ps_rank[:, 0:self.G, :],
                          self.base.unsqueeze(1).to_broadcast(self.shape), ALU.add).then_inc(self.place_ready, 1)

    def own(self, dve, g, s):
        dve.wait_ge(self.place_ready, g + 1)
        dve.tensor_tensor(self.own_of[:], self.place_of[:], self.onehot[:, s % 2], ALU.mult)
        dve.tensor_tensor(self.base, self.base, self.ps_rank[:, self.G, :], ALU.add).then_inc(self.own_ready, 1)

    def dest(self, dve, g, s):
        dve.wait_ge(self.own_ready, g + 1)
        dve.tensor_reduce(self.dest_of[:], self.own_of[:], AX.X, ALU.add).then_inc(self.dest_ready, 1)

    def index(self, dve, g, s, idx):
        return dve.scalar_tensor_tensor(idx, self.dest_of[:], -1.0, self.dest_of[:], ALU.mult, ALU.max)


def normalise_rows(dve, out, x, mean, rstd, groups):
    for j in range(groups):
        ins = dve.tensor_scalar(out[:, j, :], x[:, j, :], mean[:, j, :], rstd[:, j, :], ALU.subtract, ALU.mult)
    return ins


def gat(nc, K, T):
    G, N, U = 4, B // 4, 8
    x_in = T["x"].rearrange("(g j) n d -> g n j d", j=G)
    with Phase(nc, "gat") as ph:
        x = ph.sb("x", [P, U, G, P], F32)
        bn = ph.sb("bn", [P, 2, G, 6], F32)
        mv = ph.sb("mv", [P, 4, G, 2], F32)
        shift = ph.sb("shift", [P, 4, G], F32)
        xn = ph.sb("xn", [P, 2, G, P], F32)
        xT = ph.sb("xT", [P, 2, G, P], F32)
        h = ph.sb("h", [P, 4, G, P], F32)
        es = ph.sb("es", [P, 2, G], F32)
        ev = ph.sb("ev", [P, 2, G, P], F32)
        el = ph.sb("el", [P, 2, G, P], F32)
        nmax = ph.sb("nmax", [P, 2, G], F32)
        pr = ph.sb("pr", [P, 2, G, P], F32)
        prsum = ph.sb("prsum", [P, 4, G], F32)
        rsum = ph.sb("rsum", [P, 4, G], F32)
        prT = ph.sb("prT", [P, 2, G, P], F32)
        hp = ph.sb("hp", [P, 2, G, P], F32)
        row = ph.sb("row", [P, U, G, ROW], F32)
        bn2 = ph.sb("bn2", [P, 2, G, 6], F32)
        shift2 = ph.sb("shift2", [P, 4, G], F32)
        xn2 = ph.sb("xn2", [P, 2, G, P], F32)
        xT2 = ph.sb("xT2", [P, 2, G, P], F32)
        onehot = ph.sb("onehot", [P, 2, G, E0], BF16)
        idx = ph.sb("idx", [P, U, G], I32)

        ps_xT = ph.psum("ps_xT", [P, G, P])
        ps_ed = ph.psum("ps_ed", [P, G, P])
        ps_h = ph.psum("ps_h", [P, G, P])
        ps_es = ph.psum("ps_es", [P, 512])
        ps_prT = ph.psum("ps_prT", [P, G, P])
        ps_hp = ph.psum("ps_hp", [P, G, P])
        ps_xT2 = ph.psum("ps_xT2", [P, G, P])
        ps_r = ph.psum("ps_r", [P, 512])
        ps_logit = ps_r[:, 0:G * E0].rearrange("p (j e) -> p j e", j=G)
        ps_rank = ps_r[:, 256:256 + (G + 1) * E0].rearrange("p (j e) -> p j e", j=G + 1)

        x_loaded = ph.sems("x_loaded", U)
        stats_ready = ph.sem("stats_ready")
        var_ready = ph.sem("var_ready")
        veps_ready = ph.sem("veps_ready")
        rstd_ready = ph.sem("rstd_ready")
        shift_ready = ph.sem("shift_ready")
        xn_ready = ph.sem("xn_ready")
        xn_turned = ph.sem("xn_turned")
        xT_ready = ph.sem("xT_ready")
        projected = ph.sem("projected")
        es_ready = ph.sem("es_ready")
        h_ready = ph.sem("h_ready")
        edges_ready = ph.sem("edges_ready")
        leaky_ready = ph.sem("leaky_ready")
        max_ready = ph.sem("max_ready")
        pr_ready = ph.sem("pr_ready")
        pr_turned = ph.sem("pr_turned")
        prT_ready = ph.sem("prT_ready")
        attended = ph.sem("attended")
        hp_ready = ph.sem("hp_ready")
        rsum_ready = ph.sem("rsum_ready")
        x1_ready = ph.sem("x1_ready")
        stats2_ready = ph.sem("stats2_ready")
        var2_ready = ph.sem("var2_ready")
        veps2_ready = ph.sem("veps2_ready")
        rstd2_ready = ph.sem("rstd2_ready")
        shift2_ready = ph.sem("shift2_ready")
        xn2_ready = ph.sem("xn2_ready")
        xn2_turned = ph.sem("xn2_turned")
        xT2_ready = ph.sem("xT2_ready")
        logit_ready = ph.sem("logit_ready")
        onehot_ready = ph.sem("onehot_ready")
        rank_ready = ph.sem("rank_ready")
        idx_ready = ph.sem("idx_ready")
        rows_stored = ph.sems("rows_stored", U)
        slots_free = ph.sem("slots_free")
        router = Router(ph, K, (logit_ready, rank_ready, onehot_ready), G, E0, K["base0"][:], ps_logit, ps_rank,
                        onehot)
        block = ph.block()

        @block.sync
        def _(sp):
            def load(g, s, r):
                freed(sp, x1_ready, g, U)
                src = x_in[g] if isinstance(g, int) else x_in[bass.ds(g, 1)].rearrange("o n j d -> (o n) j d")
                sp.dma_start(x[:, s], src).then_inc(x_loaded[s], 16)

            pipeline(sp, N, U, [(0, load)])

        @block.gpsimd
        def _(pool):
            pool.sem_inc(slots_free, U)

            def rstd(g, s, r):
                pool.wait_ge(veps_ready, g + 1)
                pool.tensor_tensor(mv[:, s % 4, :, 1], mv[:, s % 4, :, 1], K["minus_half"][:, 0:G],
                                   ALU.pow).then_inc(rstd_ready, 1)

            def rstd2(g, s, r):
                pool.wait_ge(veps2_ready, g + 1)
                pool.tensor_tensor(row[:, s, :, RSTD], row[:, s, :, RSTD], K["minus_half"][:, 0:G],
                                   ALU.pow).then_inc(rstd2_ready, 1)

            def scatter(g, s, r):
                wait_alone(K, pool, idx_ready, g + 1)
                for j in range(G):
                    pool.indirect_dma_start(
                        K["sorted0"], bass.IndirectOffsetOnAxis(ap=idx[:, s, j:j + 1], axis=0),
                        row[:, s, j, :], None).then_inc(rows_stored[s], 16)

            def release(g, s, r):
                pool.wait_ge(rows_stored[s], r * (16 * G) + 16 * G)
                pool.sem_inc(slots_free, 1)

            pipeline(pool, N, U, [(0, rstd), (6, scatter), (3, rstd2), (7, release)])

        @block.vector
        def _(dve):
            dve.memset(row[:, :, :, PROB:NUM + 1], 0.0)

            def stats(g, s, r):
                dve.wait_ge(x_loaded[s], r * 16 + 16)
                for j in range(G):
                    ins = dve.bn_stats(bn[:, s % 2, j, :], x[:, s, j, :])
                ins.then_inc(stats_ready, 1)

            def aggregate(g, s, r):
                if not isinstance(g, int) or g >= 4:
                    wait_alone(K, dve, xn_ready, g - 3)
                wait_alone(K, dve, stats_ready, g + 1)
                for j in range(G):
                    ins = dve.bn_aggr(mv[:, s % 4, j, :], bn[:, s % 2, j, :])
                ins.then_inc(var_ready, 1)

            def add_eps(g, s, r):
                dve.wait_ge(var_ready, g + 1)
                dve.tensor_scalar(mv[:, s % 4, :, 1], mv[:, s % 4, :, 1], EPS, None, ALU.add).then_inc(veps_ready, 1)

            def shifts(g, s, r):
                dve.wait_ge(rstd_ready, g + 1)
                dve.scalar_tensor_tensor(shift[:, s % 4], mv[:, s % 4, :, 0], -1.0, mv[:, s % 4, :, 1], ALU.mult,
                                         ALU.mult).then_inc(shift_ready, 1)

            def edges(g, s, r):
                dve.wait_ge(es_ready, g + 1)
                for j in range(G):
                    ins = dve.scalar_tensor_tensor(ev[:, s % 2, j, :], ps_ed[:, j, :], es[:, s % 2, j:j + 1],
                                                   K["cap"][:], ALU.add, ALU.min)
                ins.then_inc(edges_ready, 1)

            def leaky(g, s, r):
                dve.wait_ge(edges_ready, g + 1)
                freed(dve, pr_ready, g, 2)
                dve.scalar_tensor_tensor(el[:, s % 2], ev[:, s % 2], SLOPE, ev[:, s % 2], ALU.mult,
                                         ALU.max).then_inc(leaky_ready, 1)

            def row_max(g, s, r):
                dve.wait_ge(leaky_ready, g + 1)
                dve.tensor_reduce(nmax[:, s % 2], el[:, s % 2], AX.X, ALU.max, negate=True).then_inc(max_ready, 1)

            def inverse(g, s, r):
                dve.wait_ge(pr_ready, g + 1)
                dve.reciprocal(rsum[:, s % 4], prsum[:, s % 4]).then_inc(rsum_ready, 1)

            def residual(g, s, r):
                dve.wait_ge(slots_free, g + 1)
                dve.wait_ge(hp_ready, g + 1)
                dve.tensor_tensor(row[:, s, :, 0:P], x[:, s], hp[:, s % 2], ALU.add).then_inc(x1_ready, 1)

            def stats2(g, s, r):
                dve.wait_ge(x1_ready, g + 1)
                for j in range(G):
                    ins = dve.bn_stats(bn2[:, s % 2, j, :], row[:, s, j, 0:P])
                ins.then_inc(stats2_ready, 1)

            def aggregate2(g, s, r):
                wait_alone(K, dve, stats2_ready, g + 1)
                for j in range(G):
                    ins = dve.bn_aggr(row[:, s, j, MEAN:RSTD + 1], bn2[:, s % 2, j, :])
                ins.then_inc(var2_ready, 1)

            def add_eps2(g, s, r):
                dve.wait_ge(var2_ready, g + 1)
                dve.tensor_scalar(row[:, s, :, RSTD], row[:, s, :, RSTD], EPS, None, ALU.add).then_inc(veps2_ready, 1)

            def shifts2(g, s, r):
                dve.wait_ge(rstd2_ready, g + 1)
                dve.scalar_tensor_tensor(shift2[:, s % 4], row[:, s, :, MEAN], -1.0, row[:, s, :, RSTD], ALU.mult,
                                         ALU.mult).then_inc(shift2_ready, 1)

            def index(g, s, r):
                dve.wait_ge(router.dest_ready, g + 1)
                first = g * G
                dve.tensor_scalar(K["dest0"][:, first:first + G] if isinstance(g, int) else
                                  K["dest0"][:, bass.ds(first, G)], router.dest_of[:], 0.0, None, ALU.add)
                router.index(dve, g, s, idx[:, s]).then_inc(idx_ready, 1)

            def of(step):
                return lambda g, s, r: step(dve, g, s)

            pipeline(dve, N, U, [
                (0, stats), (2, inverse), (4, shifts2), (0, aggregate), (3, stats2), (0, add_eps), (5, of(router.top)), (6, index),
                (0, shifts), (3, aggregate2), (5, of(router.equal)), (3, add_eps2), (5, of(router.key)), (5, of(router.first)),
                (5, of(router.choose)), (1, edges), (5, of(router.place)), (1, leaky), (1, row_max), (2, residual),
                (5, of(router.own)), (5, of(router.dest))])

        @block.scalar
        def _(act):
            def normalise(g, s, r):
                act.wait_ge(shift_ready, g + 1)
                freed(act, xn_turned, g, 2)
                for j in range(G):
                    ins = act.activation(xn[:, s % 2, j, :], x[:, s, j, :], ACT.Identity,
                                         bias=shift[:, s % 4, j:j + 1], scale=mv[:, s % 4, j, 1:2])
                ins.then_inc(xn_ready, 1)

            def copy_xT(g, s, r):
                act.wait_ge(xn_turned, g + 1)
                freed(act, projected, g, 2)
                act.activation(xT[:, s % 2], ps_xT[:], ACT.Copy).then_inc(xT_ready, 1)

            def copy_h(g, s, r):
                act.wait_ge(projected, g + 1)
                freed(act, edges_ready, g, 2)
                act.activation(es[:, s % 2], ps_es[:, 0:G], ACT.Copy).then_inc(es_ready, 1)
                freed(act, attended, g, 4)
                act.activation(h[:, s % 4], ps_h[:], ACT.Copy).then_inc(h_ready, 1)

            def exps(g, s, r):
                act.wait_ge(max_ready, g + 1)
                freed(act, pr_turned, g, 2)
                for j in range(G):
                    ins = act.activation(pr[:, s % 2, j, :], el[:, s % 2, j, :], ACT.Exp,
                                         bias=nmax[:, s % 2, j:j + 1], accum_out=prsum[:, s % 4, j:j + 1])
                ins.then_inc(pr_ready, 1)

            def copy_prT(g, s, r):
                act.wait_ge(pr_turned, g + 1)
                freed(act, attended, g, 2)
                act.activation(prT[:, s % 2], ps_prT[:], ACT.Copy).then_inc(prT_ready, 1)

            def relu(g, s, r):
                act.wait_ge(attended, g + 1)
                act.wait_ge(rsum_ready, g + 1)
                freed(act, x1_ready, g, 2)
                for j in range(G):
                    ins = act.activation(hp[:, s % 2, j, :], ps_hp[:, j, :], ACT.Relu,
                                         scale=rsum[:, s % 4, j:j + 1])
                ins.then_inc(hp_ready, 1)

            def normalise2(g, s, r):
                act.wait_ge(shift2_ready, g + 1)
                freed(act, xn2_turned, g, 2)
                for j in range(G):
                    ins = act.activation(xn2[:, s % 2, j, :], row[:, s, j, 0:P], ACT.Identity,
                                         bias=shift2[:, s % 4, j:j + 1], scale=row[:, s, j, RSTD:RSTD + 1])
                ins.then_inc(xn2_ready, 1)

            def copy_xT2(g, s, r):
                act.wait_ge(xn2_turned, g + 1)
                freed(act, logit_ready, g, 2)
                act.activation(xT2[:, s % 2], ps_xT2[:], ACT.Copy).then_inc(xT2_ready, 1)

            pipeline(act, N, U, [(5, copy_xT2), (1, copy_xT), (2, copy_prT), (4, normalise2), (1, copy_h), (2, relu),
                                 (0, normalise), (1, exps)])

        @block.tensor
        def _(pe):
            def turn_x(g, s, r):
                pe.wait_ge(xn_ready, g + 1)
                freed(pe, xT_ready, g, 1)
                for j in range(G):
                    ins = pe.transpose(ps_xT[:, j, :], xn[:, s % 2, j, :], K["ident"][:])
                ins.then_inc(xn_turned, 1)

            def project(g, s, r):
                pe.wait_ge(xT_ready, g + 1)
                freed(pe, edges_ready, g, 1)
                freed(pe, h_ready, g, 1)
                pe.matmul(ps_ed[:].rearrange("p j n -> p (j n)"), K["wa2"][:],
                          xT[:, s % 2].rearrange("p j n -> p (j n)"), start=True, stop=True)
                for j in range(G):
                    pe.matmul(ps_es[:, j:j + 1], xT[:, s % 2, j, :], K["wa"][:, 0:1], start=True, stop=True)
                for j in range(G):
                    ins = pe.matmul(ps_h[:, j, :], xT[:, s % 2, j, :], K["wh"][:], start=True, stop=True)
                ins.then_inc(projected, 1)

            def turn_pr(g, s, r):
                pe.wait_ge(pr_ready, g + 1)
                freed(pe, prT_ready, g, 1)
                for j in range(G):
                    ins = pe.transpose(ps_prT[:, j, :], pr[:, s % 2, j, :], K["ident"][:])
                ins.then_inc(pr_turned, 1)

            def attend(g, s, r):
                pe.wait_ge(prT_ready, g + 1)
                pe.wait_ge(h_ready, g + 1)
                freed(pe, hp_ready, g, 1)
                for j in range(G):
                    ins = pe.matmul(ps_hp[:, j, :], prT[:, s % 2, j, :], h[:, s % 4, j, :], start=True, stop=True)
                ins.then_inc(attended, 1)

            def turn_x2(g, s, r):
                pe.wait_ge(xn2_ready, g + 1)
                freed(pe, xT2_ready, g, 1)
                for j in range(G):
                    ins = pe.transpose(ps_xT2[:, j, :], xn2[:, s % 2, j, :], K["ident"][:])
                ins.then_inc(xn2_turned, 1)

            def route(g, s, r):
                pe.wait_ge(xT2_ready, g + 1)
                freed(pe, router.own_ready, g, 1)
                pe.matmul(ps_logit, K["onesb"][0:3, :],
                          K["biasrows"][:, RB_AT:RB_AT + E0].unsqueeze(1).to_broadcast([3, G, E0]),
                          start=True, stop=False, skip_group_check=True)
                for j in range(G):
                    ins = pe.matmul(ps_logit[:, j, :], xT2[:, s % 2, j, :], K["rwT"][:], start=False, stop=True,
                                    skip_group_check=True)
                ins.then_inc(logit_ready, 1)

            def rank(g, s, r):
                pe.wait_ge(onehot_ready, g + 1)
                rank_rows(pe, K, ps_rank, onehot[:, s % 2], G).then_inc(rank_ready, 1)

            pipeline(pe, N, U, [(2, turn_pr), (5, route), (1, project), (2, attend), (4, turn_x2), (5, rank),
                                (0, turn_x)])


def rank_rows(pe, K, ps_rank, onehot, groups):
    for j in range(groups):
        for k in range(j):
            pe.matmul(ps_rank[:, j, :], K["onesb"][:], onehot[:, k, :], start=(k == 0), stop=False,
                      skip_group_check=True)
        pe.matmul(ps_rank[:, j, :], K["before"][:], onehot[:, j, :], start=(j == 0), stop=True,
                  skip_group_check=True)
    for k in range(groups):
        ins = pe.matmul(ps_rank[:, groups, :], K["onesb"][:], onehot[:, k, :], start=(k == 0),
                        stop=(k == groups - 1), skip_group_check=True)
    return ins


def table(nc, K, layer):
    E, NT = ((E0, NT0), (E1, NT1))[layer]
    base, rows = K[f"base{layer}"], K[f"sorted{layer}"]
    with Phase(nc, f"table{layer}") as ph:
        ends = ph.sb("ends", [1, E], I32)
        rowsof = ph.sb("rowsof", [P, E], F32)
        full = ph.sb("full", [P, E], I32)
        shifted = ph.sb("shifted", [P, E], I32)
        tilesof = ph.sb("tilesof", [P, E], F32)
        cols = ph.sb("cols", [E, 3], F32)
        upto = ph.sb("upto", [E, 1], F32)
        before = ph.sb("before", [E, 1], F32)
        signed = ph.sb("signed", [E, 1], F32)
        origin = ph.sb("origin", [E, 1], F32)
        passed = ph.sb("passed", [E, NT], F32)
        reached = ph.sb("reached", [E, NT], F32)
        within = ph.sb("within", [E, NT], F32)
        surplus = ph.sb("surplus", [1, NT], F32)
        along = ph.sb("along", [1, NT], F32)
        first = ph.sb("first", [1, NT], F32)
        jump = ph.sb("jump", [P, E], F32)
        tiles_all = ph.sb("tiles_all", [P, 1], F32)
        lift = ph.sb("lift", [P, 1], F32)
        move = ph.sb("move", [P, 2, B], F32)
        placed = ph.sb("placed", [P, B], F32)
        flip = ph.sb("flip", [P, B], I32)
        unflipped = ph.sb("unflipped", [P, B], I32)
        pt = ph.psum("pt", [P, 512])
        pc = ph.psum("pc", [P, 512])
        pr = ph.psum("pr", [P, 512])
        ends_ready = ph.sem("ends_ready")
        tilesof_ready = ph.sem("tilesof_ready")
        turned = ph.sem("turned")
        cols_ready = ph.sem("cols_ready")
        summed = ph.sem("summed")
        passed_ready = ph.sem("passed_ready")
        listed = ph.sem("listed")
        dve_step = ph.sem("dve_step")
        pads_sp = ph.sem("pads_sp")
        pads_act = ph.sem("pads_act")
        block = ph.block()

        def pads(eng, half, sem):
            eng.wait_ge(ends_ready, 1)
            with eng.Fori(0, E // 2) as i:
                end = eng.value_load(ends[0:1, bass.ds(i * 2 + half, 1)], min_val=0, max_val=E // 2 * REGION - P)
                eng.dma_start(rows[bass.ds(end, P), :], K["padrow"][:]).then_inc(sem, 16)
            eng.wait_ge(sem, 16 * (E // 2))

        @block.sync
        def _(sp):
            pads(sp, 0, pads_sp)

        @block.scalar
        def _(act):
            pads(act, 1, pads_act)

        @block.tensor
        def _(pe):
            pe.wait_ge(tilesof_ready, 1)
            for k, rowform in enumerate((tilesof[:], K["sign"][:, 0:E], K["tile0"][:, 0:E])):
                ins = pe.transpose(pt[0:E, k * P:(k + 1) * P], rowform, K["ident"][:])
            ins.then_inc(turned, 1)
            pe.wait_ge(cols_ready, 1)
            pe.matmul(pc[0:E, 0:1], K["upto"][0:E, 0:E], cols[:, 0:1], start=True, stop=True).then_inc(summed, 1)
            pe.wait_ge(passed_ready, 1)
            pe.matmul(pt[0:1, 0:NT], K["onesf"][0:E, 0:1], passed[:], start=True, stop=True)
            pe.matmul(pc[0:1, 0:NT], origin[:], within[:], start=True, stop=True)
            pe.matmul(pr[0:1, 0:NT], cols[:, 1:2], within[:], start=True, stop=True).then_inc(listed, 1)

        @block.vector
        def _(dve):
            steps = [0]

            def then(ins):
                steps[0] += 1
                ins.then_inc(dve_step, 1)
                dve.wait_ge(dve_step, steps[0])

            dve.tensor_scalar(ends[:, 0::2], base[0:1, 0::2], 0.0, None, ALU.add)
            dve.tensor_scalar(ends[:, 1::2], base[0:1, 1::2], -1.0, float(1 - P), ALU.mult,
                              ALU.add).then_inc(ends_ready, 1)
            then(dve.tensor_tensor(rowsof[:], base[:], K["start"][:, 0:E], ALU.subtract))
            then(dve.tensor_scalar(full[:], rowsof[:], float(P - 1), None, ALU.add))
            then(dve.tensor_scalar(shifted[:], full[:], 7, None, ALU.logical_shift_right))
            dve.tensor_copy(tilesof[:], shifted[:]).then_inc(tilesof_ready, 1)
            dve.wait_ge(turned, 1)
            dve.tensor_copy(cols[:], pt[0:E, 0:3 * P].rearrange("e (k p) -> e k p", k=3)[:, :, 0]).then_inc(cols_ready, 1)
            dve.wait_ge(summed, 1)
            then(dve.tensor_copy(upto[:], pc[0:E, 0:1]))
            dve.tensor_tensor(before[:], upto[:], cols[:, 0:1], ALU.subtract)
            then(dve.tensor_scalar(passed[:], K["count"][0:E, 0:NT], upto[:], None, ALU.is_ge))
            dve.tensor_tensor(signed[:], before[:], cols[:, 1:2], ALU.mult)
            then(dve.tensor_scalar(reached[:], K["count"][0:E, 0:NT], before[:], None, ALU.is_ge))
            dve.tensor_tensor(origin[:], cols[:, 2:3], signed[:], ALU.subtract)
            dve.tensor_tensor(within[:], reached[:], passed[:], ALU.subtract).then_inc(passed_ready, 1)
            dve.wait_ge(listed, 1)
            dve.tensor_scalar(K["table"][0:1, 0, 0:NT], pt[0:1, 0:NT], float(E - 1), None, ALU.min)
            dve.tensor_scalar(surplus[:], pt[0:1, 0:NT], float(E), float(E // 2 * REGION // P), ALU.is_ge, ALU.mult)
            then(dve.tensor_tensor(along[:], pr[0:1, 0:NT], K["count"][0:1, 0:NT], ALU.mult))
            then(dve.tensor_tensor(first[:], pc[0:1, 0:NT], along[:], ALU.add))
            then(dve.tensor_tensor(along[:], first[:], surplus[:], ALU.add))
            then(dve.tensor_scalar(K["table"][0:1, 1, 0:NT], along[:], float(P), None, ALU.mult))
            if layer == 0:
                dve.memset(jump[:], 0.0)
                then(dve.tensor_reduce(tiles_all[:], tilesof[:, 0:E - 1], AX.X, ALU.add))
                then(dve.tensor_tensor(jump[:, 1:E - 1:2], tilesof[:, 1:E - 1:2], tilesof[:, 2:E:2], ALU.add))
                dve.tensor_copy(jump[:, 0:1], tilesof[:, 0:1])
                then(dve.tensor_tensor(jump[:, 2:E:2], tilesof[:, 0:E - 2:2], tilesof[:, 1:E - 1:2], ALU.add))
                dve.tensor_scalar(lift[:], tiles_all[:], float(P), float(E // 2 * REGION - 1), ALU.mult, ALU.add)
                dve.tensor_scalar(jump[:, 1:E - 1:2], jump[:, 1:E - 1:2], -float(P), -float(REGION), ALU.mult, ALU.add)
                dve.tensor_scalar(jump[:, 0:1], jump[:, 0:1], -float(P), float(1 - REGION), ALU.mult, ALU.add)
                then(dve.tensor_scalar(jump[:, 2:E:2], jump[:, 2:E:2], float(P), -float(REGION), ALU.mult, ALU.add))
                dest = K["dest0"]
                dve.tensor_scalar(flip[:], dest[:], 0.0, float(P - 1), ALU.is_lt, ALU.mult)
                then(dve.tensor_scalar(placed[:], dest[:], lift[:], None, ALU.add))
                upwards = list(range(E - 3, 0, -2)) + list(range(0, E, 2))
                for n, e in enumerate(upwards):
                    start = e // 2 * REGION if e % 2 == 0 else 1 - (e + 1) // 2 * REGION
                    then(dve.tensor_scalar(move[:, n % 2, :], dest[:], float(start), jump[:, e:e + 1],
                                           ALU.is_ge, ALU.mult))
                    then(dve.tensor_tensor(placed[:], placed[:], move[:, n % 2, :], ALU.add))
                then(dve.tensor_copy(unflipped[:], placed[:]))
                then(dve.tensor_tensor(K["place0"][:], unflipped[:], flip[:], ALU.bitwise_xor))


def load_tiles(sp, K, rows, x, sem, g, G, limit):
    for j in range(G):
        tile = g * G + j
        at = K["table"][0:1, 1, tile:tile + 1] if isinstance(g, int) else K["table"][0:1, 1, bass.ds(tile, 1)]
        row = sp.value_load(at, min_val=0, max_val=limit)
        sp.dma_start(x[:, j, :], rows[bass.ds(row, P), :]).then_inc(sem, 16)


def tile_expert(pe, K, g, j, G, experts):
    tile = g * G + j
    at = K["table"][0:1, 0, tile:tile + 1] if isinstance(g, int) else K["table"][0:1, 0, bass.ds(tile, 1)]
    return pe.value_load(at, min_val=0, max_val=experts - 1)


def expert0(nc, K):
    G, N = 4, NT0 // 4
    y_out = K["mixed0"].rearrange("(g j p) d -> g p j d", j=G, p=P)
    with Phase(nc, "expert0") as ph:
        x = ph.sb("x", [P, 4, G, ROW], F32)
        xn = ph.sb("xn", [P, 2, G, P], F32)
        xT = ph.sb("xT", [P, 2, G, P], F32)
        hid = ph.sb("hid", [P, 2, G, H0], F32)
        hT = ph.sb("hT", [H0, 2, G, P], F32)
        y = ph.sb("y", [P, 4, G, P], F32)
        ps_xT = ph.psum("ps_xT", [P, G, P])
        ps_hid = ph.psum("ps_hid", [P, G, H0])
        ps_hT = ph.psum("ps_hT", [P, G, P])
        ps_y = ph.psum("ps_y", [P, G, P])
        x_loaded = ph.sems("x_loaded", 4)
        xn_ready = ph.sem("xn_ready")
        xn_turned = ph.sem("xn_turned")
        xT_ready = ph.sem("xT_ready")
        hid_done = ph.sem("hid_done")
        hid_ready = ph.sem("hid_ready")
        hid_turned = ph.sem("hid_turned")
        hT_ready = ph.sem("hT_ready")
        y_done = ph.sem("y_done")
        y_ready = ph.sem("y_ready")
        y_stored = ph.sems("y_stored", 4)
        block = ph.block()

        @block.sync
        def _(sp):
            def load(g, s, r):
                if not isinstance(g, int) or g >= 4:
                    wait_alone(K, sp, y_ready, g - 3)
                load_tiles(sp, K, K["sorted0"], x[:, s], x_loaded[s], g, G, E0 // 2 * REGION)

            def store(g, s, r):
                sp.wait_ge(y_ready, g + 1)
                dst = y_out[g] if isinstance(g, int) else y_out[bass.ds(g, 1)].rearrange("o p j d -> (o p) j d")
                sp.dma_start(dst, y[:, s]).then_inc(y_stored[s], 16)

            pipeline(sp, N, 4, [(0, load), (4, store)])
            for s in range(4):
                sp.wait_ge(y_stored[s], 16 * (N // 4))

        @block.vector
        def _(dve):
            def normalise(g, s, r):
                dve.wait_ge(x_loaded[s], r * (16 * G) + 16 * G)
                freed(dve, xn_turned, g, 2)
                normalise_rows(dve, xn[:, s % 2], x[:, s, :, 0:P], x[:, s, :, MEAN:MEAN + 1],
                               x[:, s, :, RSTD:RSTD + 1], G).then_inc(xn_ready, 1)

            def finish(g, s, r):
                dve.wait_ge(y_done, g + 1)
                if not isinstance(r, int) or r:
                    dve.wait_ge(y_stored[s], r * 16)
                dve.scalar_tensor_tensor(y[:, s], ps_y[:], 0.0, x[:, s, :, 0:P], ALU.max,
                                         ALU.add).then_inc(y_ready, 1)

            pipeline(dve, N, 4, [(1, normalise), (3, finish)])

        @block.scalar
        def _(act):
            def copy_xT(g, s, r):
                act.wait_ge(xn_turned, g + 1)
                freed(act, hid_done, g, 2)
                act.activation(xT[:, s % 2], ps_xT[:], ACT.Copy).then_inc(xT_ready, 1)

            def relu(g, s, r):
                act.wait_ge(hid_done, g + 1)
                freed(act, hid_turned, g, 2)
                act.activation(hid[:, s % 2], ps_hid[:], ACT.Relu).then_inc(hid_ready, 1)

            def copy_hT(g, s, r):
                act.wait_ge(hid_turned, g + 1)
                freed(act, y_done, g, 2)
                act.activation(hT[:, s % 2], ps_hT[0:H0], ACT.Copy).then_inc(hT_ready, 1)

            pipeline(act, N, 4, [(2, relu), (1, copy_xT), (2, copy_hT)])

        @block.tensor
        def _(pe):
            def turn_x(g, s, r):
                pe.wait_ge(xn_ready, g + 1)
                freed(pe, xT_ready, g, 1)
                for j in range(G):
                    ins = pe.transpose(ps_xT[:, j, :], xn[:, s % 2, j, :], K["ident"][:])
                ins.then_inc(xn_turned, 1)

            def hidden(g, s, r):
                e = [tile_expert(pe, K, g, j, G, E0) for j in range(G)]
                pe.wait_ge(xT_ready, g + 1)
                freed(pe, hid_ready, g, 1)
                for j in range(G):
                    pe.matmul(ps_hid[:, j, :], K["onesb"][0:3, :], K["biasrows"][:, bass.ds(e[j] * H0 + B1_AT, H0)],
                              start=(j == 0), stop=False, skip_group_check=True)
                    ins = pe.matmul(ps_hid[:, j, :], xT[:, s % 2, j, :],
                                    K["w1e"][:, bass.ds(e[j], 1), :].rearrange("p o h -> p (o h)"),
                                    start=False, stop=True, skip_group_check=True)
                ins.then_inc(hid_done, 1)

            def turn_hid(g, s, r):
                pe.wait_ge(hid_ready, g + 1)
                freed(pe, hT_ready, g, 1)
                for j in range(G):
                    ins = pe.transpose(ps_hT[0:H0, j, :], hid[:, s % 2, j, :], K["ident"][:])
                ins.then_inc(hid_turned, 1)

            def mix(g, s, r):
                e = [tile_expert(pe, K, g, j, G, E0) for j in range(G)]
                pe.wait_ge(hT_ready, g + 1)
                freed(pe, y_ready, g, 1)
                for j in range(G):
                    pe.matmul(ps_y[:, j, :], K["onesb"][0:3, :], K["biasrows"][:, bass.ds(e[j] * P + B2_AT, P)],
                              start=(j == 0), stop=False, skip_group_check=True)
                    ins = pe.matmul(ps_y[:, j, :], hT[:, s % 2, j, :],
                                    K["w2e"][:, bass.ds(e[j], 1), :].rearrange("p o h -> p (o h)"),
                                    start=False, stop=True, skip_group_check=True)
                ins.then_inc(y_done, 1)

            pipeline(pe, N, 4, [(1, turn_x), (3, mix), (2, turn_hid), (1, hidden)])


def mha(nc, K):
    G, N, U = 2, B // 2, 8
    J = G * HEADS
    SCALE = float(HD) ** -0.5
    x_out = K["x3"].rearrange("(g j p) d -> g p j d", j=G, p=P)
    with Phase(nc, "mha") as ph:
        idx = ph.sb("idx", [P, U, G], I32)
        x = ph.sb("x", [P, U, G, P], F32)
        bn = ph.sb("bn", [P, 2, G, 6], F32)
        mv = ph.sb("mv", [P, 4, G, 2], F32)
        xn = ph.sb("xn", [P, 2, G, P], F32)
        xT = ph.sb("xT", [P, 2, G, P], F32)
        qT = ph.sb("qT", [P, 2, G, P], F32)
        mx = ph.sb("mx", [P, J], F32)
        pr = ph.sb("pr", [P, 2, J, P], F32)
        prT = ph.sb("prT", [P, 2, J, P], F32)
        rs = ph.sb("rs", [P, J], F32)
        o = ph.sb("o", [P, 2, J, HD], F32)
        oT = ph.sb("oT", [P, 2, G, P], F32)
        kbd, vaug = K["kbd"], K["vaug"]

        ps_a = ph.psum("ps_a", [P, 512])
        ps_xT = ps_a[:, 0:G * P].rearrange("p (j n) -> p j n", j=G)
        ps_out = ps_a[:, G * P:2 * G * P].rearrange("p (j n) -> p j n", j=G)
        ps_qk = ph.psum("ps_qk", [P, 2, G * P])
        ps_b = ph.psum("ps_b", [P, 512])
        ps_v = ps_b[:, 0:G * P].rearrange("p (j n) -> p j n", j=G)
        ps_oT = ps_b[:, G * P:2 * G * P].rearrange("p (j n) -> p j n", j=G)
        ps_s = ph.psum("ps_s", [P, J, P])
        ps_prT = ph.psum("ps_prT", [P, J, P])
        ps_o = ph.psum("ps_o", [P, 512])
        ps_oh = ps_o[:, 0:J * (HD + 1)].rearrange("p (j d) -> p j d", j=J)

        idx_ready = ph.sem("idx_ready")
        x_loaded = ph.sems("x_loaded", U)
        stats_ready = ph.sem("stats_ready")
        var_ready = ph.sem("var_ready")
        veps_ready = ph.sem("veps_ready")
        rstd_ready = ph.sem("rstd_ready")
        xn_ready = ph.sem("xn_ready")
        xn_turned = ph.sem("xn_turned")
        xT_ready = ph.sem("xT_ready")
        qk_done = ph.sem("qk_done")
        v_done = ph.sem("v_done")
        q_ready = ph.sem("q_ready")
        k_ready = ph.sem("k_ready")
        v_ready = ph.sem("v_ready")
        scored = ph.sem("scored")
        mx_ready = ph.sem("mx_ready")
        less_ready = ph.sem("less_ready")
        pr_ready = ph.sem("pr_ready")
        pr_turned = ph.sem("pr_turned")
        prT_ready = ph.sem("prT_ready")
        attended = ph.sem("attended")
        rs_ready = ph.sem("rs_ready")
        o_ready = ph.sem("o_ready")
        o_turned = ph.sem("o_turned")
        oT_ready = ph.sem("oT_ready")
        out_done = ph.sem("out_done")
        x3_ready = ph.sem("x3_ready")
        x3_stored = ph.sems("x3_stored", U)
        block = ph.block()

        @block.sync
        def _(sp):
            def store(g, s, r):
                sp.wait_ge(x3_ready, g + 1)
                dst = x_out[g] if isinstance(g, int) else x_out[bass.ds(g, 1)].rearrange("o p j d -> (o p) j d")
                sp.dma_start(dst, x[:, s]).then_inc(x3_stored[s], 16)

            pipeline(sp, N, U, [(7, store)])
            for s in range(U):
                sp.wait_ge(x3_stored[s], 16 * (N // U))

        @block.gpsimd
        def _(pool):
            def gather(g, s, r):
                wait_alone(K, pool, idx_ready, g + 1)
                if not isinstance(r, int) or r:
                    wait_alone(K, pool, x3_stored[s], r * 16)
                for j in range(G):
                    pool.indirect_dma_start(
                        x[:, s, j, :], None, K["mixed0"],
                        bass.IndirectOffsetOnAxis(ap=idx[:, s, j:j + 1], axis=0)).then_inc(x_loaded[s], 16)

            def rstd(g, s, r):
                pool.wait_ge(veps_ready, g + 1)
                pool.tensor_tensor(mv[:, s % 4, :, 1], mv[:, s % 4, :, 1], K["minus_half"][:, 0:G],
                                   ALU.pow).then_inc(rstd_ready, 1)

            pipeline(pool, N, U, [(1, rstd), (0, gather)])

        @block.vector
        def _(dve):
            def indices(g, s, r):
                freed(dve, var_ready, g, U)
                first = g * G
                src = K["place0"][:, first:first + G] if isinstance(g, int) else K["place0"][:, bass.ds(first, G)]
                dve.tensor_copy(idx[:, s], src).then_inc(idx_ready, 1)

            def stats(g, s, r):
                dve.wait_ge(x_loaded[s], r * (16 * G) + 16 * G)
                for j in range(G):
                    ins = dve.bn_stats(bn[:, s % 2, j, :], x[:, s, j, :])
                ins.then_inc(stats_ready, 1)

            def aggregate(g, s, r):
                wait_alone(K, dve, stats_ready, g + 1)
                for j in range(G):
                    ins = dve.bn_aggr(mv[:, s % 4, j, :], bn[:, s % 2, j, :])
                ins.then_inc(var_ready, 1)

            def add_eps(g, s, r):
                dve.wait_ge(var_ready, g + 1)
                dve.tensor_scalar(mv[:, s % 4, :, 1], mv[:, s % 4, :, 1], EPS, None, ALU.add).then_inc(veps_ready, 1)

            def normalise(g, s, r):
                dve.wait_ge(rstd_ready, g + 1)
                freed(dve, xn_turned, g, 2)
                normalise_rows(dve, xn[:, s % 2], x[:, s], mv[:, s % 4, :, 0:1], mv[:, s % 4, :, 1:2],
                               G).then_inc(xn_ready, 1)

            def values(g, s, r):
                dve.wait_ge(v_done, g + 1)
                freed(dve, attended, g, 4)
                dve.tensor_tensor(vaug[:, s % 4, :, 0:HD], ps_v.rearrange("p j (h d) -> p (j h) d", h=HEADS),
                                  K["bvg"][:].rearrange("p (j d) -> p j d", j=J), ALU.add).then_inc(v_ready, 1)

            def row_max(g, s, r):
                dve.wait_ge(scored, g + 1)
                dve.tensor_reduce(mx[:], ps_s[:], AX.X, ALU.max).then_inc(mx_ready, 1)

            def less_max(g, s, r):
                dve.wait_ge(mx_ready, g + 1)
                freed(dve, pr_turned, g, 2)
                dve.tensor_tensor(pr[:, s % 2], ps_s[:], mx[:].unsqueeze(2).to_broadcast([P, J, P]),
                                  ALU.subtract).then_inc(less_ready, 1)

            def inverse(g, s, r):
                dve.wait_ge(attended, g + 1)
                dve.reciprocal(rs[:], ps_oh[:, :, HD]).then_inc(rs_ready, 1)

            def weigh(g, s, r):
                dve.wait_ge(rs_ready, g + 1)
                freed(dve, o_turned, g, 2)
                dve.scalar_tensor_tensor(o[:, s % 2], ps_oh[:, :, 0:HD], K["linked"][:],
                                         rs[:].unsqueeze(2).to_broadcast([P, J, HD]), ALU.mult,
                                         ALU.mult).then_inc(o_ready, 1)

            def residual(g, s, r):
                dve.wait_ge(out_done, g + 1)
                dve.tensor_tensor(x[:, s], ps_out, x[:, s], ALU.add).then_inc(x3_ready, 1)

            pipeline(dve, N, U, [(0, indices), (1, stats), (1, aggregate), (2, values), (1, add_eps), (6, weigh), (1, normalise),
                                 (3, row_max), (3, less_max), (5, inverse), (6, residual)])

        @block.scalar
        def _(act):
            def exps(g, s, r):
                act.wait_ge(less_ready, g + 1)
                act.activation(pr[:, s % 2], pr[:, s % 2], ACT.Exp, scale=SCALE).then_inc(pr_ready, 1)

            def copy_q(g, s, r):
                act.wait_ge(qk_done, g + 1)
                freed(act, scored, g, 2)
                act.activation(qT[:, s % 2], ps_qk[:, 0, :].rearrange("p (j n) -> p j n", j=G), ACT.Identity,
                               bias=K["bqk"][:, 0:1]).then_inc(q_ready, 1)

            def copy_k(g, s, r):
                for hd in range(HEADS):
                    part = slice(hd * HD, (hd + 1) * HD)
                    ins = act.activation(kbd[part, s % 2, :, hd, :], ps_qk[part, 1, :].rearrange("p (j n) -> p j n", j=G),
                                         ACT.Identity, bias=K["bqk"][part, 1:2])
                ins.then_inc(k_ready, 1)

            def copy_xT(g, s, r):
                act.wait_ge(xn_turned, g + 1)
                freed(act, v_done, g, 2)
                act.activation(xT[:, s % 2], ps_xT, ACT.Copy).then_inc(xT_ready, 1)

            def copy_prT(g, s, r):
                act.wait_ge(pr_turned, g + 1)
                freed(act, attended, g, 2)
                for j in range(G):
                    ins = act.activation(prT[:, s % 2, j * HEADS:(j + 1) * HEADS],
                                         ps_prT[:, j * HEADS:(j + 1) * HEADS, :], ACT.Copy)
                ins.then_inc(prT_ready, 1)

            def copy_oT(g, s, r):
                act.wait_ge(o_turned, g + 1)
                freed(act, out_done, g, 1)
                act.activation(oT[:, s % 2], ps_oT, ACT.Copy).then_inc(oT_ready, 1)

            pipeline(act, N, U, [(2, copy_q), (2, copy_k), (6, copy_oT), (1, copy_xT), (4, copy_prT), (3, exps)])

        @block.tensor
        def _(pe):
            def upto(count):
                return min(count, N) if isinstance(count, int) else count

            def out(g, s, r):
                pe.wait_ge(oT_ready, g + 1)
                pe.wait_ge(xT_ready, upto(g + 6))
                freed(pe, x3_ready, g, 1)
                pe.matmul(ps_out, K["onesb"][0:3, :],
                          K["biasrows"][:, BO_AT:BO_AT + P].unsqueeze(1).to_broadcast([3, G, P]),
                          start=True, stop=False, skip_group_check=True)
                for j in range(G):
                    ins = pe.matmul(ps_out[:, j, :], oT[:, s % 2, j, :], K["woT"][:], start=False, stop=True,
                                    skip_group_check=True)
                ins.then_inc(out_done, 1)

            def attend(g, s, r):
                pe.wait_ge(prT_ready, g + 1)
                freed(pe, o_ready, g, 1)
                for j in range(J):
                    ins = pe.matmul(ps_oh[:, j, :], prT[:, s % 2, j, :], vaug[:, s % 4, j, :], start=True, stop=True)
                ins.then_inc(attended, 1)

            def project(g, s, r):
                flat = xT[:, s % 2].rearrange("p j n -> p (j n)")
                pe.wait_ge(xT_ready, g + 1)
                freed(pe, k_ready, g, 1)
                pe.matmul(ps_qk[:, 0, :], K["wqT"][:], flat, start=True, stop=True)
                pe.matmul(ps_qk[:, 1, :], K["wkT"][:], flat, start=True, stop=True).then_inc(qk_done, 1)
                freed(pe, v_ready, g, 1)
                freed(pe, oT_ready, g, 5)
                for j in range(G):
                    ins = pe.matmul(ps_v[:, j, :], xT[:, s % 2, j, :], K["wvT"][:], start=True, stop=True)
                ins.then_inc(v_done, 1)

            def turn_x(g, s, r):
                pe.wait_ge(xn_ready, g + 1)
                freed(pe, xT_ready, g, 1)
                freed(pe, x3_ready, g, 6)
                for j in range(G):
                    ins = pe.transpose(ps_xT[:, j, :], xn[:, s % 2, j, :], K["ident"][:])
                ins.then_inc(xn_turned, 1)

            def turn_pr(g, s, r):
                pe.wait_ge(pr_ready, g + 1)
                freed(pe, prT_ready, g, 1)
                for j in range(J):
                    ins = pe.transpose(ps_prT[:, j, :], pr[:, s % 2, j, :], K["ident"][:])
                ins.then_inc(pr_turned, 1)

            def score(g, s, r):
                pe.wait_ge(k_ready, g + 1)
                freed(pe, less_ready, g, 1)
                for j in range(G):
                    rows = ps_s[:, j * HEADS:(j + 1) * HEADS, :]
                    pe.matmul(rows, K["identb"][:], K["far"][:].unsqueeze(1).to_broadcast([P, HEADS, P]),
                              start=True, stop=False)
                    ins = pe.matmul(rows, qT[:, s % 2, j, :], kbd[:, s % 2, j], start=False, stop=True)
                ins.then_inc(scored, 1)

            def turn_o(g, s, r):
                pe.wait_ge(o_ready, g + 1)
                pe.wait_ge(v_ready, upto(g + 5))
                freed(pe, oT_ready, g, 1)
                for j in range(G):
                    ins = pe.transpose(ps_oT[:, j, :],
                                       o[:, s % 2, j * HEADS:(j + 1) * HEADS].rearrange("p h d -> p (h d)"),
                                       K["ident"][:])
                ins.then_inc(o_turned, 1)

            pipeline(pe, N, U, [(3, score), (6, turn_o), (1, turn_x), (4, turn_pr), (5, attend), (6, out),
                                (1, project)])


def hidden_chunk(pe, K, ps_h, xhi, xlo, gelu_done, h_done, g, c):
    cols = slice(c * P, (c + 1) * P)
    freed(pe, gelu_done, g, 1, per=NCH, k=c + 1)
    pe.matmul(ps_h[:, c, :], K["w1lo"][:, cols], xhi, start=True, stop=False)
    pe.matmul(ps_h[:, c, :], K["w1hi"][:, cols], xlo, start=False, stop=False)
    pe.matmul(ps_h[:, c, :], K["w1hi"][:, cols], xhi, start=False, stop=True).then_inc(h_done, 1)


def gate(nc, K):
    G, N, U = 4, B // 4, 8
    x_in = K["x3"].rearrange("(g j p) d -> g p j d", j=G, p=P)
    with Phase(nc, "gate") as ph:
        row = ph.sb("row", [P, U, G, ROW], F32)
        bn = ph.sb("bn", [P, 2, G, 6], F32)
        xn = ph.sb("xn", [P, 2, G, P], F32)
        xhi = ph.sb("xhi", [P, 2, G * P], F16)
        xlo = ph.sb("xlo", [P, 2, G * P], F16)
        h = ph.sb("h", [P, 2, NCH, G * P], F32)
        onehot = ph.sb("onehot", [P, 2, G, E1], BF16)
        less = ph.sb("less", [P, G, E1], F32)
        th = ph.sb("th", [P, G, E1], F32)
        den = ph.sb("den", [P, G, E1], F32)
        rden = ph.sb("rden", [P, G, E1], F32)
        ex = ph.sb("ex", [P, G, E1], F32)
        total = ph.sb("total", [P, G], F32)
        idx = ph.sb("idx", [P, U, G], I32)
        ps_xT = ph.psum("ps_xT", [P, G * P])
        ps_h = ph.psum("ps_h", [P, NCH, G * P])
        ps_r = ph.psum("ps_r", [P, 512])
        ps_logit = ps_r[:, 0:G * E1].rearrange("p (j e) -> p j e", j=G)
        ps_rank = ps_r[:, 256:256 + (G + 1) * E1].rearrange("p (j e) -> p j e", j=G + 1)
        x_loaded = ph.sems("x_loaded", U)
        stats_ready = ph.sem("stats_ready")
        var_ready = ph.sem("var_ready")
        veps_ready = ph.sem("veps_ready")
        rstd_ready = ph.sem("rstd_ready")
        xn_ready = ph.sem("xn_ready")
        xn_turned = ph.sem("xn_turned")
        xhi_ready = ph.sem("xhi_ready")
        xlo_ready = ph.sem("xlo_ready")
        h_done = ph.sem("h_done")
        gelu_done = ph.sem("gelu_done")
        logit_ready = ph.sem("logit_ready")
        onehot_ready = ph.sem("onehot_ready")
        less_ready = ph.sem("less_ready")
        th_ready = ph.sem("th_ready")
        rank_ready = ph.sem("rank_ready")
        den_ready = ph.sem("den_ready")
        rden_ready = ph.sem("rden_ready")
        ex_ready = ph.sem("ex_ready")
        total_ready = ph.sem("total_ready")
        prob_ready = ph.sem("prob_ready")
        idx_ready = ph.sem("idx_ready")
        rows_stored = ph.sems("rows_stored", U)
        router = Router(ph, K, (logit_ready, rank_ready, onehot_ready), G, E1, K["base1"][:], ps_logit, ps_rank,
                        onehot)
        block = ph.block()

        @block.sync
        def _(sp):
            def load(g, s, r):
                if not isinstance(r, int) or r:
                    sp.wait_ge(rows_stored[s], r * (16 * G))
                src = x_in[g] if isinstance(g, int) else x_in[bass.ds(g, 1)].rearrange("o p j d -> (o p) j d")
                sp.dma_start(row[:, s, :, 0:P], src).then_inc(x_loaded[s], 16)

            pipeline(sp, N, U, [(0, load)])

        @block.gpsimd
        def _(pool):
            def rstd(g, s, r):
                pool.wait_ge(veps_ready, g + 1)
                pool.tensor_tensor(row[:, s, :, RSTD], row[:, s, :, RSTD], K["minus_half"][:, 0:G],
                                   ALU.pow).then_inc(rstd_ready, 1)

            def scatter(g, s, r):
                pool.wait_ge(prob_ready, g + 1)
                wait_alone(K, pool, idx_ready, g + 1)
                for j in range(G):
                    pool.indirect_dma_start(
                        K["sorted1"], bass.IndirectOffsetOnAxis(ap=idx[:, s, j:j + 1], axis=0),
                        row[:, s, j, :], None).then_inc(rows_stored[s], 16)

            pipeline(pool, N, U, [(0, rstd), (4, scatter)])
            for s in range(U):
                pool.wait_ge(rows_stored[s], 16 * G * (N // U))

        @block.vector
        def _(dve):
            def stats(g, s, r):
                dve.wait_ge(x_loaded[s], r * 16 + 16)
                for j in range(G):
                    ins = dve.bn_stats(bn[:, s % 2, j, :], row[:, s, j, 0:P])
                ins.then_inc(stats_ready, 1)

            def aggregate(g, s, r):
                wait_alone(K, dve, stats_ready, g + 1)
                for j in range(G):
                    ins = dve.bn_aggr(row[:, s, j, MEAN:RSTD + 1], bn[:, s % 2, j, :])
                ins.then_inc(var_ready, 1)

            def add_eps(g, s, r):
                dve.wait_ge(var_ready, g + 1)
                dve.tensor_scalar(row[:, s, :, RSTD], row[:, s, :, RSTD], EPS, None, ALU.add).then_inc(veps_ready, 1)

            def normalise(g, s, r):
                dve.wait_ge(rstd_ready, g + 1)
                freed(dve, xn_turned, g, 2)
                normalise_rows(dve, xn[:, s % 2], row[:, s, :, 0:P], row[:, s, :, MEAN:MEAN + 1],
                               row[:, s, :, RSTD:RSTD + 1], G).then_inc(xn_ready, 1)

            def low_part(g, s, r):
                dve.wait_ge(xhi_ready, g + 1)
                freed(dve, h_done, g, 2, per=NCH, k=NCH)
                dve.tensor_tensor(xlo[:, s % 2], ps_xT[:], xhi[:, s % 2], ALU.subtract).then_inc(xlo_ready, 1)

            def less_top(g, s, r):
                dve.wait_ge(router.top_ready, g + 1)
                dve.tensor_tensor(less[:], ps_logit, router.top_of[:, s % 2].unsqueeze(2).to_broadcast([P, G, E1]),
                                  ALU.subtract).then_inc(less_ready, 1)

            def one_less(g, s, r):
                dve.wait_ge(th_ready, g + 1)
                dve.tensor_scalar(den[:], th[:], -1.0, 1.0, ALU.mult, ALU.add).then_inc(den_ready, 1)

            def invert(g, s, r):
                dve.wait_ge(den_ready, g + 1)
                dve.reciprocal(rden[:], den[:]).then_inc(rden_ready, 1)

            def exps(g, s, r):
                dve.wait_ge(rden_ready, g + 1)
                dve.scalar_tensor_tensor(ex[:], th[:], 1.0, rden[:], ALU.add, ALU.mult).then_inc(ex_ready, 1)

            def add_up(g, s, r):
                dve.wait_ge(ex_ready, g + 1)
                dve.tensor_reduce(total[:], ex[:], AX.X, ALU.add).then_inc(total_ready, 1)

            def probability(g, s, r):
                dve.wait_ge(total_ready, g + 1)
                dve.reciprocal(row[:, s, :, PROB], total[:]).then_inc(prob_ready, 1)

            def index(g, s, r):
                first = g * G
                number = K["number"][:, first:first + G] if isinstance(g, int) else K["number"][:, bass.ds(first, G)]
                dve.tensor_copy(row[:, s, :, NUM:NUM + 1].bitcast(I32).rearrange("p j o -> p (j o)"), number)
                dve.wait_ge(router.dest_ready, g + 1)
                router.index(dve, g, s, idx[:, s]).then_inc(idx_ready, 1)

            def of(step):
                return lambda g, s, r: step(dve, g, s)

            pipeline(dve, N, U, [
                (0, stats), (4, of(router.dest)), (0, aggregate), (0, add_eps), (1, low_part), (4, add_up), (4, index),
                (3, of(router.top)), (4, probability), (3, of(router.equal)), (3, of(router.key)),
                (3, of(router.first)), (3, less_top), (3, of(router.choose)), (0, normalise), (3, one_less),
                (3, of(router.place)), (3, invert), (3, of(router.own)), (3, exps)])

        @block.scalar
        def _(act):
            def high_part(g, s, r):
                act.wait_ge(xn_turned, g + 1)
                freed(act, h_done, g, 2, per=NCH, k=NCH)
                act.activation(xhi[:, s % 2], ps_xT[:], ACT.Copy).then_inc(xhi_ready, 1)

            def tanh(g, s, r):
                act.wait_ge(less_ready, g + 1)
                freed(act, ex_ready, g, 1)
                act.activation(th[:], less[:], ACT.Tanh, scale=0.5).then_inc(th_ready, 1)

            def gelu(c):
                def step(g, s, r):
                    if c == 0:
                        freed(act, logit_ready, g, 2)
                    act.wait_ge(h_done, g * NCH + c + 1)
                    act.activation(h[:, s % 2, c, :], ps_h[:, c, :], ACT.Gelu,
                                   bias=K["b1"][:, c:c + 1]).then_inc(gelu_done, 1)
                return step

            pipeline(act, N, U, [(2, gelu(1)), (2, gelu(2)), (2, gelu(3)), (3, tanh), (1, gelu(0)), (0, high_part)])

        @block.tensor
        def _(pe):
            def logits(g, s, r):
                pe.wait_ge(gelu_done, g * NCH + NCH)
                freed(pe, router.own_ready, g, 1)
                pe.matmul(ps_logit, K["onesb"][0:3, :],
                          K["biasrows"][:, BG_AT:BG_AT + E1].unsqueeze(1).to_broadcast([3, G, E1]),
                          start=True, stop=False, skip_group_check=True)
                for j in range(G):
                    for c in range(NCH):
                        ins = pe.matmul(ps_logit[:, j, :], h[:, s % 2, c, j * P:(j + 1) * P], K["wg"][:, c, :],
                                        start=False, stop=(c == NCH - 1), skip_group_check=True)
                ins.then_inc(logit_ready, 1)

            def turn_x(g, s, r):
                pe.wait_ge(xn_ready, g + 1)
                freed(pe, xlo_ready, g, 1)
                for j in range(G):
                    ins = pe.transpose(ps_xT[:, j * P:(j + 1) * P], xn[:, s % 2, j, :], K["ident"][:])
                ins.then_inc(xn_turned, 1)

            def rank(g, s, r):
                pe.wait_ge(onehot_ready, g + 1)
                pe.wait_ge(less_ready, g + 1)
                rank_rows(pe, K, ps_rank, onehot[:, s % 2], G).then_inc(rank_ready, 1)

            def hidden(c):
                def step(g, s, r):
                    pe.wait_ge(xlo_ready, g + 1)
                    hidden_chunk(pe, K, ps_h, xhi[:, s % 2], xlo[:, s % 2], gelu_done, h_done, g, c)
                return step

            pipeline(pe, N, U, [(3, logits), (1, hidden(0)), (1, hidden(1)), (1, hidden(2)), (3, rank), (0, turn_x),
                                (1, hidden(3))])


def expert1(nc, K, out_rows):
    G, N = 4, NT1 // 4
    with Phase(nc, "expert1") as ph:
        x = ph.sb("x", [P, 4, G, ROW], F32)
        xn = ph.sb("xn", [P, 2, G, P], F32)
        xhi = ph.sb("xhi", [P, 2, G * P], F16)
        xlo = ph.sb("xlo", [P, 2, G * P], F16)
        h = ph.sb("h", [P, 2, NCH, G * P], F32)
        y = ph.sb("y", [P, 4, G, P], F32)
        ps_xT = ph.psum("ps_xT", [P, G * P])
        ps_h = ph.psum("ps_h", [P, NCH, G * P])
        ps_y = ph.psum("ps_y", [P, 2, G, P])
        x_loaded = ph.sems("x_loaded", 4)
        xn_ready = ph.sem("xn_ready")
        xn_turned = ph.sem("xn_turned")
        xhi_ready = ph.sem("xhi_ready")
        xlo_ready = ph.sem("xlo_ready")
        h_done = ph.sem("h_done")
        gelu_done = ph.sem("gelu_done")
        y_done = ph.sem("y_done")
        y_ready = ph.sem("y_ready")
        y_stored = ph.sems("y_stored", 4)
        block = ph.block()

        @block.sync
        def _(sp):
            def load(g, s, r):
                if not isinstance(r, int) or r:
                    wait_alone(K, sp, y_stored[s], r * (16 * G))
                load_tiles(sp, K, K["sorted1"], x[:, s], x_loaded[s], g, G, E1 // 2 * REGION)

            pipeline(sp, N, 4, [(0, load)])

        @block.gpsimd
        def _(pool):
            def scatter(g, s, r):
                wait_alone(K, pool, y_ready, g + 1)
                for j in range(G):
                    pool.indirect_dma_start(
                        out_rows, bass.IndirectOffsetOnAxis(ap=x[:, s, j, NUM:NUM + 1].bitcast(I32), axis=0),
                        y[:, s, j, :], None, bounds_check=ROWS - 1, oob_is_err=False).then_inc(y_stored[s], 16)

            pipeline(pool, N, 4, [(4, scatter)])
            for s in range(4):
                pool.wait_ge(y_stored[s], 16 * G * len(range(s, N, 4)))

        @block.vector
        def _(dve):
            def normalise(g, s, r):
                dve.wait_ge(x_loaded[s], r * (16 * G) + 16 * G)
                freed(dve, xn_turned, g, 2)
                normalise_rows(dve, xn[:, s % 2], x[:, s, :, 0:P], x[:, s, :, MEAN:MEAN + 1],
                               x[:, s, :, RSTD:RSTD + 1], G).then_inc(xn_ready, 1)

            def low_part(g, s, r):
                dve.wait_ge(xhi_ready, g + 1)
                freed(dve, h_done, g, 2, per=NCH, k=NCH)
                dve.tensor_tensor(xlo[:, s % 2], ps_xT[:], xhi[:, s % 2], ALU.subtract).then_inc(xlo_ready, 1)

            def finish(g, s, r):
                dve.wait_ge(y_done, g + 1)
                if not isinstance(r, int) or r:
                    dve.wait_ge(y_stored[s], r * (16 * G))
                for j in range(G):
                    ins = dve.scalar_tensor_tensor(y[:, s, j, :], ps_y[:, s % 2, j, :], x[:, s, j, PROB:PROB + 1],
                                                   x[:, s, j, 0:P], ALU.mult, ALU.add)
                ins.then_inc(y_ready, 1)

            pipeline(dve, N, 4, [(2, low_part), (4, finish), (1, normalise)])

        @block.scalar
        def _(act):
            def high_part(g, s, r):
                act.wait_ge(xn_turned, g + 1)
                freed(act, h_done, g, 2, per=NCH, k=NCH)
                act.activation(xhi[:, s % 2], ps_xT[:], ACT.Copy).then_inc(xhi_ready, 1)

            def gelu(c):
                def step(g, s, r):
                    if c == 0:
                        freed(act, y_done, g, 2)
                    act.wait_ge(h_done, g * NCH + c + 1)
                    act.activation(h[:, s % 2, c, :], ps_h[:, c, :], ACT.Gelu,
                                   bias=K["b1"][:, c:c + 1]).then_inc(gelu_done, 1)
                return step

            pipeline(act, N, 4, [(2, gelu(0)), (2, gelu(1)), (1, high_part), (2, gelu(2)), (2, gelu(3))])

        @block.tensor
        def _(pe):
            def turn_x(g, s, r):
                pe.wait_ge(xn_ready, g + 1)
                freed(pe, xlo_ready, g, 1)
                for j in range(G):
                    ins = pe.transpose(ps_xT[:, j * P:(j + 1) * P], xn[:, s % 2, j, :], K["ident"][:])
                ins.then_inc(xn_turned, 1)

            def hidden(c):
                def step(g, s, r):
                    pe.wait_ge(xlo_ready, g + 1)
                    hidden_chunk(pe, K, ps_h, xhi[:, s % 2], xlo[:, s % 2], gelu_done, h_done, g, c)
                return step

            def mix(j):
                def step(g, s, r):
                    e = tile_expert(pe, K, g, j, G, E1)
                    if j == 0:
                        pe.wait_ge(gelu_done, g * NCH + NCH)
                        freed(pe, y_ready, g, 2)
                    y_of = ps_y[:, s % 2, j, :]
                    pe.matmul(y_of, K["onesb"][0:3, :], K["biasrows"][:, bass.ds(e * P + BD_AT, P)],
                              start=(j == 0), stop=False, skip_group_check=True)
                    for c in range(NCH):
                        w = K["wd"][:, bass.ds(e, 1), c, :].rearrange("p o d -> p (o d)")
                        ins = pe.matmul(y_of, h[:, s % 2, c, j * P:(j + 1) * P], w,
                                        start=False, stop=(c == NCH - 1), skip_group_check=True)
                    if j == G - 1:
                        ins.then_inc(y_done, 1)
                return step

            pipeline(pe, N, 4, [(3, mix(0)), (2, hidden(0)), (3, mix(1)), (2, hidden(1)), (1, turn_x), (3, mix(2)),
                                (2, hidden(2)), (3, mix(3)), (2, hidden(3))])


def build(nc, T, out):
    with ExitStack() as ctx:
        K = {}
        for name, shape, dt in [
            ("ident", [P, P], F32), ("identb", [P, P], BF16), ("onesf", [P, P], F32), ("onesb", [P, P], BF16),
            ("before", [P, P], BF16), ("upto", [E0, E0], F32), ("count", [P, 256], F32), ("rev0", [P, E0], F32),
            ("sign", [P, E0], F32), ("tile0", [P, E0], F32), ("start", [P, E0], F32), ("number", [P, B], I32), ("minus_half", [P, 4], F32), ("padrow", [P, ROW], F32),
            ("cap", [P, P], F32), ("far", [P, P], BF16), ("linked", [P, 1], F32),
            ("wa", [P, 2], F32), ("wa2", [P, P], F32), ("wh", [P, P], F32), ("rwT", [P, E0], F32),
            ("wqT", [P, P], F32), ("wkT", [P, P], F32), ("wvT", [P, P], F32), ("woT", [P, P], F32),
            ("bqk", [P, 2], F32), ("bv", [P, P], F32), ("bvg", [P, 2 * P], F32), ("b1", [P, NCH], F32),
            ("biasrows", [3, NBIAS], BF16), ("w1e", [P, E0, H0], F32), ("w2e", [H0, E0, P], F32),
            ("w1", [P, HID], F32), ("w1hi", [P, HID], F16), ("w1lo", [P, HID], F16),
            ("wg", [P, NCH, E1], F32), ("wd", [P, E1, NCH, P], F32),
            ("kbd", [P, 2, 2, HEADS, P], F32), ("vaug", [P, 4, 2 * HEADS, HD + 1], F32),
            ("base0", [P, E0], F32), ("base1", [P, E1], F32), ("dest0", [P, B], F32), ("place0", [P, B], I32),
            ("table", [1, 2, NT0], I32),
        ]:
            K[name] = ctx.enter_context(nc.sbuf_tensor(f"k_{name}", shape, dt))
        K["passed"] = ctx.enter_context(nc.semaphore("passed"))
        K["sorted0"] = nc.dram_tensor("sorted0", (E0 // 2 * REGION + P, ROW), F32, kind="Internal").ap()
        K["sorted1"] = nc.dram_tensor("sorted1", (E1 // 2 * REGION + P, ROW), F32, kind="Internal").ap()
        K["mixed0"] = nc.dram_tensor("mixed0", (NT0 * P, P), F32, kind="Internal").ap()
        K["x3"] = nc.dram_tensor("x3", (ROWS, P), F32, kind="Internal").ap()
        setup(nc, K, T)
        gat(nc, K, T)
        table(nc, K, 0)
        expert0(nc, K)
        mha(nc, K)
        gate(nc, K)
        table(nc, K, 1)
        expert1(nc, K, out.rearrange("b n d -> (b n) d"))


_INS = ["x", "adj", "L0_gnn_W", "L0_gnn_a", "L0_ffn_router_w", "L0_ffn_router_b", "L0_ffn_W1", "L0_ffn_b1",
        "L0_ffn_W2", "L0_ffn_b2", "L1_gnn_wq", "L1_gnn_bq", "L1_gnn_wk", "L1_gnn_bk", "L1_gnn_wv", "L1_gnn_bv",
        "L1_gnn_wo", "L1_gnn_bo", "L1_ffn_W1", "L1_ffn_b1", "L1_ffn_Wg", "L1_ffn_bg", "L1_ffn_Wd", "L1_ffn_bd"]


def kernel(**inputs):
    import numpy as _np
    import concourse.bacc as _bacc
    from concourse import mybir as _mybir
    from concourse.bass_utils import run_bass_kernel_spmd as _run

    nc = _bacc.Bacc("TRN2", target_bir_lowering=False, num_devices=1)
    arrays, T = {}, {}
    for name in _INS:
        a = _np.ascontiguousarray(inputs[name])
        arrays[f"in_{name}"] = a
        T[name] = nc.dram_tensor(f"in_{name}", a.shape, _mybir.dt.from_np(a.dtype), kind="ExternalInput").ap()
    out = nc.dram_tensor("out_0", (B, P, P), F32, kind="ExternalOutput").ap()
    build(nc, T, out)
    r = _run(nc, [arrays], core_ids=[0])
    return r.results[0]["out_0"]
```

```python
from contextlib import ExitStack

import concourse.bass as bass
from concourse import mybir

ALU = mybir.AluOpType
ACT = mybir.ActivationFunctionType
AX = mybir.AxisListType
F32 = mybir.dt.float32
F16 = mybir.dt.float16
BF16 = mybir.dt.bfloat16
I32 = mybir.dt.int32

P = 128
B = 128
ROWS = B * P
E0, H0 = 32, 32
E1, HID = 8, 512
NCH = HID // P
HEADS, HD = 4, 32
EPS = 1e-5
REGION = ROWS + 2 * P
NT0 = ROWS // P + E0
NT1 = ROWS // P + E1
ROW = P + 4
MEAN, RSTD, PROB, NUM = P, P + 1, P + 2, P + 3
NO_ROW = 1 << 20
MASKED_E0 = -1e9
SLOPE = 0.01
FAR = -1e30

B1_AT = 0
B2_AT = B1_AT + E0 * H0
BD_AT = B2_AT + E0 * P
RB_AT = BD_AT + E1 * P
BO_AT = RB_AT + E0
BG_AT = BO_AT + P
NBIAS = BG_AT + E1


def pipeline(eng, n, unroll, steps, peel=8):
    last = max(lag for lag, _ in steps)
    assert last <= peel and peel % unroll == 0

    def peeled(t):
        for lag, f in steps:
            if 0 <= t - lag < n:
                f(t - lag, (t - lag) % unroll, (t - lag) // unroll)

    for t in range(peel):
        peeled(t)
    with eng.Fori(peel // unroll, n // unroll) as i:
        for u in range(unroll):
            for lag, f in steps:
                f(i * unroll + (u - lag), (u - lag) % unroll, i + (u - lag) // unroll)
    for t in range(n // unroll * unroll, n + last):
        peeled(t)


def freed(eng, sem, g, depth, per=1, k=1):
    if not isinstance(g, int) or g >= depth:
        eng.wait_ge(sem, (g - depth) * per + k)


def wait_alone(K, eng, sem, value):
    eng.wait_ge(sem, value)
    if not isinstance(value, int):
        eng.sem_inc(K["passed"], 1)


class Phase:

    def __init__(self, nc, name):
        self.nc, self.name, self.ctx, self.used = nc, name, ExitStack(), []

    def __enter__(self):
        return self

    def __exit__(self, *exc):
        self.ctx.__exit__(*exc)
        self.nc.clear_and_free_semaphores(self.used)
        self.nc.all_engine_barrier()

    def sb(self, name, shape, dt):
        return self.ctx.enter_context(self.nc.sbuf_tensor(f"{self.name}_{name}", shape, dt))

    def psum(self, name, shape, dt=F32):
        return self.ctx.enter_context(self.nc.psum_tensor(f"{self.name}_{name}", shape, dt))

    def sem(self, name):
        self.used.append(self.nc.alloc_semaphore(f"{self.name}_{name}"))
        return self.used[-1]

    def sems(self, name, n):
        return [self.sem(f"{name}{i}") for i in range(n)]

    def block(self):
        return self.ctx.enter_context(self.nc.Block())


def setup(nc, K, T):
    with Phase(nc, "setup") as ph:
        wload = ph.sb("wload", [P, 6, P], F32)
        acol = ph.sb("acol", [P, 2], F32)
        wT = ph.sb("wT", [P, P], F32)
        wa = ph.sb("wa", [P, 2], F32)
        adj = ph.sb("adj", [P, P], I32)
        off = ph.sb("off", [P, P], F32)
        biasf = ph.sb("biasf", [P, 64], F32)
        res1 = ph.sb("res1", [P, 64], F32)
        res2 = ph.sb("res2", [P, 64], F32)
        part = [ph.sb(f"part{k}", [P, 64], BF16) for k in range(3)]
        bvrow = ph.sb("bvrow", [P, P], F32)
        pt = ph.psum("pt", [P, 8, 512])

        loads = ph.sem("loads")
        bias_zero = ph.sem("bias_zero")
        ones_set = ph.sem("ones_set")
        pool_step = ph.sem("pool_step")
        transposed = ph.sem("transposed")
        wT_ready = ph.sem("wT_ready")
        wa_ready = ph.sem("wa_ready")
        dve_step = ph.sem("dve_step")
        parts_ready = ph.sem("parts_ready")
        rows_stored = ph.sem("rows_stored")
        rows_stored_pool = ph.sem("rows_stored_pool")
        block = ph.block()

        pieces = [
            ("L0_ffn_b1", 0, E0 * H0 // P, P, B1_AT),
            ("L0_ffn_b2", 8, E0, P, B2_AT),
            ("L1_ffn_bd", 40, E1, P, BD_AT),
            ("L0_ffn_router_b", 48, 1, E0, RB_AT),
            ("L1_gnn_bo", 49, 1, P, BO_AT),
            ("L1_ffn_bg", 50, 1, E1, BG_AT),
        ]

        def flat(ap):
            return ap.rearrange("a b -> (a b)") if len(ap.shape) == 2 else ap

        def bias_rows(eng, k, sem):
            with nc.allow_non_contiguous_dma(reason="a few hundred bias values"):
                for name, at, cols, parts, to in pieces:
                    eng.dma_start(K["biasrows"][k:k + 1, to:to + parts * cols],
                                  part[k][0:parts, at:at + cols]).then_inc(sem, 16)

        @block.sync
        def _(sp):
            sp.wait_ge(bias_zero, 1)
            with nc.allow_non_contiguous_dma(reason="a few hundred bias values"):
                for name, at, cols, parts, _ in pieces:
                    sp.dma_start(biasf[0:parts, at:at + cols],
                                 flat(T[name]).rearrange("(p c) -> p c", c=cols)).then_inc(loads, 16)
            for k, name in enumerate(["L0_gnn_W", "L1_gnn_wq", "L1_gnn_wk", "L1_gnn_wv", "L1_gnn_wo"]):
                sp.dma_start(wload[:, k, :], T[name]).then_inc(loads, 16)
            sp.dma_start(wload[0:E0, 5, :], T["L0_ffn_router_w"]).then_inc(loads, 16)
            sp.wait_ge(parts_ready, 1)
            bias_rows(sp, 0, rows_stored)
            sp.wait_ge(rows_stored, 16 * 2 * len(pieces))

        NLOADS = 14 + len(pieces)

        @block.scalar
        def _(act):
            act.dma_start(adj[:], T["adj"]).then_inc(loads, 16)
            with nc.allow_non_contiguous_dma(reason="a few hundred bias values"):
                act.dma_start(acol[:], T["L0_gnn_a"].rearrange("(t p) o -> p (t o)", p=P)).then_inc(loads, 16)
                act.dma_start(K["bqk"][:, 0:1], T["L1_gnn_bq"].rearrange("(p o) -> p o", o=1)).then_inc(loads, 16)
                act.dma_start(K["bqk"][:, 1:2], T["L1_gnn_bk"].rearrange("(p o) -> p o", o=1)).then_inc(loads, 16)
                act.dma_start(K["b1"][:], T["L1_ffn_b1"].rearrange("(c p) -> p c", p=P)).then_inc(loads, 16)
            act.dma_start(K["bv"][0:1, :], T["L1_gnn_bv"].rearrange("(o n) -> o n", o=1)).then_inc(loads, 16)
            act.dma_start(K["wg"][:], T["L1_ffn_Wg"].rearrange("(c p) e -> p c e", p=P)).then_inc(loads, 16)
            act.dma_start(K["w1"][:], T["L1_ffn_W1"]).then_inc(loads, 16)
            act.wait_ge(parts_ready, 1)
            bias_rows(act, 1, rows_stored)

        @block.gpsimd
        def _(pool):
            pool.memset(K["w2pad"][:, 0:2], 0.0)
            pool.memset(K["padrow"][:], 0.0).then_inc(pool_step, 1)
            pool.memset(K["onesf"][:], 1.0).then_inc(pool_step, 1)
            pool.memset(K["onesb"][:], 1.0).then_inc(pool_step, 1)
            pool.memset(K["ident"][:], 0.0).then_inc(pool_step, 1)
            pool.wait_ge(pool_step, 4)
            pool.memset(K["padrow"][:, NUM:NUM + 1].bitcast(I32), NO_ROW)
            pool.affine_select(out=K["ident"][:], in_=K["ident"][:], compare_op=ALU.not_equal, fill=1.0, base=0,
                               pattern=[[-1, P]], channel_multiplier=1).then_inc(pool_step, 1)
            pool.affine_select(out=K["before"][:], in_=K["onesb"][:], compare_op=ALU.is_gt, fill=0.0, base=0,
                               pattern=[[1, P]], channel_multiplier=-1).then_inc(pool_step, 1)
            pool.affine_select(out=K["upto"][:], in_=K["onesf"][0:E0, 0:E0], compare_op=ALU.is_ge, fill=0.0,
                               base=0, pattern=[[1, E0]], channel_multiplier=-1).then_inc(pool_step, 1)
            pool.iota(K["count"][:], [[1, 256]], base=0, channel_multiplier=0,
                      allow_small_or_imprecise_dtypes=True).then_inc(pool_step, 1)
            pool.iota(K["rev0"][:], [[-1, E0]], base=E0, channel_multiplier=0,
                      allow_small_or_imprecise_dtypes=True).then_inc(pool_step, 1)
            pool.iota(K["number"][:], [[P, B]], base=0, channel_multiplier=1,
                      allow_small_or_imprecise_dtypes=True).then_inc(pool_step, 1)
            pool.memset(K["minus_half"][:], -0.5)
            pool.wait_ge(loads, 16 * NLOADS)
            pool.partition_broadcast(bvrow[:], K["bv"][0:1, :]).then_inc(pool_step, 1)
            pool.wait_ge(parts_ready, 1)
            bias_rows(pool, 2, rows_stored_pool)
            pool.wait_ge(rows_stored_pool, 16 * len(pieces))

        @block.tensor
        def _(pe):
            pe.wait_ge(loads, 16 * NLOADS)
            pe.wait_ge(pool_step, 5)
            for k in range(5):
                pe.transpose(pt[:, k, 0:P], wload[:, k, :], K["ident"][:])
            pe.transpose(pt[:, 5, 0:E0], wload[0:E0, 5, :], K["ident"][0:E0, 0:E0]).then_inc(transposed, 1)
            pe.wait_ge(wT_ready, 1)
            pe.matmul(pt[:, 6, 0:2], wT[:], acol[:], start=True, stop=True).then_inc(wa_ready, 1)

        @block.vector
        def _(dve):
            steps = [0]

            def then(ins):
                steps[0] += 1
                ins.then_inc(dve_step, 1)
                dve.wait_ge(dve_step, steps[0])

            dve.memset(biasf[:], 0.0).then_inc(bias_zero, 1)
            dve.memset(K["w2pad"][:, 2:4], 0.0)
            dve.wait_ge(loads, 16 * NLOADS)
            dve.wait_ge(pool_step, 11)
            for j in range(2):
                dve.tensor_copy(K["bvg"][:, j * P:(j + 1) * P], bvrow[:])
            then(dve.tensor_scalar(off[:], adj[:], 0.0, None, ALU.is_equal))
            then(dve.tensor_scalar(K["cap"][:], off[:], -1.0, -3e38, ALU.add, ALU.mult))
            dve.scalar_tensor_tensor(K["cap"][:], off[:], MASKED_E0 / SLOPE, K["cap"][:], ALU.mult, ALU.add)
            dve.tensor_scalar(K["far"][:], off[:], FAR, None, ALU.mult)
            then(dve.tensor_reduce(K["linked"][:], off[:], AX.X, ALU.min))
            then(dve.tensor_scalar(K["linked"][:], K["linked"][:], -1.0, 1.0, ALU.mult, ALU.add))
            dve.tensor_copy(K["identb"][:], K["ident"][:])
            then(dve.tensor_copy(part[0][:], biasf[:]))
            then(dve.tensor_tensor(res1[:], biasf[:], part[0][:], ALU.subtract))
            then(dve.tensor_copy(part[1][:], res1[:]))
            then(dve.tensor_tensor(res2[:], res1[:], part[1][:], ALU.subtract))
            dve.tensor_copy(part[2][:], res2[:]).then_inc(parts_ready, 1)
            then(dve.tensor_copy(K["w1hi"][:], K["w1"][:]))
            then(dve.tensor_tensor(K["w1lo"][:], K["w1"][:], K["w1hi"][:], ALU.subtract))
            pair = K["count"][:, 0:E0 // 2]
            dve.memset(K["sign"][:, 0::2], 1.0)
            dve.memset(K["sign"][:, 1::2], -1.0)
            dve.tensor_scalar(K["tile0"][:, 0::2], pair, float(REGION // P), None, ALU.mult)
            dve.tensor_scalar(K["tile0"][:, 1::2], pair, float(REGION // P), float(REGION // P - 1), ALU.mult, ALU.add)
            dve.tensor_scalar(K["start"][:, 0::2], pair, float(REGION), None, ALU.mult)
            then(dve.tensor_scalar(K["start"][:, 1::2], pair, -float(REGION), float(1 - REGION), ALU.mult, ALU.add))
            dve.tensor_copy(K["base0"][:], K["start"][:])
            then(dve.tensor_copy(K["base1"][:], K["start"][:, 0:E1]))
            dve.wait_ge(transposed, 1)
            dve.tensor_copy(wT[:], pt[:, 0, 0:P]).then_inc(wT_ready, 1)
            for k in range(3):
                dve.tensor_copy(K["wqkv"][:, k, :], pt[:, 1 + k, 0:P])
            then(dve.tensor_copy(K["woT"][:], pt[:, 4, 0:P]))
            then(dve.tensor_copy(K["wqkv_hi"][:], K["wqkv"][:]))
            then(dve.tensor_tensor(K["wqkv_lo"][:], K["wqkv"][:], K["wqkv_hi"][:], ALU.subtract))
            dve.tensor_copy(K["rwT"][:], pt[:, 5, 0:E0])
            dve.tensor_copy(K["wh"][:, 0:P], wload[:, 0, :])
            dve.wait_ge(wa_ready, 1)
            dve.tensor_copy(K["wh"][:, P:P + 1], pt[:, 6, 0:1])
            then(dve.tensor_copy(wa[:], pt[:, 6, 0:2]))
            dve.tensor_scalar(K["wa2"][:], K["onesf"][:], wa[:, 1:2], None, ALU.mult)


class Router:

    def __init__(self, ph, K, dve_sems, groups, experts, base, ps_logit, ps_rank, onehot):
        self.base, self.ps_logit, self.ps_rank, self.onehot = base, ps_logit, ps_rank, onehot
        self.logit_ready, self.rank_ready, self.onehot_ready = dve_sems
        self.shape = [P, groups, experts]
        self.G = groups
        self.rev = K["rev0"][:, E0 - experts:E0]
        self.top_of = ph.sb("top", [P, 2, groups], F32)
        self.eq_of = ph.sb("eq", self.shape, F32)
        self.key_of = ph.sb("key", self.shape, F32)
        self.first_of = ph.sb("first", [P, groups], F32)
        self.place_of = ph.sb("place", self.shape, F32)
        self.own_of = ph.sb("own", self.shape, F32)
        self.dest_of = ph.sb("dest", [P, groups], F32)
        self.top_ready = ph.sem("top_ready")
        self.eq_ready = ph.sem("eq_ready")
        self.key_ready = ph.sem("key_ready")
        self.first_ready = ph.sem("first_ready")
        self.place_ready = ph.sem("place_ready")
        self.own_ready = ph.sem("own_ready")
        self.dest_ready = ph.sem("dest_ready")

    def top(self, dve, g, s):
        dve.wait_ge(self.logit_ready, g + 1)
        dve.tensor_reduce(self.top_of[:, s % 2], self.ps_logit[s % 2], AX.X, ALU.max).then_inc(self.top_ready, 1)

    def equal(self, dve, g, s):
        dve.wait_ge(self.top_ready, g + 1)
        dve.tensor_tensor(self.eq_of[:], self.ps_logit[s % 2],
                          self.top_of[:, s % 2].unsqueeze(2).to_broadcast(self.shape),
                          ALU.is_ge).then_inc(self.eq_ready, 1)

    def key(self, dve, g, s):
        dve.wait_ge(self.eq_ready, g + 1)
        dve.tensor_tensor(self.key_of[:], self.eq_of[:], self.rev.unsqueeze(1).to_broadcast(self.shape),
                          ALU.mult).then_inc(self.key_ready, 1)

    def first(self, dve, g, s):
        dve.wait_ge(self.key_ready, g + 1)
        dve.tensor_reduce(self.first_of[:], self.key_of[:], AX.X, ALU.max).then_inc(self.first_ready, 1)

    def choose(self, dve, g, s):
        dve.wait_ge(self.first_ready, g + 1)
        dve.tensor_tensor(self.onehot[:, s % 2], self.key_of[:],
                          self.first_of[:].unsqueeze(2).to_broadcast(self.shape),
                          ALU.is_equal).then_inc(self.onehot_ready, 1)

    def place(self, dve, g, s):
        dve.wait_ge(self.rank_ready, g + 1)
        freed(dve, self.own_ready, g, 1)
        dve.tensor_tensor(self.place_of[:], self.ps_rank[:, 0:self.G, :],
                          self.base.unsqueeze(1).to_broadcast(self.shape), ALU.add).then_inc(self.place_ready, 1)

    def own(self, dve, g, s):
        dve.wait_ge(self.place_ready, g + 1)
        dve.tensor_tensor(self.own_of[:], self.place_of[:], self.onehot[:, s % 2], ALU.mult)
        dve.tensor_tensor(self.base, self.base, self.ps_rank[:, self.G, :], ALU.add).then_inc(self.own_ready, 1)

    def dest(self, dve, g, s):
        dve.wait_ge(self.own_ready, g + 1)
        dve.tensor_reduce(self.dest_of[:], self.own_of[:], AX.X, ALU.add).then_inc(self.dest_ready, 1)

    def index(self, dve, g, s, idx):
        return dve.scalar_tensor_tensor(idx, self.dest_of[:], -1.0, self.dest_of[:], ALU.mult, ALU.max)


def normalise_rows(dve, out, x, mean, rstd, groups):
    for j in range(groups):
        ins = dve.tensor_scalar(out[:, j, :], x[:, j, :], mean[:, j, :], rstd[:, j, :], ALU.subtract, ALU.mult)
    return ins


def gat(nc, K, T):
    G, N, U = 4, B // 4, 8
    x_in = T["x"].rearrange("(g j) n d -> g n j d", j=G)
    with Phase(nc, "gat") as ph:
        x = ph.sb("x", [P, U, G, P], F32)
        bn = ph.sb("bn", [P, 2, G, 6], F32)
        mv = ph.sb("mv", [P, 4, G, 2], F32)
        shift = ph.sb("shift", [P, 4, G], F32)
        xn = ph.sb("xn", [P, 2, G, P], F32)
        xT = ph.sb("xT", [P, 2, G, P], F32)
        h = ph.sb("h", [P, 4, G, P + 1], F32)
        ev = ph.sb("ev", [P, 2, G, P], F32)
        el = ph.sb("el", [P, 2, G, P], F32)
        nmax = ph.sb("nmax", [P, 2, G], F32)
        pr = ph.sb("pr", [P, 2, G, P], F32)
        prsum = ph.sb("prsum", [P, 4, G], F32)
        rsum = ph.sb("rsum", [P, 4, G], F32)
        prT = ph.sb("prT", [P, 2, G, P], F32)
        hp = ph.sb("hp", [P, 2, G, P], F32)
        row = ph.sb("row", [P, U, G, ROW], F32)
        bn2 = ph.sb("bn2", [P, 2, G, 6], F32)
        shift2 = ph.sb("shift2", [P, 4, G], F32)
        xn2 = ph.sb("xn2", [P, 2, G, P], F32)
        xT2 = ph.sb("xT2", [P, 2, G, P], F32)
        onehot = ph.sb("onehot", [P, 2, G, E0], BF16)
        idx = ph.sb("idx", [P, U, G], I32)

        ps_xT = ph.psum("ps_xT", [P, G, P])
        ps_ed = ph.psum("ps_ed", [P, G, P])
        ps_h2 = ph.psum("ps_h", [P, 2, 512])
        ps_h = ps_h2[:, :, 0:G // 2 * (P + 1)].rearrange("p b (j n) -> p b j n", j=G // 2)
        ps_prT = ph.psum("ps_prT", [P, G, P])
        ps_hp = ph.psum("ps_hp", [P, G, P])
        ps_xT2 = ph.psum("ps_xT2", [P, G, P])
        ps_r = ph.psum("ps_r", [P, 512])
        ps_logit = ps_r[:, 0:G * E0].rearrange("p (j e) -> p j e", j=G)
        ps_rank = ps_r[:, 256:256 + (G + 1) * E0].rearrange("p (j e) -> p j e", j=G + 1)

        x_loaded = ph.sems("x_loaded", U)
        stats_ready = ph.sem("stats_ready")
        var_ready = ph.sem("var_ready")
        veps_ready = ph.sem("veps_ready")
        rstd_ready = ph.sem("rstd_ready")
        shift_ready = ph.sem("shift_ready")
        xn_ready = ph.sem("xn_ready")
        xn_turned = ph.sem("xn_turned")
        xT_ready = ph.sem("xT_ready")
        projected = ph.sem("projected")
        h_ready = ph.sem("h_ready")
        edges_ready = ph.sem("edges_ready")
        leaky_ready = ph.sem("leaky_ready")
        max_ready = ph.sem("max_ready")
        pr_ready = ph.sem("pr_ready")
        pr_turned = ph.sem("pr_turned")
        prT_ready = ph.sem("prT_ready")
        attended = ph.sem("attended")
        hp_ready = ph.sem("hp_ready")
        rsum_ready = ph.sem("rsum_ready")
        x1_ready = ph.sem("x1_ready")
        stats2_ready = ph.sem("stats2_ready")
        var2_ready = ph.sem("var2_ready")
        veps2_ready = ph.sem("veps2_ready")
        rstd2_ready = ph.sem("rstd2_ready")
        shift2_ready = ph.sem("shift2_ready")
        xn2_ready = ph.sem("xn2_ready")
        xn2_turned = ph.sem("xn2_turned")
        xT2_ready = ph.sem("xT2_ready")
        logit_ready = ph.sem("logit_ready")
        onehot_ready = ph.sem("onehot_ready")
        rank_ready = ph.sem("rank_ready")
        idx_ready = ph.sem("idx_ready")
        rows_stored = ph.sems("rows_stored", U)
        slots_free = ph.sem("slots_free")
        router = Router(ph, K, (logit_ready, rank_ready, onehot_ready), G, E0, K["base0"][:], [ps_logit] * 2, ps_rank,
                        onehot)
        block = ph.block()

        @block.sync
        def _(sp):
            def load(g, s, r):
                freed(sp, x1_ready, g, U)
                src = x_in[g] if isinstance(g, int) else x_in[bass.ds(g, 1)].rearrange("o n j d -> (o n) j d")
                sp.dma_start(x[:, s], src).then_inc(x_loaded[s], 16)

            pipeline(sp, N, U, [(0, load)])

        @block.gpsimd
        def _(pool):
            pool.sem_inc(slots_free, U)

            def rstd(g, s, r):
                pool.wait_ge(veps_ready, g + 1)
                pool.tensor_tensor(mv[:, s % 4, :, 1], mv[:, s % 4, :, 1], K["minus_half"][:, 0:G],
                                   ALU.pow).then_inc(rstd_ready, 1)

            def rstd2(g, s, r):
                pool.wait_ge(veps2_ready, g + 1)
                pool.tensor_tensor(row[:, s, :, RSTD], row[:, s, :, RSTD], K["minus_half"][:, 0:G],
                                   ALU.pow).then_inc(rstd2_ready, 1)

            def scatter(g, s, r):
                wait_alone(K, pool, idx_ready, g + 1)
                for j in range(G):
                    pool.indirect_dma_start(
                        K["sorted0"], bass.IndirectOffsetOnAxis(ap=idx[:, s, j:j + 1], axis=0),
                        row[:, s, j, :], None).then_inc(rows_stored[s], 16)

            def release(g, s, r):
                pool.wait_ge(rows_stored[s], r * (16 * G) + 16 * G)
                pool.sem_inc(slots_free, 1)

            pipeline(pool, N, U, [
                (0, rstd), (3, rstd2), (5, scatter), (6, release)])

        @block.vector
        def _(dve):
            dve.memset(row[:, :, :, PROB:NUM + 1], 0.0)

            def stats(g, s, r):
                dve.wait_ge(x_loaded[s], r * 16 + 16)
                for j in range(G):
                    ins = dve.bn_stats(bn[:, s % 2, j, :], x[:, s, j, :])
                ins.then_inc(stats_ready, 1)

            def aggregate(g, s, r):
                if not isinstance(g, int) or g >= 4:
                    wait_alone(K, dve, xn_ready, g - 3)
                wait_alone(K, dve, stats_ready, g + 1)
                for j in range(G):
                    ins = dve.bn_aggr(mv[:, s % 4, j, :], bn[:, s % 2, j, :])
                ins.then_inc(var_ready, 1)

            def add_eps(g, s, r):
                dve.wait_ge(var_ready, g + 1)
                dve.tensor_scalar(mv[:, s % 4, :, 1], mv[:, s % 4, :, 1], EPS, None, ALU.add).then_inc(veps_ready, 1)

            def shifts(g, s, r):
                dve.wait_ge(rstd_ready, g + 1)
                dve.scalar_tensor_tensor(shift[:, s % 4], mv[:, s % 4, :, 0], -1.0, mv[:, s % 4, :, 1], ALU.mult,
                                         ALU.mult).then_inc(shift_ready, 1)

            def edges(g, s, r):
                dve.wait_ge(h_ready, g + 1)
                for j in range(G):
                    ins = dve.scalar_tensor_tensor(ev[:, s % 2, j, :], ps_ed[:, j, :], h[:, s % 4, j, P:P + 1],
                                                   K["cap"][:], ALU.add, ALU.min)
                ins.then_inc(edges_ready, 1)

            def leaky(g, s, r):
                dve.wait_ge(edges_ready, g + 1)
                freed(dve, pr_ready, g, 2)
                dve.scalar_tensor_tensor(el[:, s % 2], ev[:, s % 2], SLOPE, ev[:, s % 2], ALU.mult,
                                         ALU.max).then_inc(leaky_ready, 1)

            def row_max(g, s, r):
                dve.wait_ge(leaky_ready, g + 1)
                dve.tensor_reduce(nmax[:, s % 2], el[:, s % 2], AX.X, ALU.max, negate=True).then_inc(max_ready, 1)

            def inverse(g, s, r):
                dve.wait_ge(pr_ready, g + 1)
                dve.reciprocal(rsum[:, s % 4], prsum[:, s % 4]).then_inc(rsum_ready, 1)

            def residual(g, s, r):
                dve.wait_ge(slots_free, g + 1)
                dve.wait_ge(hp_ready, g + 1)
                dve.tensor_tensor(row[:, s, :, 0:P], x[:, s], hp[:, s % 2], ALU.add).then_inc(x1_ready, 1)

            def stats2(g, s, r):
                dve.wait_ge(x1_ready, g + 1)
                for j in range(G):
                    ins = dve.bn_stats(bn2[:, s % 2, j, :], row[:, s, j, 0:P])
                ins.then_inc(stats2_ready, 1)

            def aggregate2(g, s, r):
                wait_alone(K, dve, stats2_ready, g + 1)
                for j in range(G):
                    ins = dve.bn_aggr(row[:, s, j, MEAN:RSTD + 1], bn2[:, s % 2, j, :])
                ins.then_inc(var2_ready, 1)

            def add_eps2(g, s, r):
                dve.wait_ge(var2_ready, g + 1)
                dve.tensor_scalar(row[:, s, :, RSTD], row[:, s, :, RSTD], EPS, None, ALU.add).then_inc(veps2_ready, 1)

            def shifts2(g, s, r):
                dve.wait_ge(rstd2_ready, g + 1)
                dve.scalar_tensor_tensor(shift2[:, s % 4], row[:, s, :, MEAN], -1.0, row[:, s, :, RSTD], ALU.mult,
                                         ALU.mult).then_inc(shift2_ready, 1)

            def index(g, s, r):
                dve.wait_ge(router.dest_ready, g + 1)
                first = g * G
                dve.tensor_scalar(K["dest0"][:, first:first + G] if isinstance(g, int) else
                                  K["dest0"][:, bass.ds(first, G)], router.dest_of[:], 0.0, None, ALU.add)
                router.index(dve, g, s, idx[:, s]).then_inc(idx_ready, 1)

            def of(step):
                return lambda g, s, r: step(dve, g, s)

            pipeline(dve, N, U, [
                (0, stats), (3, residual), (5, of(router.equal)), (2, inverse), (5, of(router.key)), (0, aggregate),
                (0, add_eps), (3, stats2), (5, of(router.first)), (5, of(router.choose)), (3, aggregate2),
                (0, shifts), (1, edges), (3, add_eps2), (5, of(router.place)), (5, of(router.own)),
                (5, of(router.dest)), (5, index), (3, shifts2), (1, leaky), (1, row_max), (4, of(router.top))])

        @block.scalar
        def _(act):
            act.wait_ge(x_loaded[0], 16)
            act.dma_start(K["w1e"][:], T["L0_ffn_W1"].rearrange("e d h -> d e h")).then_inc(K["loaded0"], 16)
            for j in range(P // H0):
                act.dma_start(K["w2pad"][j * H0:(j + 1) * H0, j],
                              T["L0_ffn_W2"].rearrange("e h d -> h e d")).then_inc(K["loaded0"], 16)
            act.dma_start(K["wd"][:].rearrange("p e c d -> p (e c) d"),
                          T["L1_ffn_Wd"].rearrange("e (c p) d -> p (e c) d", p=P)).then_inc(K["loaded1"], 16)
            act.dma_start(K["sorted0"][E0 // 2 * REGION:, :], K["padrow"][:]).then_inc(K["loaded0"], 16)
            act.dma_start(K["sorted1"][E1 // 2 * REGION:, :], K["padrow"][:]).then_inc(K["loaded1"], 16)

            def normalise(g, s, r):
                act.wait_ge(shift_ready, g + 1)
                freed(act, xn_turned, g, 2)
                for j in range(G):
                    ins = act.activation(xn[:, s % 2, j, :], x[:, s, j, :], ACT.Identity,
                                         bias=shift[:, s % 4, j:j + 1], scale=mv[:, s % 4, j, 1:2])
                ins.then_inc(xn_ready, 1)

            def copy_xT(g, s, r):
                act.wait_ge(xn_turned, g + 1)
                freed(act, projected, g, 2)
                act.activation(xT[:, s % 2], ps_xT[:], ACT.Copy).then_inc(xT_ready, 1)

            def copy_h(g, s, r):
                act.wait_ge(projected, g + 1)
                freed(act, attended, g, 4)
                act.activation(h[:, s % 4].rearrange("p (b j) n -> p b j n", b=2), ps_h, ACT.Copy).then_inc(h_ready, 1)

            def exps(g, s, r):
                act.wait_ge(max_ready, g + 1)
                freed(act, pr_turned, g, 2)
                for j in range(G):
                    ins = act.activation(pr[:, s % 2, j, :], el[:, s % 2, j, :], ACT.Exp,
                                         bias=nmax[:, s % 2, j:j + 1], accum_out=prsum[:, s % 4, j:j + 1])
                ins.then_inc(pr_ready, 1)

            def copy_prT(g, s, r):
                act.wait_ge(pr_turned, g + 1)
                freed(act, attended, g, 2)
                act.activation(prT[:, s % 2], ps_prT[:], ACT.Copy).then_inc(prT_ready, 1)

            def relu(g, s, r):
                act.wait_ge(attended, g + 1)
                act.wait_ge(rsum_ready, g + 1)
                freed(act, x1_ready, g, 2)
                for j in range(G):
                    ins = act.activation(hp[:, s % 2, j, :], ps_hp[:, j, :], ACT.Relu,
                                         scale=rsum[:, s % 4, j:j + 1])
                ins.then_inc(hp_ready, 1)

            def normalise2(g, s, r):
                act.wait_ge(shift2_ready, g + 1)
                freed(act, xn2_turned, g, 2)
                for j in range(G):
                    ins = act.activation(xn2[:, s % 2, j, :], row[:, s, j, 0:P], ACT.Identity,
                                         bias=shift2[:, s % 4, j:j + 1], scale=row[:, s, j, RSTD:RSTD + 1])
                ins.then_inc(xn2_ready, 1)

            def copy_xT2(g, s, r):
                act.wait_ge(xn2_turned, g + 1)
                freed(act, logit_ready, g, 2)
                act.activation(xT2[:, s % 2], ps_xT2[:], ACT.Copy).then_inc(xT2_ready, 1)

            pipeline(act, N, U, [
                (4, normalise2), (1, copy_h), (2, copy_prT), (0, normalise), (4, copy_xT2), (0, copy_xT), (2, relu),
                (1, exps)])

        @block.tensor
        def _(pe):
            def turn_x(g, s, r):
                pe.wait_ge(xn_ready, g + 1)
                freed(pe, xT_ready, g, 1)
                for j in range(G):
                    ins = pe.transpose(ps_xT[:, j, :], xn[:, s % 2, j, :], K["ident"][:])
                ins.then_inc(xn_turned, 1)

            def project_dst(g, s, r):
                pe.wait_ge(xT_ready, g + 1)
                freed(pe, edges_ready, g, 1)
                pe.matmul(ps_ed[:].rearrange("p j n -> p (j n)"), K["wa2"][:],
                          xT[:, s % 2].rearrange("p j n -> p (j n)"), start=True, stop=True)

            def project(g, s, r):
                freed(pe, h_ready, g, 1)
                for j in range(G):
                    ins = pe.matmul(ps_h[:, j // 2, j % 2, :], xT[:, s % 2, j, :], K["wh"][:], start=True, stop=True)
                ins.then_inc(projected, 1)

            def turn_pr(g, s, r):
                pe.wait_ge(pr_ready, g + 1)
                freed(pe, prT_ready, g, 1)
                for j in range(G):
                    ins = pe.transpose(ps_prT[:, j, :], pr[:, s % 2, j, :], K["ident"][:])
                ins.then_inc(pr_turned, 1)

            def attend(g, s, r):
                pe.wait_ge(prT_ready, g + 1)
                pe.wait_ge(h_ready, g + 1)
                freed(pe, hp_ready, g, 1)
                for j in range(G):
                    ins = pe.matmul(ps_hp[:, j, :], prT[:, s % 2, j, :], h[:, s % 4, j, 0:P], start=True,
                                    stop=True)
                ins.then_inc(attended, 1)

            def turn_x2(g, s, r):
                pe.wait_ge(xn2_ready, g + 1)
                freed(pe, xT2_ready, g, 1)
                for j in range(G):
                    ins = pe.transpose(ps_xT2[:, j, :], xn2[:, s % 2, j, :], K["ident"][:])
                ins.then_inc(xn2_turned, 1)

            def route(g, s, r):
                pe.wait_ge(xT2_ready, g + 1)
                freed(pe, router.own_ready, g, 1)
                pe.matmul(ps_logit, K["onesb"][0:3, :],
                          K["biasrows"][:, RB_AT:RB_AT + E0].unsqueeze(1).to_broadcast([3, G, E0]),
                          start=True, stop=False, skip_group_check=True)
                for j in range(G):
                    ins = pe.matmul(ps_logit[:, j, :], xT2[:, s % 2, j, :], K["rwT"][:], start=False, stop=True,
                                    skip_group_check=True)
                ins.then_inc(logit_ready, 1)

            def rank(g, s, r):
                pe.wait_ge(onehot_ready, g + 1)
                rank_rows(pe, K, ps_rank, onehot[:, s % 2], G).then_inc(rank_ready, 1)

            pipeline(pe, N, U, [
                (1, project_dst), (1, project), (2, turn_pr), (4, turn_x2), (5, rank), (2, attend), (0, turn_x),
                (4, route)])


def rank_rows(pe, K, ps_rank, onehot, groups):
    for j in range(groups):
        for k in range(j):
            pe.matmul(ps_rank[:, j, :], K["onesb"][:], onehot[:, k, :], start=(k == 0), stop=False,
                      skip_group_check=True)
        pe.matmul(ps_rank[:, j, :], K["before"][:], onehot[:, j, :], start=(j == 0), stop=True,
                  skip_group_check=True)
    for k in range(groups):
        ins = pe.matmul(ps_rank[:, groups, :], K["onesb"][:], onehot[:, k, :], start=(k == 0),
                        stop=(k == groups - 1), skip_group_check=True)
    return ins


def table(nc, K, layer):
    E, NT = ((E0, NT0), (E1, NT1))[layer]
    base, rows = K[f"base{layer}"], K[f"sorted{layer}"]
    with Phase(nc, f"table{layer}") as ph:
        ends = ph.sb("ends", [1, E], I32)
        rowsof = ph.sb("rowsof", [P, E], F32)
        full = ph.sb("full", [P, E], I32)
        shifted = ph.sb("shifted", [P, E], I32)
        tilesof = ph.sb("tilesof", [P, E], F32)
        cols = ph.sb("cols", [E, 3], F32)
        upto = ph.sb("upto", [E, 1], F32)
        before = ph.sb("before", [E, 1], F32)
        signed = ph.sb("signed", [E, 1], F32)
        origin = ph.sb("origin", [E, 1], F32)
        passed = ph.sb("passed", [E, NT], F32)
        reached = ph.sb("reached", [E, NT], F32)
        within = ph.sb("within", [E, NT], F32)
        surplus = ph.sb("surplus", [1, NT], F32)
        expert = ph.sb("expert", [1, NT], F32)
        packed = ph.sb("packed", [1, 2, NT // 4], F32)
        along = ph.sb("along", [1, NT], F32)
        first = ph.sb("first", [1, NT], F32)
        tiles_all = ph.sb("tiles_all", [P, 1], F32)
        pt = ph.psum("pt", [P, 512])
        pc = ph.psum("pc", [P, 512])
        pr = ph.psum("pr", [P, 512])
        ends_ready = ph.sem("ends_ready")
        tilesof_ready = ph.sem("tilesof_ready")
        turned = ph.sem("turned")
        cols_ready = ph.sem("cols_ready")
        summed = ph.sem("summed")
        passed_ready = ph.sem("passed_ready")
        listed = ph.sem("listed")
        dve_step = ph.sem("dve_step")
        pads_sp = ph.sem("pads_sp")
        pads_act = ph.sem("pads_act")
        pads_pool = ph.sem("pads_pool")
        block = ph.block()

        def pads(eng, k, sem):
            eng.wait_ge(ends_ready, 1)
            with eng.Fori(0, len(range(k, E, 3))) as i:
                end = eng.value_load(ends[0:1, bass.ds(i * 3 + k, 1)], min_val=0, max_val=E // 2 * REGION - P)
                eng.dma_start(rows[bass.ds(end, P), :], K["padrow"][:]).then_inc(sem, 16)
            eng.wait_ge(sem, 16 * len(range(k, E, 3)))

        @block.sync
        def _(sp):
            pads(sp, 0, pads_sp)

        @block.scalar
        def _(act):
            pads(act, 1, pads_act)

        @block.gpsimd
        def _(pool):
            pads(pool, 2, pads_pool)

        @block.tensor
        def _(pe):
            pe.wait_ge(tilesof_ready, 1)
            for k, rowform in enumerate((tilesof[:], K["sign"][:, 0:E], K["tile0"][:, 0:E])):
                ins = pe.transpose(pt[0:E, k * P:(k + 1) * P], rowform, K["ident"][:])
            ins.then_inc(turned, 1)
            pe.wait_ge(cols_ready, 1)
            pe.matmul(pc[0:E, 0:1], K["upto"][0:E, 0:E], cols[:, 0:1], start=True, stop=True).then_inc(summed, 1)
            pe.wait_ge(passed_ready, 1)
            pe.matmul(pt[0:1, 0:NT], K["onesf"][0:E, 0:1], passed[:], start=True, stop=True)
            pe.matmul(pc[0:1, 0:NT], origin[:], within[:], start=True, stop=True)
            pe.matmul(pr[0:1, 0:NT], cols[:, 1:2], within[:], start=True, stop=True).then_inc(listed, 1)

        @block.vector
        def _(dve):
            steps = [0]

            def then(ins):
                steps[0] += 1
                ins.then_inc(dve_step, 1)
                dve.wait_ge(dve_step, steps[0])

            dve.tensor_scalar(ends[:, 0::2], base[0:1, 0::2], 0.0, None, ALU.add)
            dve.tensor_scalar(ends[:, 1::2], base[0:1, 1::2], -1.0, float(1 - P), ALU.mult,
                              ALU.add).then_inc(ends_ready, 1)
            then(dve.tensor_tensor(rowsof[:], base[:], K["start"][:, 0:E], ALU.subtract))
            then(dve.tensor_scalar(full[:], rowsof[:], float(P - 1), None, ALU.add))
            then(dve.tensor_scalar(shifted[:], full[:], 7, None, ALU.logical_shift_right))
            dve.tensor_copy(tilesof[:], shifted[:]).then_inc(tilesof_ready, 1)
            dve.wait_ge(turned, 1)
            dve.tensor_copy(cols[:],
                            pt[0:E, 0:3 * P].rearrange("e (k p) -> e k p", k=3)[:, :, 0]).then_inc(cols_ready, 1)
            dve.wait_ge(summed, 1)
            then(dve.tensor_copy(upto[:], pc[0:E, 0:1]))
            dve.tensor_tensor(before[:], upto[:], cols[:, 0:1], ALU.subtract)
            then(dve.tensor_scalar(passed[:], K["count"][0:E, 0:NT], upto[:], None, ALU.is_ge))
            dve.tensor_tensor(signed[:], before[:], cols[:, 1:2], ALU.mult)
            then(dve.tensor_scalar(reached[:], K["count"][0:E, 0:NT], before[:], None, ALU.is_ge))
            dve.tensor_tensor(origin[:], cols[:, 2:3], signed[:], ALU.subtract)
            dve.tensor_tensor(within[:], reached[:], passed[:], ALU.subtract).then_inc(passed_ready, 1)
            dve.wait_ge(listed, 1)
            then(dve.tensor_scalar(expert[:], pt[0:1, 0:NT], float(E - 1), None, ALU.min))
            by_four = expert[:].rearrange("o (g j) -> o g j", j=4)
            then(dve.scalar_tensor_tensor(packed[:, 0], by_four[:, :, 3], float(E), by_four[:, :, 2], ALU.mult,
                                          ALU.add))
            then(dve.scalar_tensor_tensor(packed[:, 1], packed[:, 0], float(E), by_four[:, :, 1], ALU.mult, ALU.add))
            dve.scalar_tensor_tensor(K["experts"][:, 0:NT // 4], packed[:, 1], float(E), by_four[:, :, 0], ALU.mult,
                                     ALU.add)
            dve.tensor_scalar(surplus[:], pt[0:1, 0:NT], float(E), float(E // 2 * REGION // P), ALU.is_ge, ALU.mult)
            then(dve.tensor_tensor(along[:], pr[0:1, 0:NT], K["count"][0:1, 0:NT], ALU.mult))
            then(dve.tensor_tensor(first[:], pc[0:1, 0:NT], along[:], ALU.add))
            then(dve.tensor_tensor(along[:], first[:], surplus[:], ALU.add))
            then(dve.tensor_scalar(K["table"][0:1, 0:NT], along[:], float(P), None, ALU.mult))
            if layer == 0:
                jump, lift = K["jump"], K["lift"]
                dve.memset(jump[:], 0.0)
                then(dve.tensor_reduce(tiles_all[:], tilesof[:, 0:E - 1], AX.X, ALU.add))
                then(dve.tensor_tensor(jump[:, 1:E - 1:2], tilesof[:, 1:E - 1:2], tilesof[:, 2:E:2], ALU.add))
                dve.tensor_copy(jump[:, 0:1], tilesof[:, 0:1])
                then(dve.tensor_tensor(jump[:, 2:E:2], tilesof[:, 0:E - 2:2], tilesof[:, 1:E - 1:2], ALU.add))
                dve.tensor_scalar(lift[:], tiles_all[:], float(P), float(E // 2 * REGION - 1), ALU.mult, ALU.add)
                dve.tensor_scalar(jump[:, 1:E - 1:2], jump[:, 1:E - 1:2], -float(P), -float(REGION), ALU.mult, ALU.add)
                dve.tensor_scalar(jump[:, 0:1], jump[:, 0:1], -float(P), float(1 - REGION), ALU.mult, ALU.add)
                then(dve.tensor_scalar(jump[:, 2:E:2], jump[:, 2:E:2], float(P), -float(REGION), ALU.mult, ALU.add))


def tile_places(pool, K, move, step):
    dest, placed, steps = K["dest0"], K["placed"], 0
    pool.tensor_scalar(placed[:], dest[:], K["lift"][:], None, ALU.add)
    for n, e in enumerate(list(range(E0 - 3, 0, -2)) + list(range(0, E0, 2))):
        start = e // 2 * REGION if e % 2 == 0 else 1 - (e + 1) // 2 * REGION
        pool.tensor_scalar(move[:, n % 2, :], dest[:], float(start), K["jump"][:, e:e + 1], ALU.is_ge,
                           ALU.mult).then_inc(step, 1)
        steps += 1
        pool.wait_ge(step, steps)
        pool.tensor_tensor(placed[:], placed[:], move[:, n % 2, :], ALU.add).then_inc(step, 1)
        steps += 1
    pool.wait_ge(step, steps)


def load_tiles(eng, K, rows, x, sem, g, G, tiles, limit):
    for j in tiles:
        tile = g * G + j
        at = K["table"][0:1, tile:tile + 1] if isinstance(g, int) else K["table"][0:1, bass.ds(tile, 1)]
        row = eng.value_load(at, min_val=0, max_val=limit)
        eng.dma_start(x[:, j, :], rows[bass.ds(row, P), :]).then_inc(sem, 16)


def tile_experts(pe, K, g, experts):
    at = K["experts"][0:1, g:g + 1] if isinstance(g, int) else K["experts"][0:1, bass.ds(g, 1)]
    packed = pe.value_load(at, min_val=0, max_val=experts ** 4 - 1)
    return [(packed // experts ** j) % experts for j in range(4)]


def expert0(nc, K):
    G, N, U = 4, NT0 // 4, 8
    y_out = K["mixed0"].rearrange("(g j p) d -> g p j d", j=G, p=P)
    with Phase(nc, "expert0") as ph:
        x = ph.sb("x", [P, U, G, ROW], F32)
        xn = ph.sb("xn", [P, 2, G, P], F32)
        xT = ph.sb("xT", [P, 2, G, P], F32)
        y = ph.sb("y", [P, U, G, P], F32)
        hid = ph.sb("hid", [P, 2, G, H0], F32)
        hT = ph.sb("hT", [P, 2, P], F32)
        ps_xT = ph.psum("ps_xT", [P, G, P])
        ps_hid2 = [ph.psum(f"ps_hid{k}", [P, 512]) for k in range(2)]
        ps_hid = [b[:, 0:G * H0].rearrange("p (j h) -> p j h", j=G) for b in ps_hid2]
        ps_hT = ph.psum("ps_hT", [P, 512])
        ps_y = ph.psum("ps_y", [P, 2, G, P])
        x_loaded = ph.sems("x_loaded", U)
        xn_ready = ph.sem("xn_ready")
        xn_turned = ph.sem("xn_turned")
        xT_ready = ph.sem("xT_ready")
        hid_done = ph.sem("hid_done")
        hid_ready = ph.sem("hid_ready")
        hid_turned = ph.sem("hid_turned")
        hT_ready = ph.sem("hT_ready")
        y_done = ph.sem("y_done")
        y_ready = ph.sem("y_ready")
        y_stored = ph.sems("y_stored", U)
        move = ph.sb("move", [P, 2, B], F32)
        places_step = ph.sem("places_step")
        block = ph.block()

        def loads(eng, tiles):
            def load(g, s, r):
                if not isinstance(g, int) or g >= U:
                    wait_alone(K, eng, y_ready, g - U + 1)
                load_tiles(eng, K, K["sorted0"], x[:, s], x_loaded[s], g, G, tiles, E0 // 2 * REGION)
            return load

        @block.gpsimd
        def _(pool):
            tile_places(pool, K, move, places_step)

        @block.sync
        def _(sp):
            sp.wait_ge(K["loaded0"], 16 * (P // H0 + 2))

            def store(g, s, r):
                sp.wait_ge(y_ready, g + 1)
                dst = y_out[g] if isinstance(g, int) else y_out[bass.ds(g, 1)].rearrange("o p j d -> (o p) j d")
                sp.dma_start(dst, y[:, s]).then_inc(y_stored[s], 16)

            pipeline(sp, N, U, [(8, store), (0, loads(sp, (0, 1)))], peel=2 * U)
            for s in range(U):
                sp.wait_ge(y_stored[s], 16 * (N // U))

        @block.vector
        def _(dve):
            def normalise(g, s, r):
                dve.wait_ge(x_loaded[s], r * (16 * G) + 16 * G)
                freed(dve, xn_turned, g, 2)
                normalise_rows(dve, xn[:, s % 2], x[:, s, :, 0:P], x[:, s, :, MEAN:MEAN + 1],
                               x[:, s, :, RSTD:RSTD + 1], G).then_inc(xn_ready, 1)

            def finish(g, s, r):
                dve.wait_ge(y_done, g + 1)
                if not isinstance(r, int) or r:
                    dve.wait_ge(y_stored[s], r * 16)
                dve.scalar_tensor_tensor(y[:, s], ps_y[:, s % 2], 0.0, x[:, s, :, 0:P], ALU.max,
                                         ALU.add).then_inc(y_ready, 1)

            pipeline(dve, N, U, [(7, finish), (2, normalise)], peel=2 * U)

        @block.scalar
        def _(act):
            act.wait_ge(K["loaded0"], 16 * (P // H0 + 2))

            def copy_xT(g, s, r):
                act.wait_ge(xn_turned, g + 1)
                freed(act, hid_done, g, 2)
                act.activation(xT[:, s % 2], ps_xT[:], ACT.Copy).then_inc(xT_ready, 1)

            def relu(g, s, r):
                act.wait_ge(hid_done, g + 1)
                freed(act, hid_turned, g, 2)
                act.activation(hid[:, s % 2], ps_hid[s % 2], ACT.Relu).then_inc(hid_ready, 1)

            def copy_hT(g, s, r):
                act.wait_ge(hid_turned, g + 1)
                freed(act, y_done, g, 2)
                act.activation(hT[:, s % 2], ps_hT[:, 0:P], ACT.Copy).then_inc(hT_ready, 1)

            pipeline(act, N, U, [(5, copy_hT), (3, copy_xT), (4, relu), (0, loads(act, (2, 3)))], peel=2 * U)

        @block.tensor
        def _(pe):
            pe.wait_ge(K["loaded0"], 16 * (P // H0 + 2))
            hidden_experts, mix_experts = [], []

            def turn_x(g, s, r):
                pe.wait_ge(xn_ready, g + 1)
                freed(pe, xT_ready, g, 1)
                for j in range(G):
                    ins = pe.matmul(ps_xT[:, j, :], xn[:, s % 2, j, :], K["ident"][:], start=True, stop=True)
                ins.then_inc(xn_turned, 1)

            def fetch(experts):
                def step(g, s, r):
                    experts[:] = tile_experts(pe, K, g, E0)
                return step

            def hidden(j):
                def step(g, s, r):
                    if j == 0:
                        pe.wait_ge(xT_ready, g + 1)
                        freed(pe, hid_ready, g, 2)
                    e, hid_of = hidden_experts[j], ps_hid[s % 2][:, j, :]
                    pe.matmul(hid_of, K["onesb"][0:3, :], K["biasrows"][:, bass.ds(e * H0 + B1_AT, H0)],
                              start=(j == 0), stop=False, skip_group_check=True)
                    ins = pe.matmul(hid_of, xT[:, s % 2, j, :],
                                    K["w1e"][:, bass.ds(e, 1), :].rearrange("p o h -> p (o h)"),
                                    start=False, stop=True, skip_group_check=True)
                    if j == G - 1:
                        ins.then_inc(hid_done, 1)
                return step

            def turn_hid(g, s, r):
                pe.wait_ge(hid_ready, g + 1)
                freed(pe, hT_ready, g, 1)
                pe.matmul(ps_hT[:, 0:P], hid[:, s % 2].rearrange("p j h -> p (j h)"), K["ident"][:],
                          start=True, stop=True).then_inc(hid_turned, 1)

            def mix(j):
                def step(g, s, r):
                    if j == 0:
                        pe.wait_ge(hT_ready, g + 1)
                        freed(pe, y_ready, g, 2)
                    e, y_of = mix_experts[j], ps_y[:, s % 2, j, :]
                    pe.matmul(y_of, K["onesb"][0:3, :], K["biasrows"][:, bass.ds(e * P + B2_AT, P)],
                              start=(j == 0), stop=False, skip_group_check=True)
                    ins = pe.matmul(y_of, hT[:, s % 2],
                                    K["w2pad"][:, j, bass.ds(e, 1), :].rearrange("p o h -> p (o h)"),
                                    start=False, stop=True, skip_group_check=True)
                    if j == G - 1:
                        ins.then_inc(y_done, 1)
                return step

            pipeline(pe, N, U, [(3, turn_x), (6, fetch(mix_experts)), (4, fetch(hidden_experts)), (6, mix(0)),
                                (4, hidden(0)), (5, turn_hid), (6, mix(1)), (4, hidden(1)), (6, mix(2)),
                                (4, hidden(2)), (6, mix(3)), (4, hidden(3))], peel=2 * U)


def mha(nc, K):
    G, N, U = 2, B // 2, 8
    J = G * HEADS
    SCALE = float(HD) ** -0.5
    x_out = K["x3"].rearrange("(g j p) d -> g p j d", j=G, p=P)
    with Phase(nc, "mha") as ph:
        idx = ph.sb("idx", [P, U, G], I32)
        x = ph.sb("x", [P, U, G, P], F32)
        bn = ph.sb("bn", [P, 2, G, 6], F32)
        mv = ph.sb("mv", [P, 4, G, 2], F32)
        shift = ph.sb("shift", [P, 4, G], F32)
        xn = ph.sb("xn", [P, 2, G, P], F32)
        xhi = ph.sb("xhi", [P, 2, G * P], F16)
        xlo = ph.sb("xlo", [P, 2, G * P], F16)
        qT = ph.sb("qT", [P, 2, G, P], F32)
        mx = ph.sb("mx", [P, J], F32)
        pr = ph.sb("pr", [P, 2, J, P], F32)
        prT = ph.sb("prT", [P, 2, J, P], F32)
        rs = ph.sb("rs", [P, J], F32)
        o = ph.sb("o", [P, 2, J, HD], F32)
        oT = ph.sb("oT", [P, 2, G, P], F32)
        kbd = ph.sb("kbd", [P, 2, G, HEADS, P], F32)
        vaug = ph.sb("vaug", [P, 4, J, HD + 1], F32)
        kbd_zero = ph.sem("kbd_zero")
        flip = ph.sb("flip", [P, B], I32)
        unflipped = ph.sb("unflipped", [P, B], I32)
        flip_ready = ph.sem("flip_ready")

        ps_a = ph.psum("ps_a", [P, 512])
        ps_xT = ps_a[:, 0:G * P]
        ps_out = ps_a[:, G * P:2 * G * P].rearrange("p (j n) -> p j n", j=G)
        ps_qk = ph.psum("ps_qk", [P, 2, G * P])
        ps_b = ph.psum("ps_b", [P, 512])
        ps_v = ps_b[:, 0:G * P].rearrange("p (j n) -> p j n", j=G)
        ps_oT = ps_b[:, G * P:2 * G * P].rearrange("p (j n) -> p j n", j=G)
        ps_s = ph.psum("ps_s", [P, J, P])
        ps_prT = ph.psum("ps_prT", [P, J, P])
        ps_o = ph.psum("ps_o", [P, 512])
        ps_oh = ps_o[:, 0:J * (HD + 1)].rearrange("p (j d) -> p j d", j=J)

        idx_ready = ph.sem("idx_ready")
        x_loaded = ph.sems("x_loaded", U)
        stats_ready = ph.sem("stats_ready")
        var_ready = ph.sem("var_ready")
        veps_ready = ph.sem("veps_ready")
        rstd_ready = ph.sem("rstd_ready")
        xn_ready = ph.sem("xn_ready")
        xn_turned = ph.sem("xn_turned")
        xhi_ready = ph.sem("xhi_ready")
        xlo_ready = ph.sem("xlo_ready")
        shift_ready = ph.sem("shift_ready")
        masked = ph.sem("masked")
        qk_done = ph.sem("qk_done")
        v_done = ph.sem("v_done")
        q_ready = ph.sem("q_ready")
        k_ready = ph.sem("k_ready")
        v_ready = ph.sem("v_ready")
        scored = ph.sem("scored")
        mx_ready = ph.sem("mx_ready")
        less_ready = ph.sem("less_ready")
        pr_ready = ph.sem("pr_ready")
        pr_turned = ph.sem("pr_turned")
        prT_ready = ph.sem("prT_ready")
        attended = ph.sem("attended")
        rs_ready = ph.sem("rs_ready")
        o_ready = ph.sem("o_ready")
        o_turned = ph.sem("o_turned")
        oT_ready = ph.sem("oT_ready")
        out_done = ph.sem("out_done")
        x3_ready = ph.sem("x3_ready")
        x3_stored = ph.sems("x3_stored", U)
        block = ph.block()

        @block.sync
        def _(sp):
            def store(g, s, r):
                sp.wait_ge(x3_ready, g + 1)
                dst = x_out[g] if isinstance(g, int) else x_out[bass.ds(g, 1)].rearrange("o p j d -> (o p) j d")
                sp.dma_start(dst, x[:, s]).then_inc(x3_stored[s], 16)

            pipeline(sp, N, U, [(7, store)])
            for s in range(U):
                sp.wait_ge(x3_stored[s], 16 * (N // U))

        @block.gpsimd
        def _(pool):
            def gather(g, s, r):
                wait_alone(K, pool, idx_ready, g + 1)
                if not isinstance(r, int) or r:
                    wait_alone(K, pool, x3_stored[s], r * 16)
                for j in range(G):
                    pool.indirect_dma_start(
                        x[:, s, j, :], None, K["mixed0"],
                        bass.IndirectOffsetOnAxis(ap=idx[:, s, j:j + 1], axis=0)).then_inc(x_loaded[s], 16)

            def rstd(g, s, r):
                pool.wait_ge(veps_ready, g + 1)
                pool.tensor_tensor(mv[:, s % 4, :, 1], mv[:, s % 4, :, 1], K["minus_half"][:, 0:G],
                                   ALU.pow).then_inc(rstd_ready, 1)

            pipeline(pool, N, U, [
                (1, rstd), (0, gather)])

        @block.vector
        def _(dve):
            dve.memset(kbd[:], 0.0).then_inc(kbd_zero, 1)
            dve.memset(vaug[:], 1.0).then_inc(kbd_zero, 1)
            dve.tensor_scalar(flip[:], K["dest0"][:], 0.0, float(P - 1), ALU.is_lt, ALU.mult)
            dve.tensor_copy(unflipped[:], K["placed"][:]).then_inc(flip_ready, 1)
            dve.wait_ge(flip_ready, 1)
            dve.tensor_tensor(K["place0"][:], unflipped[:], flip[:], ALU.bitwise_xor).then_inc(flip_ready, 1)
            dve.wait_ge(flip_ready, 2)

            def indices(g, s, r):
                freed(dve, var_ready, g, U)
                first = g * G
                src = K["place0"][:, first:first + G] if isinstance(g, int) else K["place0"][:, bass.ds(first, G)]
                dve.tensor_copy(idx[:, s], src).then_inc(idx_ready, 1)

            def stats(g, s, r):
                dve.wait_ge(x_loaded[s], r * (16 * G) + 16 * G)
                for j in range(G):
                    ins = dve.bn_stats(bn[:, s % 2, j, :], x[:, s, j, :])
                ins.then_inc(stats_ready, 1)

            def aggregate(g, s, r):
                wait_alone(K, dve, stats_ready, g + 1)
                for j in range(G):
                    ins = dve.bn_aggr(mv[:, s % 4, j, :], bn[:, s % 2, j, :])
                ins.then_inc(var_ready, 1)

            def add_eps(g, s, r):
                dve.wait_ge(var_ready, g + 1)
                dve.tensor_scalar(mv[:, s % 4, :, 1], mv[:, s % 4, :, 1], EPS, None, ALU.add).then_inc(veps_ready, 1)

            def shifts(g, s, r):
                dve.wait_ge(rstd_ready, g + 1)
                dve.scalar_tensor_tensor(shift[:, s % 4], mv[:, s % 4, :, 0], -1.0, mv[:, s % 4, :, 1], ALU.mult,
                                         ALU.mult).then_inc(shift_ready, 1)

            def low_part(g, s, r):
                dve.wait_ge(xhi_ready, g + 1)
                freed(dve, v_done, g, 2)
                dve.tensor_tensor(xlo[:, s % 2], ps_xT, xhi[:, s % 2], ALU.subtract).then_inc(xlo_ready, 1)

            def values(g, s, r):
                dve.wait_ge(v_done, g + 1)
                freed(dve, attended, g, 4)
                dve.tensor_tensor(vaug[:, s % 4, :, 0:HD], ps_v.rearrange("p j (h d) -> p (j h) d", h=HEADS),
                                  K["bvg"][:].rearrange("p (j d) -> p j d", j=J), ALU.add).then_inc(v_ready, 1)

            def mask(g, s, r):
                dve.wait_ge(scored, g + 1)
                freed(dve, pr_turned, g, 2)
                dve.tensor_tensor(pr[:, s % 2], ps_s[:], K["far"][:].unsqueeze(1).to_broadcast([P, J, P]),
                                  ALU.add).then_inc(masked, 1)

            def row_max(g, s, r):
                dve.wait_ge(masked, g + 1)
                dve.tensor_reduce(mx[:], pr[:, s % 2], AX.X, ALU.max).then_inc(mx_ready, 1)

            def less_max(g, s, r):
                dve.wait_ge(mx_ready, g + 1)
                dve.tensor_tensor(pr[:, s % 2], pr[:, s % 2], mx[:].unsqueeze(2).to_broadcast([P, J, P]),
                                  ALU.subtract).then_inc(less_ready, 1)

            def inverse(g, s, r):
                dve.wait_ge(attended, g + 1)
                dve.reciprocal(rs[:], ps_oh[:, :, HD]).then_inc(rs_ready, 1)

            def weigh(g, s, r):
                dve.wait_ge(rs_ready, g + 1)
                freed(dve, o_turned, g, 2)
                dve.scalar_tensor_tensor(o[:, s % 2], ps_oh[:, :, 0:HD], K["linked"][:],
                                         rs[:].unsqueeze(2).to_broadcast([P, J, HD]), ALU.mult,
                                         ALU.mult).then_inc(o_ready, 1)

            def residual(g, s, r):
                dve.wait_ge(out_done, g + 1)
                dve.tensor_tensor(x[:, s], ps_out, x[:, s], ALU.add).then_inc(x3_ready, 1)

            pipeline(dve, N, U, [
                (0, indices), (1, stats), (4, mask), (1, aggregate), (1, add_eps), (2, low_part), (4, row_max),
                (4, less_max), (7, residual), (2, values), (6, inverse), (1, shifts), (6, weigh)])

        @block.scalar
        def _(act):
            act.wait_ge(kbd_zero, 1)

            def exps(g, s, r):
                act.wait_ge(less_ready, g + 1)
                act.activation(pr[:, s % 2], pr[:, s % 2], ACT.Exp, scale=SCALE).then_inc(pr_ready, 1)

            def copy_q(g, s, r):
                act.wait_ge(qk_done, g + 1)
                freed(act, scored, g, 2)
                act.activation(qT[:, s % 2], ps_qk[:, 0, :].rearrange("p (j n) -> p j n", j=G), ACT.Identity,
                               bias=K["bqk"][:, 0:1]).then_inc(q_ready, 1)

            def copy_k(g, s, r):
                for hd in range(HEADS):
                    part = slice(hd * HD, (hd + 1) * HD)
                    ins = act.activation(kbd[part, s % 2, :, hd, :],
                                         ps_qk[part, 1, :].rearrange("p (j n) -> p j n", j=G),
                                         ACT.Identity, bias=K["bqk"][part, 1:2])
                ins.then_inc(k_ready, 1)

            def normalise(g, s, r):
                act.wait_ge(shift_ready, g + 1)
                freed(act, xn_turned, g, 2)
                for j in range(G):
                    ins = act.activation(xn[:, s % 2, j, :], x[:, s, j, :], ACT.Identity,
                                         bias=shift[:, s % 4, j:j + 1], scale=mv[:, s % 4, j, 1:2])
                ins.then_inc(xn_ready, 1)

            def high_part(g, s, r):
                act.wait_ge(xn_turned, g + 1)
                freed(act, v_done, g, 2)
                act.activation(xhi[:, s % 2], ps_xT, ACT.Copy).then_inc(xhi_ready, 1)

            def copy_prT(g, s, r):
                act.wait_ge(pr_turned, g + 1)
                freed(act, attended, g, 2)
                for j in range(G):
                    ins = act.activation(prT[:, s % 2, j * HEADS:(j + 1) * HEADS],
                                         ps_prT[:, j * HEADS:(j + 1) * HEADS, :], ACT.Copy)
                ins.then_inc(prT_ready, 1)

            def copy_oT(g, s, r):
                act.wait_ge(o_turned, g + 1)
                freed(act, out_done, g, 1)
                act.activation(oT[:, s % 2], ps_oT, ACT.Copy).then_inc(oT_ready, 1)

            pipeline(act, N, U, [
                (3, copy_q), (7, copy_oT), (2, high_part), (3, copy_k), (5, copy_prT), (4, exps), (1, normalise)])

        @block.tensor
        def _(pe):
            def upto(count):
                return min(count, N) if isinstance(count, int) else count

            def out(g, s, r):
                pe.wait_ge(oT_ready, g + 1)
                pe.wait_ge(xlo_ready, upto(g + 6))
                freed(pe, x3_ready, g, 1)
                pe.matmul(ps_out, K["onesb"][0:3, :],
                          K["biasrows"][:, BO_AT:BO_AT + P].unsqueeze(1).to_broadcast([3, G, P]),
                          start=True, stop=False, skip_group_check=True)
                for j in range(G):
                    ins = pe.matmul(ps_out[:, j, :], oT[:, s % 2, j, :], K["woT"][:], start=False, stop=True,
                                    skip_group_check=True)
                ins.then_inc(out_done, 1)

            def attend(g, s, r):
                pe.wait_ge(prT_ready, g + 1)
                freed(pe, o_ready, g, 1)
                for j in range(J):
                    ins = pe.matmul(ps_oh[:, j, :], prT[:, s % 2, j, :], vaug[:, s % 4, j, :], start=True, stop=True)
                ins.then_inc(attended, 1)

            def project(g, s, r):
                pe.wait_ge(xlo_ready, g + 1)
                freed(pe, k_ready, g, 1)
                hi, lo = xhi[:, s % 2], xlo[:, s % 2]
                for k in range(2):
                    pe.matmul(ps_qk[:, k, :], K["wqkv_lo"][:, k, :], hi, start=True, stop=False)
                    pe.matmul(ps_qk[:, k, :], K["wqkv_hi"][:, k, :], lo, start=False, stop=False)
                    ins = pe.matmul(ps_qk[:, k, :], K["wqkv_hi"][:, k, :], hi, start=False, stop=True)
                ins.then_inc(qk_done, 1)
                freed(pe, v_ready, g, 1)
                freed(pe, oT_ready, g, 5)
                for j in range(G):
                    rows = slice(j * P, (j + 1) * P)
                    pe.matmul(ps_v[:, j, :], lo[:, rows], K["wqkv_hi"][:, 2, :], start=True, stop=False)
                    pe.matmul(ps_v[:, j, :], hi[:, rows], K["wqkv_lo"][:, 2, :], start=False, stop=False)
                    ins = pe.matmul(ps_v[:, j, :], hi[:, rows], K["wqkv_hi"][:, 2, :], start=False, stop=True)
                ins.then_inc(v_done, 1)

            def turn_x(g, s, r):
                pe.wait_ge(xn_ready, g + 1)
                freed(pe, xlo_ready, g, 1)
                freed(pe, x3_ready, g, 6)
                for j in range(G):
                    ins = pe.transpose(ps_xT[:, j * P:(j + 1) * P], xn[:, s % 2, j, :], K["ident"][:])
                ins.then_inc(xn_turned, 1)

            def turn_pr(g, s, r):
                pe.wait_ge(pr_ready, g + 1)
                freed(pe, prT_ready, g, 1)
                for j in range(J):
                    ins = pe.transpose(ps_prT[:, j, :], pr[:, s % 2, j, :], K["ident"][:])
                ins.then_inc(pr_turned, 1)

            def score(g, s, r):
                pe.wait_ge(k_ready, g + 1)
                freed(pe, masked, g, 1)
                for j in range(G):
                    ins = pe.matmul(ps_s[:, j * HEADS:(j + 1) * HEADS, :], qT[:, s % 2, j, :], kbd[:, s % 2, j],
                                    start=True, stop=True)
                ins.then_inc(scored, 1)

            def turn_o(g, s, r):
                pe.wait_ge(o_ready, g + 1)
                pe.wait_ge(v_ready, upto(g + 5))
                freed(pe, oT_ready, g, 1)
                for j in range(G):
                    ins = pe.transpose(ps_oT[:, j, :],
                                       o[:, s % 2, j * HEADS:(j + 1) * HEADS].rearrange("p h d -> p (h d)"),
                                       K["ident"][:])
                ins.then_inc(o_turned, 1)

            pipeline(pe, N, U, [
                (7, turn_o), (2, turn_x), (5, turn_pr), (6, attend), (7, out), (2, project), (3, score)])


def hidden_chunk(pe, K, ps_h, xhi, xlo, gelu_done, h_done, g, c):
    cols = slice(c * P, (c + 1) * P)
    freed(pe, gelu_done, g, 1, per=NCH, k=c + 1)
    pe.matmul(ps_h[:, c, :], K["w1lo"][:, cols], xhi, start=True, stop=False)
    pe.matmul(ps_h[:, c, :], K["w1hi"][:, cols], xlo, start=False, stop=False)
    pe.matmul(ps_h[:, c, :], K["w1hi"][:, cols], xhi, start=False, stop=True).then_inc(h_done, 1)


def gate(nc, K):
    G, N, U = 4, B // 4, 8
    x_in = K["x3"].rearrange("(g j p) d -> g p j d", j=G, p=P)
    with Phase(nc, "gate") as ph:
        row = ph.sb("row", [P, U, G, ROW], F32)
        bn = ph.sb("bn", [P, 2, G, 6], F32)
        xn = ph.sb("xn", [P, 2, G, P], F32)
        xhi = ph.sb("xhi", [P, 2, G * P], F16)
        xlo = ph.sb("xlo", [P, 2, G * P], F16)
        h = ph.sb("h", [P, 2, NCH, G * P], F32)
        onehot = ph.sb("onehot", [P, 2, G, E1], BF16)
        less = ph.sb("less", [P, G, E1], F32)
        th = ph.sb("th", [P, G, E1], F32)
        den = ph.sb("den", [P, G, E1], F32)
        rden = ph.sb("rden", [P, G, E1], F32)
        ex = ph.sb("ex", [P, G, E1], F32)
        total = ph.sb("total", [P, G], F32)
        idx = ph.sb("idx", [P, U, G], I32)
        ps_xT = ph.psum("ps_xT", [P, G * P])
        ps_h = ph.psum("ps_h", [P, NCH, G * P])
        ps_l = [ph.psum(f"ps_l{k}", [P, 512]) for k in range(2)]
        ps_logit = [b[:, 0:G * E1].rearrange("p (j e) -> p j e", j=G) for b in ps_l]
        ps_r = ph.psum("ps_r", [P, 512])
        ps_rank = ps_r[:, 0:(G + 1) * E1].rearrange("p (j e) -> p j e", j=G + 1)
        x_loaded = ph.sems("x_loaded", U)
        stats_ready = ph.sem("stats_ready")
        var_ready = ph.sem("var_ready")
        veps_ready = ph.sem("veps_ready")
        rstd_ready = ph.sem("rstd_ready")
        xn_ready = ph.sem("xn_ready")
        xn_turned = ph.sem("xn_turned")
        xhi_ready = ph.sem("xhi_ready")
        xlo_ready = ph.sem("xlo_ready")
        h_done = ph.sem("h_done")
        gelu_done = ph.sem("gelu_done")
        logit_ready = ph.sem("logit_ready")
        onehot_ready = ph.sem("onehot_ready")
        less_ready = ph.sem("less_ready")
        th_ready = ph.sem("th_ready")
        rank_ready = ph.sem("rank_ready")
        den_ready = ph.sem("den_ready")
        rden_ready = ph.sem("rden_ready")
        ex_ready = ph.sem("ex_ready")
        total_ready = ph.sem("total_ready")
        prob_ready = ph.sem("prob_ready")
        idx_ready = ph.sem("idx_ready")
        rows_stored = ph.sems("rows_stored", U)
        router = Router(ph, K, (logit_ready, rank_ready, onehot_ready), G, E1, K["base1"][:], ps_logit, ps_rank,
                        onehot)
        block = ph.block()

        @block.sync
        def _(sp):
            def load(g, s, r):
                if not isinstance(r, int) or r:
                    sp.wait_ge(rows_stored[s], r * (16 * G))
                src = x_in[g] if isinstance(g, int) else x_in[bass.ds(g, 1)].rearrange("o p j d -> (o p) j d")
                sp.dma_start(row[:, s, :, 0:P], src).then_inc(x_loaded[s], 16)

            pipeline(sp, N, U, [(0, load)])

        @block.gpsimd
        def _(pool):
            def rstd(g, s, r):
                pool.wait_ge(veps_ready, g + 1)
                pool.tensor_tensor(row[:, s, :, RSTD], row[:, s, :, RSTD], K["minus_half"][:, 0:G],
                                   ALU.pow).then_inc(rstd_ready, 1)

            def scatter(g, s, r):
                pool.wait_ge(prob_ready, g + 1)
                wait_alone(K, pool, idx_ready, g + 1)
                for j in range(G):
                    pool.indirect_dma_start(
                        K["sorted1"], bass.IndirectOffsetOnAxis(ap=idx[:, s, j:j + 1], axis=0),
                        row[:, s, j, :], None).then_inc(rows_stored[s], 16)

            pipeline(pool, N, U, [(0, rstd), (6, scatter)])
            for s in range(U):
                pool.wait_ge(rows_stored[s], 16 * G * (N // U))

        @block.vector
        def _(dve):
            def stats(g, s, r):
                dve.wait_ge(x_loaded[s], r * 16 + 16)
                for j in range(G):
                    ins = dve.bn_stats(bn[:, s % 2, j, :], row[:, s, j, 0:P])
                ins.then_inc(stats_ready, 1)

            def aggregate(g, s, r):
                wait_alone(K, dve, stats_ready, g + 1)
                for j in range(G):
                    ins = dve.bn_aggr(row[:, s, j, MEAN:RSTD + 1], bn[:, s % 2, j, :])
                ins.then_inc(var_ready, 1)

            def add_eps(g, s, r):
                dve.wait_ge(var_ready, g + 1)
                dve.tensor_scalar(row[:, s, :, RSTD], row[:, s, :, RSTD], EPS, None, ALU.add).then_inc(veps_ready, 1)

            def normalise(g, s, r):
                dve.wait_ge(rstd_ready, g + 1)
                freed(dve, xn_turned, g, 2)
                normalise_rows(dve, xn[:, s % 2], row[:, s, :, 0:P], row[:, s, :, MEAN:MEAN + 1],
                               row[:, s, :, RSTD:RSTD + 1], G).then_inc(xn_ready, 1)

            def low_part(g, s, r):
                dve.wait_ge(xhi_ready, g + 1)
                freed(dve, h_done, g, 2, per=NCH, k=NCH)
                dve.tensor_tensor(xlo[:, s % 2], ps_xT[:], xhi[:, s % 2], ALU.subtract).then_inc(xlo_ready, 1)

            def less_top(g, s, r):
                dve.wait_ge(router.top_ready, g + 1)
                dve.tensor_tensor(less[:], ps_logit[s % 2],
                                  router.top_of[:, s % 2].unsqueeze(2).to_broadcast([P, G, E1]),
                                  ALU.subtract).then_inc(less_ready, 1)

            def one_less(g, s, r):
                dve.wait_ge(th_ready, g + 1)
                dve.tensor_scalar(den[:], th[:], -1.0, 1.0, ALU.mult, ALU.add).then_inc(den_ready, 1)

            def invert(g, s, r):
                dve.wait_ge(den_ready, g + 1)
                dve.reciprocal(rden[:], den[:]).then_inc(rden_ready, 1)

            def exps(g, s, r):
                dve.wait_ge(rden_ready, g + 1)
                dve.scalar_tensor_tensor(ex[:], th[:], 1.0, rden[:], ALU.add, ALU.mult).then_inc(ex_ready, 1)

            def add_up(g, s, r):
                dve.wait_ge(ex_ready, g + 1)
                dve.tensor_reduce(total[:], ex[:], AX.X, ALU.add).then_inc(total_ready, 1)

            def probability(g, s, r):
                dve.wait_ge(total_ready, g + 1)
                dve.reciprocal(row[:, s, :, PROB], total[:]).then_inc(prob_ready, 1)

            def index(g, s, r):
                first = g * G
                number = K["number"][:, first:first + G] if isinstance(g, int) else K["number"][:, bass.ds(first, G)]
                dve.tensor_copy(row[:, s, :, NUM:NUM + 1].bitcast(I32).rearrange("p j o -> p (j o)"), number)
                dve.wait_ge(router.dest_ready, g + 1)
                router.index(dve, g, s, idx[:, s]).then_inc(idx_ready, 1)

            def of(step):
                return lambda g, s, r: step(dve, g, s)

            pipeline(dve, N, U, [
                (2, low_part), (5, one_less), (4, of(router.top)), (0, stats), (5, invert), (4, less_top),
                (4, of(router.equal)), (5, exps), (0, aggregate), (4, of(router.key)), (5, of(router.place)),
                (5, add_up), (4, of(router.first)), (5, of(router.own)), (5, probability), (4, of(router.choose)),
                (0, add_eps), (5, of(router.dest)), (1, normalise), (5, index)])

        @block.scalar
        def _(act):
            def high_part(g, s, r):
                act.wait_ge(xn_turned, g + 1)
                freed(act, h_done, g, 2, per=NCH, k=NCH)
                act.activation(xhi[:, s % 2], ps_xT[:], ACT.Copy).then_inc(xhi_ready, 1)

            def tanh(g, s, r):
                act.wait_ge(less_ready, g + 1)
                freed(act, ex_ready, g, 1)
                act.activation(th[:], less[:], ACT.Tanh, scale=0.5).then_inc(th_ready, 1)

            def gelu(c):
                def step(g, s, r):
                    if c == 0:
                        freed(act, logit_ready, g, 2)
                    act.wait_ge(h_done, g * NCH + c + 1)
                    act.activation(h[:, s % 2, c, :], ps_h[:, c, :], ACT.Gelu,
                                   bias=K["b1"][:, c:c + 1]).then_inc(gelu_done, 1)
                return step

            pipeline(act, N, U, [(2, gelu(0)), (4, tanh), (2, gelu(1)), (1, high_part), (2, gelu(2)), (2, gelu(3))])

        @block.tensor
        def _(pe):
            def logits(c):
                def step(g, s, r):
                    pe.wait_ge(gelu_done, g * NCH + c + 1)
                    if c == 0:
                        freed(pe, less_ready, g, 2)
                        freed(pe, router.eq_ready, g, 2)
                        pe.matmul(ps_logit[s % 2], K["onesb"][0:3, :],
                                  K["biasrows"][:, BG_AT:BG_AT + E1].unsqueeze(1).to_broadcast([3, G, E1]),
                                  start=True, stop=False, skip_group_check=True)
                    for j in range(G):
                        ins = pe.matmul(ps_logit[s % 2][:, j, :], h[:, s % 2, c, j * P:(j + 1) * P], K["wg"][:, c, :],
                                        start=False, stop=(c == NCH - 1), skip_group_check=True)
                    if c == NCH - 1:
                        ins.then_inc(logit_ready, 1)
                return step

            def turn_x(g, s, r):
                pe.wait_ge(xn_ready, g + 1)
                freed(pe, xlo_ready, g, 1)
                for j in range(G):
                    ins = pe.transpose(ps_xT[:, j * P:(j + 1) * P], xn[:, s % 2, j, :], K["ident"][:])
                ins.then_inc(xn_turned, 1)

            def rank(g, s, r):
                pe.wait_ge(onehot_ready, g + 1)
                freed(pe, router.own_ready, g, 1)
                rank_rows(pe, K, ps_rank, onehot[:, s % 2], G).then_inc(rank_ready, 1)

            def hidden(c):
                def step(g, s, r):
                    pe.wait_ge(xlo_ready, g + 1)
                    hidden_chunk(pe, K, ps_h, xhi[:, s % 2], xlo[:, s % 2], gelu_done, h_done, g, c)
                return step

            pipeline(pe, N, U, [(3, logits(0)), (2, hidden(0)), (3, logits(1)), (2, hidden(1)), (1, turn_x),
                                (3, logits(2)), (2, hidden(2)), (3, logits(3)), (2, hidden(3)), (4, rank)])


def expert1(nc, K, out_rows):
    G, N, U = 4, NT1 // 4, 8
    with Phase(nc, "expert1") as ph:
        x = ph.sb("x", [P, U, G, ROW], F32)
        xn = ph.sb("xn", [P, 2, G, P], F32)
        xhi = ph.sb("xhi", [P, 2, G * P], F16)
        xlo = ph.sb("xlo", [P, 2, G * P], F16)
        h = ph.sb("h", [P, 2, NCH, G * P], F32)
        ps_xT = ph.psum("ps_xT", [P, G * P])
        ps_h = ph.psum("ps_h", [P, NCH, G * P])
        ps_y = ph.psum("ps_y", [P, 2, G, P])
        x_loaded = ph.sems("x_loaded", U)
        xn_ready = ph.sem("xn_ready")
        xn_turned = ph.sem("xn_turned")
        xhi_ready = ph.sem("xhi_ready")
        xlo_ready = ph.sem("xlo_ready")
        h_done = ph.sem("h_done")
        gelu_done = ph.sem("gelu_done")
        y_done = ph.sem("y_done")
        y_ready = ph.sem("y_ready")
        y_stored = ph.sems("y_stored", U)
        block = ph.block()

        @block.sync
        def _(sp):
            sp.wait_ge(K["loaded1"], 16 * 2)

            def load(g, s, r):
                if not isinstance(r, int) or r:
                    wait_alone(K, sp, y_stored[s], r * (16 * G))
                load_tiles(sp, K, K["sorted1"], x[:, s], x_loaded[s], g, G, range(G), E1 // 2 * REGION)

            pipeline(sp, N, U, [(0, load)])

        @block.gpsimd
        def _(pool):
            def scatter(g, s, r):
                wait_alone(K, pool, y_ready, g + 1)
                for j in range(G):
                    pool.indirect_dma_start(
                        out_rows, bass.IndirectOffsetOnAxis(ap=x[:, s, j, NUM:NUM + 1].bitcast(I32), axis=0),
                        x[:, s, j, 0:P], None, bounds_check=ROWS - 1, oob_is_err=False).then_inc(y_stored[s], 16)

            pipeline(pool, N, U, [(5, scatter)])
            for s in range(U):
                pool.wait_ge(y_stored[s], 16 * G * len(range(s, N, U)))

        @block.vector
        def _(dve):
            def normalise(g, s, r):
                dve.wait_ge(x_loaded[s], r * (16 * G) + 16 * G)
                freed(dve, xn_turned, g, 2)
                normalise_rows(dve, xn[:, s % 2], x[:, s, :, 0:P], x[:, s, :, MEAN:MEAN + 1],
                               x[:, s, :, RSTD:RSTD + 1], G).then_inc(xn_ready, 1)

            def low_part(g, s, r):
                dve.wait_ge(xhi_ready, g + 1)
                freed(dve, h_done, g, 2, per=NCH, k=NCH)
                dve.tensor_tensor(xlo[:, s % 2], ps_xT[:], xhi[:, s % 2], ALU.subtract).then_inc(xlo_ready, 1)

            def finish(g, s, r):
                dve.wait_ge(y_done, g + 1)
                for j in range(G):
                    ins = dve.scalar_tensor_tensor(x[:, s, j, 0:P], ps_y[:, s % 2, j, :], x[:, s, j, PROB:PROB + 1],
                                                   x[:, s, j, 0:P], ALU.mult, ALU.add)
                ins.then_inc(y_ready, 1)

            pipeline(dve, N, U, [(3, low_part), (5, finish), (2, normalise)])

        @block.scalar
        def _(act):
            def high_part(g, s, r):
                act.wait_ge(xn_turned, g + 1)
                freed(act, h_done, g, 2, per=NCH, k=NCH)
                act.activation(xhi[:, s % 2], ps_xT[:], ACT.Copy).then_inc(xhi_ready, 1)

            def gelu(c):
                def step(g, s, r):
                    if c == 0:
                        freed(act, y_done, g, 2)
                    act.wait_ge(h_done, g * NCH + c + 1)
                    act.activation(h[:, s % 2, c, :], ps_h[:, c, :], ACT.Gelu,
                                   bias=K["b1"][:, c:c + 1]).then_inc(gelu_done, 1)
                return step

            pipeline(act, N, U, [(3, gelu(0)), (3, gelu(1)), (2, high_part), (3, gelu(2)), (3, gelu(3))])

        @block.tensor
        def _(pe):
            pe.wait_ge(K["loaded1"], 16 * 2)

            def turn_x(g, s, r):
                pe.wait_ge(xn_ready, g + 1)
                freed(pe, xlo_ready, g, 1)
                for j in range(G):
                    ins = pe.transpose(ps_xT[:, j * P:(j + 1) * P], xn[:, s % 2, j, :], K["ident"][:])
                ins.then_inc(xn_turned, 1)

            def hidden(c):
                def step(g, s, r):
                    pe.wait_ge(xlo_ready, g + 1)
                    hidden_chunk(pe, K, ps_h, xhi[:, s % 2], xlo[:, s % 2], gelu_done, h_done, g, c)
                return step

            experts = []

            def mix(c):
                def step(g, s, r):
                    if c == 0:
                        experts[:] = tile_experts(pe, K, g, E1)
                        freed(pe, y_ready, g, 2)
                        for j in range(G):
                            pe.matmul(ps_y[:, s % 2, j, :], K["onesb"][0:3, :],
                                      K["biasrows"][:, bass.ds(experts[j] * P + BD_AT, P)],
                                      start=(j == 0), stop=False, skip_group_check=True)
                    pe.wait_ge(gelu_done, g * NCH + c + 1)
                    for j in range(G):
                        w = K["wd"][:, bass.ds(experts[j], 1), c, :].rearrange("p o d -> p (o d)")
                        ins = pe.matmul(ps_y[:, s % 2, j, :], h[:, s % 2, c, j * P:(j + 1) * P], w,
                                        start=False, stop=(c == NCH - 1), skip_group_check=True)
                    if c == NCH - 1:
                        ins.then_inc(y_done, 1)
                return step

            pipeline(pe, N, U, [(4, mix(0)), (3, hidden(0)), (4, mix(1)), (3, hidden(1)), (2, turn_x), (4, mix(2)),
                                (3, hidden(2)), (4, mix(3)), (3, hidden(3))])


def build(nc, T, out):
    with ExitStack() as ctx:
        K = {}
        for name, shape, dt in [
            ("ident", [P, P], F32), ("identb", [P, P], BF16), ("onesf", [P, P], F32), ("onesb", [P, P], BF16),
            ("before", [P, P], BF16), ("upto", [E0, E0], F32), ("count", [P, 256], F32), ("rev0", [P, E0], F32),
            ("sign", [P, E0], F32), ("tile0", [P, E0], F32), ("start", [P, E0], F32), ("number", [P, B], I32),
            ("minus_half", [P, 4], F32), ("padrow", [P, ROW], F32),
            ("cap", [P, P], F32), ("far", [P, P], BF16), ("linked", [P, 1], F32),
            ("wa2", [P, P], F32), ("wh", [P, P + 1], F32), ("rwT", [P, E0], F32),
            ("wqkv", [P, 3, P], F32), ("wqkv_hi", [P, 3, P], F16), ("wqkv_lo", [P, 3, P], F16), ("woT", [P, P], F32),
            ("bqk", [P, 2], F32), ("bv", [P, P], F32), ("bvg", [P, 2 * P], F32), ("b1", [P, NCH], F32),
            ("biasrows", [3, NBIAS], BF16), ("w1e", [P, E0, H0], F32), ("w2pad", [P, P // H0, E0, P], F32),
            ("w1", [P, HID], F32), ("w1hi", [P, HID], F16), ("w1lo", [P, HID], F16),
            ("wg", [P, NCH, E1], F32), ("wd", [P, E1, NCH, P], F32),
            ("base0", [P, E0], F32), ("base1", [P, E1], F32), ("dest0", [P, B], F32), ("jump", [P, E0], F32),
            ("lift", [P, 1], F32), ("placed", [P, B], F32), ("place0", [P, B], I32),
            ("table", [1, NT0], I32), ("experts", [1, NT0 // 4], I32),
        ]:
            K[name] = ctx.enter_context(nc.sbuf_tensor(f"k_{name}", shape, dt))
        K["loaded0"] = ctx.enter_context(nc.semaphore("loaded0"))
        K["loaded1"] = ctx.enter_context(nc.semaphore("loaded1"))
        K["passed"] = ctx.enter_context(nc.semaphore("passed"))
        K["sorted0"] = nc.dram_tensor("sorted0", (E0 // 2 * REGION + P, ROW), F32, kind="Internal").ap()
        K["sorted1"] = nc.dram_tensor("sorted1", (E1 // 2 * REGION + P, ROW), F32, kind="Internal").ap()
        K["mixed0"] = nc.dram_tensor("mixed0", (NT0 * P, P), F32, kind="Internal").ap()
        K["x3"] = nc.dram_tensor("x3", (ROWS, P), F32, kind="Internal").ap()
        setup(nc, K, T)
        gat(nc, K, T)
        table(nc, K, 0)
        expert0(nc, K)
        mha(nc, K)
        gate(nc, K)
        table(nc, K, 1)
        expert1(nc, K, out.rearrange("b n d -> (b n) d"))


_INS = ["x", "adj", "L0_gnn_W", "L0_gnn_a", "L0_ffn_router_w", "L0_ffn_router_b", "L0_ffn_W1", "L0_ffn_b1",
        "L0_ffn_W2", "L0_ffn_b2", "L1_gnn_wq", "L1_gnn_bq", "L1_gnn_wk", "L1_gnn_bk", "L1_gnn_wv", "L1_gnn_bv",
        "L1_gnn_wo", "L1_gnn_bo", "L1_ffn_W1", "L1_ffn_b1", "L1_ffn_Wg", "L1_ffn_bg", "L1_ffn_Wd", "L1_ffn_bd"]


def kernel(**inputs):
    import numpy as _np
    import concourse.bacc as _bacc
    from concourse import mybir as _mybir
    from concourse.bass_utils import run_bass_kernel_spmd as _run

    nc = _bacc.Bacc("TRN2", target_bir_lowering=False, num_devices=1)
    arrays, T = {}, {}
    for name in _INS:
        a = _np.ascontiguousarray(inputs[name])
        arrays[f"in_{name}"] = a
        T[name] = nc.dram_tensor(f"in_{name}", a.shape, _mybir.dt.from_np(a.dtype), kind="ExternalInput").ap()
    out = nc.dram_tensor("out_0", (B, P, P), F32, kind="ExternalOutput").ap()
    build(nc, T, out)
    r = _run(nc, [arrays], core_ids=[0])
    return r.results[0]["out_0"]
```
